# Optimizing a Trainium2 kernel written in Bass

```python
import numpy as np
import jax
import jax.numpy as jnp

def _softmax(x, axis=-1):
    return jax.nn.softmax(x, axis=axis)

def _gelu(x):
    return jax.nn.gelu(x, approximate=True)

def _silu(x):
    return jax.nn.silu(x)

def _sigmoid(x):
    return jax.nn.sigmoid(x)

def _layernorm(x, axis=-1, eps=1e-05):
    m = jnp.mean(x, axis=axis, keepdims=True)
    v = jnp.var(x, axis=axis, keepdims=True)
    return (x - m) / jnp.sqrt(v + eps)

def _scatter_add(tgt, idx, src, axis=0):
    return tgt.at[idx].add(src)

def _segment_sum(src, seg, n):
    return jax.ops.segment_sum(src, seg, n)
kernel_name = 'mk_gnn_ffn_d1_gnn_r8_2d7bef'

def setup_inputs(seed: int=0):
    np.random.seed(seed)
    _w = jnp.asarray

    def _rec_inputs():
        import jax
        import jax.numpy as jnp
        _gk = jax.random.key(seed)
        x = -0.0002117 + 1 * jax.random.normal(jax.random.fold_in(_gk, 1), (3125, 1024), jnp.float32)
        src = jax.random.randint(jax.random.fold_in(_gk, 2), (50000,), 0, 3125, jnp.int32)
        dst = jax.random.randint(jax.random.fold_in(_gk, 3), (50000,), 0, 3125, jnp.int32)
        _o = jnp.argsort(dst, stable=True)
        src = src[_o]
        dst = dst[_o]
        return (x, src, dst)
    x, src, dst = _rec_inputs()

    def _L0_gnn_setup():
        import jax, jax.numpy as jnp
        import numpy as np
        N = 3125
        E = 50000
        H = 4
        C = 256
        D_IN = 1024
        NEG_SLOPE = 0.2
        key = jax.random.key(seed)
        k1, k2, k3, k4, k5, k6 = jax.random.split(key, 6)
        x = jax.random.normal(k1, (N, D_IN), dtype=jnp.float32)
        edge_index = jax.random.randint(k2, (2, E), 0, N, dtype=jnp.int64)
        scale = 1.0 / np.sqrt(D_IN)
        W = jax.random.normal(k3, (D_IN, H * C), dtype=jnp.float32) * scale
        att_src = jax.random.normal(k4, (H, C), dtype=jnp.float32) * 0.1
        att_dst = jax.random.normal(k5, (H, C), dtype=jnp.float32) * 0.1
        bias = jax.random.normal(k6, (H * C,), dtype=jnp.float32) * 0.01
        return {'x': x, 'edge_index': edge_index, 'W': W, 'att_src': att_src, 'att_dst': att_dst, 'bias': bias}
    _L0_gnn_all = _L0_gnn_setup()
    _L0_gnn_in = {k: v for k, v in _L0_gnn_all.items() if k in ('W', 'att_src', 'att_dst', 'bias')}
    del _L0_gnn_all

    def _L0_ffn_setup():
        import jax, jax.numpy as jnp
        import numpy as np
        NUM_EXPERTS = 8
        EXPERT_CAPACITY = 2.0
        DIM = 1024
        HIDDEN_DIM = 512
        key = jax.random.key(seed)
        k_x, k_g, k_w1, k_w2 = jax.random.split(key, 4)
        n, t, d, f, e = (8, 1024, DIM, HIDDEN_DIM, NUM_EXPERTS)
        x = jax.random.normal(k_x, (n, t, d), dtype=jnp.float32)
        gate_w = jax.random.normal(k_g, (e, d), dtype=jnp.float32) * 0.02
        w1 = jax.random.normal(k_w1, (e, d, f), dtype=jnp.float32) * 0.02
        w2 = jax.random.normal(k_w2, (e, f, d), dtype=jnp.float32) * 0.02
        return {'x': x, 'gate_w': gate_w, 'w1': w1, 'w2': w2}
    _L0_ffn_all = _L0_ffn_setup()
    _L0_ffn_in = {k: v for k, v in _L0_ffn_all.items() if k in ('gate_w', 'w1', 'w2')}
    del _L0_ffn_all
    return {'x': x, 'src': src, 'dst': dst, 'L0_gnn_W': _L0_gnn_in['W'], 'L0_gnn_att_src': _L0_gnn_in['att_src'], 'L0_gnn_att_dst': _L0_gnn_in['att_dst'], 'L0_gnn_bias': _L0_gnn_in['bias'], 'L0_ffn_gate_w': _L0_ffn_in['gate_w'], 'L0_ffn_w1': _L0_ffn_in['w1'], 'L0_ffn_w2': _L0_ffn_in['w2']}

def reference(x, src, dst, L0_gnn_W, L0_gnn_att_src, L0_gnn_att_dst, L0_gnn_bias, L0_ffn_gate_w, L0_ffn_w1, L0_ffn_w2):
    import jax
    import jax.numpy as jnp

    def _L0_gnn_ref(x, edge_index, W, att_src, att_dst, bias):
        import jax, jax.numpy as jnp
        import numpy as np
        N = 3125
        E = 50000
        H = 4
        C = 256
        D_IN = 1024
        NEG_SLOPE = 0.2
        xp = (x @ W).reshape(N, H, C)
        a_src = jnp.einsum('nhc,hc->nh', xp, att_src)
        a_dst = jnp.einsum('nhc,hc->nh', xp, att_dst)
        loops = jnp.arange(N, dtype=edge_index.dtype)
        src = jnp.concatenate([edge_index[0], loops])
        dst = jnp.concatenate([edge_index[1], loops])
        e = jax.nn.leaky_relu(a_src[src] + a_dst[dst], NEG_SLOPE)
        m = jax.ops.segment_max(e, dst, num_segments=N)
        ee = jnp.exp(e - m[dst])
        z = jax.ops.segment_sum(ee, dst, num_segments=N)
        alpha = ee / z[dst]
        msgs = xp[src] * alpha[:, :, None]
        out = jax.ops.segment_sum(msgs, dst, num_segments=N)
        out = out.reshape(N, H * C) + bias
        return jax.nn.relu(out)

    def _L0_ffn_ref(x, gate_w, w1, w2):
        import jax, jax.numpy as jnp
        import numpy as np
        NUM_EXPERTS = 8
        EXPERT_CAPACITY = 2.0
        DIM = 1024
        HIDDEN_DIM = 512
        n, t, d = x.shape
        e = gate_w.shape[0]
        k = int(EXPERT_CAPACITY * t / e)
        scores = jnp.einsum('ntd,ed->nte', x, gate_w)
        probs = jax.nn.softmax(scores, axis=-1)
        g, m = jax.lax.top_k(probs.transpose(0, 2, 1), k)
        batch_idx = jnp.arange(n)[:, None, None]
        xin = x[batch_idx, m]
        h = jnp.einsum('nekd,edf->nekf', xin, w1)
        h = jax.nn.gelu(h, approximate=False)
        h = jnp.einsum('nekf,efd->nekd', h, w2)
        out_tok = g[..., None] * h
        out = jnp.zeros((n, t, d), dtype=x.dtype).at[batch_idx, m].add(out_tok)
        return out
    edge_index = jnp.stack([src, dst])
    x = x + _L0_gnn_ref(_layernorm(x, axis=-1), edge_index, L0_gnn_W, L0_gnn_att_src, L0_gnn_att_dst, L0_gnn_bias)
    x = x + _L0_ffn_ref(_layernorm(x, axis=-1)[None], L0_ffn_gate_w, L0_ffn_w1, L0_ffn_w2)[0]
    return x

_drawn_inputs = setup_inputs


def setup_inputs(seed=0):
    import zlib

    import numpy as np

    out = dict(_drawn_inputs(seed))
    spreads = {}
    factors = {'L0_gnn_bias': 7.63}
    for name, (base, spread) in spreads.items():
        noise = np.random.default_rng([zlib.crc32(name.encode()), seed]).standard_normal(out[name].shape)
        drawn = base * np.exp(spread * noise) if base else spread * noise
        out[name] = jnp.asarray(drawn.astype(out[name].dtype))
    for name, factor in factors.items():
        out[name] = (out[name] * factor).astype(out[name].dtype)
    return out
```

```python
from contextlib import ExitStack

import concourse.bass as bass
from concourse import mybir

F32 = mybir.dt.float32
I32 = mybir.dt.int32
ALU = mybir.AluOpType
ACT = mybir.ActivationFunctionType
AX = mybir.AxisListType

P = 128
N = 3125
D = 1024
KT = D // P
NB = -(-N // P)
LAST = N - (NB - 1) * P
NP = NB * P
H = 4
C = D // H
E = 50000
SUB = 2
CH = SUB * P
NC = -(-E // CH)
EC = NC * CH // P
PADS = NC * CH - E
ELAST = E - (P - 1) * EC
ITEMS = NC + NB - 1
REC = 12
W_AT, SELF_AT, FIRST_AT, DST_AT, SRC_AT = 0, 4, 8, 9, 11
SLOPE = 0.2
EPS = 1e-5
NEG = -1e38
X = 8
FH = 512
FT = FH // P
TOPK = 2 * N // X
ST = -(-TOPK // P)
SLAST = TOPK - (ST - 1) * P
REP = P // X
GATHERS = 8


class Links:

    def __init__(self, eng, sem):
        self.eng, self.sem, self.n = eng, sem, 0

    def add(self, ins):
        ins.then_inc(self.sem, 1)
        self.n += 1

    def wait(self):
        self.eng.wait_ge(self.sem, self.n)

    def link(self, ins):
        self.add(ins)
        self.wait()


class Core:
    pass


def new_sems(nc, ctx, *names):
    return [ctx.enter_context(nc.semaphore(n)) for n in names]


def gate(nc, g, sem, turn):
    nc.gpsimd.wait_ge(sem, turn + 1)
    nc.gpsimd.tensor_tensor(g.gate[0:1, 1:2], g.gate[0:1, 0:1], g.gate[0:1, 0:1], ALU.add).then_inc(sem, 1)


def rows(b):
    return P if b < NB - 1 else LAST


def setup(nc, ctx, g):
    sb = lambda n, s, d=F32: ctx.enter_context(nc.sbuf_tensor(n, s, d))
    g.iota = sb("iota", [P, NP])
    g.ident = sb("ident", [P, P])
    g.ones = sb("ones", [P, P])
    g.gate = sb("gate", [P, 2])
    g.pcol = sb("pcol", [P, 1])
    iota_done, consts_done = new_sems(nc, ctx, "iota_done", "consts_done")
    with nc.sbuf_tensor("iota_int", [P, NP], I32) as ints, nc.sbuf_tensor("pcol_int", [P, 1], I32) as pint, nc.Block() as block:
        @block.gpsimd
        def _(pool):
            nc.gpsimd.iota(ints[:], [[1, NP]], base=0, channel_multiplier=0).then_inc(iota_done, 1)
            nc.gpsimd.iota(pint[:], [[0, 1]], base=0, channel_multiplier=1).then_inc(iota_done, 1)

        @block.vector
        def _(dve):
            own = Links(dve, consts_done)
            own.add(nc.vector.memset(g.ones[:], 1.0))
            own.add(nc.vector.memset(g.gate[:], 0.0))
            dve.wait_ge(iota_done, 2)
            own.add(nc.vector.tensor_copy(g.iota[:], ints[:]))
            own.link(nc.vector.tensor_copy(g.pcol[:], pint[:]))
            own.link(nc.vector.tensor_scalar(g.ident[:], g.iota[:, 0:P], g.pcol[:], None, ALU.is_equal))


def stage_nodes(nc, g, atab_out, x, W, att_src, att_dst):
    with ExitStack() as ctx:
        sb = lambda n, s, d=F32: ctx.enter_context(nc.sbuf_tensor(n, s, d))
        ps = lambda n, s: ctx.enter_context(nc.psum_tensor(n, s, F32))
        wa = sb("wa", [P, KT, 2 * H])
        stats = sb("ln_stats", [P, NB, 12])
        mv = sb("ln_mv", [P, NB, 2])
        rstd = sb("ln_rstd", [P, NB])
        eps = sb("ln_eps", [P, 1])
        xn = [sb(f"xn{i}", [P, D]) for i in range(2)]
        xt = [sb(f"xt{i}", [P, D]) for i in range(2)]
        att, prod = xt, xn[0]
        tp = [ps(f"tp{i}", [P, D]) for i in range(2)]
        ap = [ps(f"ap{i}", [P, 2 * H]) for i in range(2)]
        (w_in, x_in, att_in, own_dve, wa_done, var_done, std_done, xn_done, tp_done, evac_act, evac_dve,
         a_done, atab_done, pad_done) = new_sems(
            nc, g.ctx, "w_in", "x_in", "att_in", "nodes_dve", "wa_done", "var_done", "std_done", "xn_done",
            "tp_done", "evac_act", "evac_dve", "a_done", "atab_done", "pad_done")
        with nc.Block() as block:
            @block.sync
            def _(sp):
                sp.dma_start(g.w[:], W.rearrange("(k p) n -> p k n", p=P)).then_inc(w_in, 16)
                sp.wait_ge(pad_done, 1)
                with sp.Fori(0, NB - 1) as b:
                    sp.dma_start(g.big[:, bass.ds(b, 1), :], x[bass.ds(b * P, P), :].unsqueeze(1)).then_inc(x_in, 16)
                sp.dma_start(g.big[0:LAST, NB - 1, :], x[(NB - 1) * P:N, :]).then_inc(x_in, 16)
                sp.wait_ge(atab_done, NB)
                sp.dma_start(g.a_src.rearrange("(b p) h -> p b h", p=P), g.atab[:, :, 0:H]).then_inc(atab_out, 16)
                sp.dma_start(g.a_both.rearrange("(b p) h -> p b h", p=P), g.atab[:]).then_inc(atab_out, 16)
                sp.wait_ge(atab_out, 32)

            @block.scalar
            def _(act):
                act.dma_start(att[0][:], att_src.rearrange("h c -> (h c)").unsqueeze(0).broadcast_to([P, D])).then_inc(att_in, 16)
                act.dma_start(att[1][:], att_dst.rearrange("h c -> (h c)").unsqueeze(0).broadcast_to([P, D])).then_inc(att_in, 16)
                act.wait_ge(var_done, 1)
                nc.scalar.activation(rstd[:], mv[:, :, 1], ACT.Sqrt, bias=eps[:]).then_inc(std_done, 1)

                def evacuate(b, i, at):
                    act.wait_ge(evac_dve, b + 1)
                    nc.scalar.copy(at, xt[i][:]).then_inc(evac_act, 1)

                with act.Fori(0, NB - 1, 2) as b:
                    for i in range(2):
                        evacuate(b + i, i, g.big[:, bass.ds(b + i, 1), :].rearrange("p a n -> p (a n)"))
                evacuate(NB - 1, 0, g.big[:, NB - 1, :])

            @block.vector
            def _(dve):
                own = Links(dve, own_dve)
                own.add(nc.vector.memset(eps[:], EPS))
                nc.vector.memset(g.big[:, NB - 1, :], 0.0).then_inc(pad_done, 1)
                dve.wait_ge(w_in, 16)
                dve.wait_ge(att_in, 32)
                for k in range(KT):
                    for j in range(2):
                        own.link(nc.vector.tensor_tensor(prod[:], g.w[:, k, :], att[j][:], ALU.mult))
                        own.link(nc.vector.tensor_reduce(wa[:, k, j * H:(j + 1) * H],
                                                         prod[:].rearrange("p (h c) -> p h c", h=H), AX.X, ALU.add))
                nc.vector.engine_nop().then_inc(wa_done, 1)
                dve.wait_ge(x_in, 16 * NB)
                for b in range(NB):
                    for j in range(2):
                        own.add(nc.vector.bn_stats(stats[:, b, j * 6:j * 6 + 6], g.big[:, b, j * 512:(j + 1) * 512]))
                own.wait()
                for b in range(NB):
                    own.add(nc.vector.bn_aggr(mv[:, b, :], stats[:, b, :]))
                own.wait()
                nc.vector.engine_nop().then_inc(var_done, 1)
                dve.wait_ge(std_done, 1)
                own.link(nc.vector.reciprocal(rstd[:], rstd[:]))

                def normalise(b, i, src, mean, r, first):
                    if not first:
                        dve.wait_ge(tp_done, b - 1)
                    nc.vector.tensor_scalar(xn[i][:], src, mean, r, ALU.subtract, ALU.mult).then_inc(xn_done, 1)

                def evacuate(b, i, col, first):
                    dve.wait_ge(tp_done, b + 1)
                    if not first:
                        dve.wait_ge(a_done, b - 1)
                        dve.wait_ge(evac_act, b - 1)
                    nc.vector.tensor_copy(xt[i][:], tp[i][:]).then_inc(evac_dve, 1)
                    dve.wait_ge(a_done, b + 1)
                    nc.vector.tensor_copy(col, ap[i][:]).then_inc(atab_done, 1)

                def block_of(b, i, first=False):
                    one = lambda t: t[:, bass.ds(b, 1)]
                    normalise(b, i, g.big[:, bass.ds(b, 1), :].rearrange("p a n -> p (a n)"),
                              mv[:, bass.ds(b, 1), 0:1].rearrange("p a n -> p (a n)"), one(rstd), first)
                    evacuate(b, i, g.atab[:, bass.ds(b, 1), :].rearrange("p a n -> p (a n)"), first)

                block_of(0, 0, True)
                block_of(1, 1, True)
                with dve.Fori(2, NB - 1, 2) as b:
                    for i in range(2):
                        block_of(b + i, i)
                block_of(NB - 1, 0)

            @block.tensor
            def _(pe):
                def transposes(b, i, first):
                    pe.wait_ge(xn_done, b + 1)
                    if not first:
                        pe.wait_ge(evac_dve, b - 1)
                    for k in range(KT):
                        t = nc.tensor.transpose(tp[i][:, k * P:(k + 1) * P], xn[i][:, k * P:(k + 1) * P], g.ident[:])
                    t.then_inc(tp_done, 1)

                def scores(b, i, first):
                    if not first:
                        pe.wait_ge(atab_done, b - 1)
                    pe.wait_ge(evac_dve, b + 1)
                    for k in range(KT):
                        t = nc.tensor.matmul(ap[i][:], xt[i][:, k * P:(k + 1) * P], wa[:, k, :],
                                             start=(k == 0), stop=(k == KT - 1))
                    t.then_inc(a_done, 1)

                pe.wait_ge(wa_done, 1)
                for b in range(2):
                    transposes(b, b, True)
                    scores(b, b, True)
                with pe.Fori(2, NB - 1, 2) as b:
                    for i in range(2):
                        transposes(b + i, i, False)
                        scores(b + i, i, False)
                transposes(NB - 1, 0, False)
                scores(NB - 1, 0, False)


def stage_project(nc, g, atab_out, src, dst):
    with ExitStack() as ctx:
        sb = lambda n, s, d=F32: ctx.enter_context(nc.sbuf_tensor(n, s, d))
        ps = lambda n, s: ctx.enter_context(nc.psum_tensor(n, s, F32))
        xt = [sb(f"pxt{i}", [P, D]) for i in range(2)]
        xo = [sb(f"pxo{i}", [P, D]) for i in range(2)]
        pp = [ps(f"pp{i}", [P, D]) for i in range(2)]
        dgi = sb("dst_gather", [P, EC], I32)
        idx = [sb(f"gidx{i}", [P, 2, GATHERS], I32) for i in range(2)]
        got = [sb(f"got{i}", [P, GATHERS, 3 * H]) for i in range(2)]
        xt_done, pp_done, xo_done, edges_in, own_dve, gated, idx_done, got_copied, fills = new_sems(
            nc, g.ctx, "pxt_done", "pp_done", "pxo_done", "edges_in", "project_dve", "project_gated", "idx_done",
            "got_copied", "edge_fills")
        xp_out = new_sems(nc, g.ctx, "xp_out0", "xp_out1")
        got_in = new_sems(nc, g.ctx, "got_in0", "got_in1")
        STEPS = EC // GATHERS
        assert EC % GATHERS == 0

        with nc.Block() as block:
            @block.sync
            def _(sp):
                sp.wait_ge(fills, 2)
                sp.dma_start(g.dst_i[0:1, 1:EC + 2], dst[0:EC + 1].unsqueeze(0)).then_inc(edges_in, 16)
                inner = dst[EC - 1:EC - 1 + EC]
                sp.dma_start(g.dst_i[1:P - 1, :], bass.AP(inner.tensor, EC - 1, [[EC, P - 2], [1, EC + 2]])).then_inc(edges_in, 16)
                sp.dma_start(g.dst_i[P - 1:P, 0:ELAST + 1], dst[(P - 1) * EC - 1:E].unsqueeze(0)).then_inc(edges_in, 16)
                sp.dma_start(g.src_i[0:P - 1, :], src[0:(P - 1) * EC].rearrange("(p n) -> p n", p=P - 1)).then_inc(edges_in, 16)
                sp.dma_start(g.src_i[P - 1:P, 0:ELAST], src[(P - 1) * EC:E].unsqueeze(0)).then_inc(edges_in, 16)

                def store(b, i):
                    sp.wait_ge(xo_done, b + 1)
                    sp.dma_start(g.xp[bass.ds(b * P, P), :], xo[i][:]).then_inc(xp_out[i], 16)

                with sp.Fori(0, NB - 1, 2) as b:
                    for i in range(2):
                        store(b + i, i)
                store(NB - 1, 0)
                sp.wait_ge(xp_out[0], 16 * ((NB + 1) // 2))
                sp.wait_ge(xp_out[1], 16 * (NB // 2))

            @block.gpsimd
            def _(pool):
                nc.gpsimd.memset(g.gate[0:1, 1:2], 0.0).then_inc(gated, 1)

                def gather(s, i):
                    pool.wait_ge(idx_done, s * 2 + 2)
                    gate(nc, g, gated, s)
                    for j in range(GATHERS):
                        nc.gpsimd.indirect_dma_start(
                            got[i][:, j, 0:H], None, g.a_src[:, :],
                            bass.IndirectOffsetOnAxis(idx[i][:, 0, j:j + 1], 0)).then_inc(got_in[i], 16)
                        nc.gpsimd.indirect_dma_start(
                            got[i][:, j, H:3 * H], None, g.a_both[:, :],
                            bass.IndirectOffsetOnAxis(idx[i][:, 1, j:j + 1], 0)).then_inc(got_in[i], 16)

                with pool.Fori(0, STEPS - 1, 2) as s:
                    for i in range(2):
                        gather(s + i, i)
                if STEPS % 2:
                    gather(STEPS - 1, 0)

            @block.vector
            def _(dve):
                own = Links(dve, own_dve)
                nc.vector.memset(g.dst_i[:], -1).then_inc(fills, 1)
                nc.vector.memset(g.src_i[:], 0).then_inc(fills, 1)
                dve.wait_ge(edges_in, 16 * 5)
                own.add(nc.vector.tensor_copy(g.dst_f[:], g.dst_i[:]))
                own.link(nc.vector.tensor_scalar_max(dgi[:], g.dst_i[:, 1:EC + 1], 0))

                def project(b, i, first):
                    if not first:
                        dve.wait_ge(pp_done, b - 1)
                    nc.vector.tensor_copy(xt[i][:], g.big[:, bass.ds(b, 1), :].rearrange("p a n -> p (a n)")).then_inc(xt_done, 1)

                def indices(s, i, turn):
                    if turn is not None:
                        dve.wait_ge(got_in[i], turn * 32 * GATHERS)
                        collect(s - 2, i)
                    at = bass.ds(s * GATHERS, GATHERS)
                    nc.vector.tensor_copy(idx[i][:, 0, :], g.src_i[:, at]).then_inc(idx_done, 1)
                    nc.vector.tensor_copy(idx[i][:, 1, :], dgi[:, at]).then_inc(idx_done, 1)

                def collect(s, i):
                    at = bass.ds(s * GATHERS, GATHERS)
                    nc.vector.tensor_copy(g.edge_a[:, at, :], got[i][:]).then_inc(got_copied, 1)
                    dve.wait_ge(got_copied, s + 1)

                indices(0, 0, None)
                indices(1, 1, None)
                project(0, 0, True)
                project(1, 1, True)
                with dve.Fori(1, (NB - 1) // 2) as t:
                    for j in range(2):
                        for i in range(2):
                            indices(t * 4 - 2 + 2 * j + i, i, t * 2 - 1 + j)
                        project(t * 2 + j, j, False)
                project(NB - 1, 0, False)
                done = 4 * ((NB - 1) // 2) - 2
                assert done + 3 == STEPS
                for s in range(done, STEPS):
                    indices(s, s % 2, s // 2)
                for s in range(STEPS - 2, STEPS):
                    dve.wait_ge(got_in[s % 2], 32 * GATHERS * (s // 2 + 1))
                    collect(s, s % 2)

            @block.tensor
            def _(pe):
                def project(b, i, first):
                    pe.wait_ge(xt_done, b + 1)
                    if not first:
                        pe.wait_ge(xo_done, b - 1)
                    for n in range(2):
                        for k in range(KT):
                            t = nc.tensor.matmul(pp[i][:, n * 512:(n + 1) * 512], xt[i][:, k * P:(k + 1) * P],
                                                 g.w[:, k, n * 512:(n + 1) * 512], start=(k == 0), stop=(k == KT - 1))
                    t.then_inc(pp_done, 1)

                project(0, 0, True)
                project(1, 1, True)
                with pe.Fori(2, NB - 1, 2) as b:
                    for i in range(2):
                        project(b + i, i, False)
                project(NB - 1, 0, False)

            @block.scalar
            def _(act):
                def copy(b, i, turn):
                    act.wait_ge(pp_done, b + 1)
                    if turn is not None:
                        act.wait_ge(xp_out[i], 16 * turn)
                    nc.scalar.copy(xo[i][:], pp[i][:]).then_inc(xo_done, 1)

                copy(0, 0, None)
                copy(1, 1, None)
                with act.Fori(1, (NB - 1) // 2) as t:
                    for i in range(2):
                        copy(t * 2 + i, i, t)
                copy(NB - 1, 0, (NB - 1) // 2)


def stage_weights(nc, g):
    with ExitStack() as ctx:
        sb = lambda n, s, d=F32: ctx.enter_context(nc.sbuf_tensor(n, s, d))
        ps = lambda n, s: ctx.enter_context(nc.psum_tensor(n, s, F32))
        rec = sb("rec_all", [P, EC, REC])
        first, last, nf, nl, seen_f, seen_l = (sb(n, [P, EC]) for n in ("first", "last", "nf", "nl", "seen_f", "seen_l"))
        fmax, bmax = sb("fmax", [P, EC, H]), sb("bmax", [P, EC, H])
        ew, mw, sw = sb("ew", [P, EC, H]), sb("mw", [P, EC, H]), sb("sw", [P, EC, H])
        tail4 = sb("tail4", [P, 2, H])
        rowt = sb("rowt", [H, 2, P])
        run = sb("run", [H, P])
        shifted = sb("shifted", [H, P])
        carry = sb("carry", [P, 2, H])
        tps = [ps(f"row_ps{i}", [P, 2, P]) for i in range(2)]
        cps = [ps(f"col_ps{i}", [P, H]) for i in range(2)]
        counts = sb("counts", [P, NB - 1])
        cnt_ps = ps("cnt_ps", [P, NB - 1])
        cnt_i = sb("cnt_i", [P, NB - 1], I32)
        step_at = sb("step_at", [P, NB - 1])
        passed = g.big[:].rearrange("p b n -> p (b n)")[:, 0:ITEMS * (NB - 1)].rearrange("p (i k) -> p i k", k=NB - 1)
        blk_f, chk_f = sb("blk_f", [P, ITEMS]), sb("chk_f", [P, ITEMS])
        own_dve, t_in, t_done, r_in, c_done, cnt_in, cnt_done, e_in, e_done, rec_done, rec_out, zeroed = new_sems(
            nc, g.ctx, "weights_dve", "tails_in", "tails_done", "runs_in", "carry_done", "cnt_in", "cnt_done",
            "exps_in", "exps_done", "rec_done", "rec_out", "acc_zeroed")
        a_s, d_s, d_d = (g.edge_a[:, :, i * H:(i + 1) * H] for i in range(3))
        with nc.Block() as block:
            @block.vector
            def _(dve):
                own = Links(dve, own_dve)
                v = nc.vector
                cur = g.dst_f[:, 1:EC + 1]
                own.add(v.tensor_tensor(first[:], cur, g.dst_f[:, 0:EC], ALU.not_equal))
                own.add(v.tensor_tensor(last[:], cur, g.dst_f[:, 2:EC + 2], ALU.not_equal))
                for k in range(1, NB):
                    own.link(v.tensor_scalar(nf[:], cur, float(k * P), None, ALU.is_lt, ALU.add, accum_out=counts[:, k - 1:k]))
                v.engine_nop().then_inc(cnt_in, 1)
                own.wait()
                own.add(v.tensor_scalar(nf[:], first[:], NEG, None, ALU.mult))
                own.add(v.tensor_scalar(nl[:], last[:], NEG, None, ALU.mult))
                own.add(v.tensor_tensor_scan(seen_f[:], first[:], first[:], 0.0, ALU.max, ALU.max))
                own.add(v.tensor_tensor_scan(seen_l[:, ::-1], last[:, ::-1], last[:, ::-1], 0.0, ALU.max, ALU.max))
                own.wait()
                own.add(v.tensor_scalar(seen_f[:], seen_f[:], NEG, None, ALU.mult))
                own.add(v.tensor_scalar(seen_l[:], seen_l[:], NEG, None, ALU.mult))
                own.wait()

                def carried(n, out, inp, seg, seen, tail, back):
                    rev = slice(None, None, -1) if back else slice(None)
                    for h in range(H):
                        own.add(v.tensor_tensor_scan(out[:, rev, h], seg[:, rev], inp[:, rev, h], NEG, ALU.add, ALU.max))
                    own.wait()
                    own.add(v.tensor_copy(tail4[:, 0, :], out[:, tail, :]))
                    own.link(v.tensor_copy(tail4[:, 1, :], seen[:, tail:tail + 1].broadcast_to([P, H])))
                    v.engine_nop().then_inc(t_in, 1)
                    dve.wait_ge(t_done, n + 1)
                    own.link(v.tensor_copy(rowt[:], tps[n][0:H, :, :]))
                    own.add(v.memset(shifted[:], NEG))
                    own.link(v.tensor_tensor_scan(run[:, rev], rowt[:, 1, rev], rowt[:, 0, rev], NEG, ALU.add, ALU.max))
                    if back:
                        own.link(v.tensor_copy(shifted[:, 0:P - 1], run[:, 1:P]))
                    else:
                        own.link(v.tensor_copy(shifted[:, 1:P], run[:, 0:P - 1]))
                    v.engine_nop().then_inc(r_in, 1)
                    dve.wait_ge(c_done, n + 1)
                    own.link(v.tensor_copy(carry[:, n, :], cps[n][:]))
                    for h in range(H):
                        own.add(v.scalar_tensor_tensor(out=out[:, :, h], in0=seen[:], scalar=carry[:, n, h:h + 1],
                                                       in1=out[:, :, h], op0=ALU.add, op1=ALU.max))
                    own.wait()

                carried(0, fmax, a_s, nf, seen_f, EC - 1, False)
                carried(1, bmax, fmax, nl, seen_l, 0, True)
                own.add(v.tensor_tensor(mw[:], bmax[:], d_s, ALU.max))
                own.add(v.tensor_tensor(ew[:], a_s, d_d, ALU.add))
                own.add(v.tensor_tensor(sw[:], d_s, d_d, ALU.add))
                own.wait()
                own.link(v.tensor_tensor(mw[:], mw[:], d_d, ALU.add))
                for t in (mw, ew, sw):
                    own.add(v.scalar_tensor_tensor(out=t[:], in0=t[:], scalar=SLOPE, in1=t[:], op0=ALU.mult, op1=ALU.max))
                own.wait()
                own.add(v.tensor_tensor(ew[:], ew[:], mw[:], ALU.subtract))
                own.link(v.tensor_tensor(sw[:], sw[:], mw[:], ALU.subtract))
                v.engine_nop().then_inc(e_in, 1)
                own.add(v.tensor_copy(rec[:, :, FIRST_AT:FIRST_AT + 1], first[:].unsqueeze(2)))
                own.add(v.tensor_copy(rec[:, :, DST_AT:DST_AT + 1], cur.unsqueeze(2)))
                own.add(v.memset(rec[:, :, DST_AT + 1:DST_AT + 2], 0.0))
                own.add(v.tensor_copy(rec[:, :, SRC_AT:SRC_AT + 1].bitcast(I32), g.src_i[:].unsqueeze(2)))
                dve.wait_ge(cnt_done, 1)
                own.link(v.tensor_scalar(counts[:], cnt_ps[:], float(-PADS), float(E - 1), ALU.add, ALU.min))
                own.link(v.tensor_copy(cnt_i[:], counts[:]))
                own.link(v.tensor_scalar(cnt_i[:], cnt_i[:], CH.bit_length() - 1, None, ALU.logical_shift_right))
                own.link(v.tensor_copy(counts[:], cnt_i[:]))
                own.link(v.tensor_tensor(step_at[:], counts[:], g.iota[:, 1:NB], ALU.add))
                own.link(v.tensor_tensor(passed, step_at[:].unsqueeze(1).broadcast_to([P, ITEMS, NB - 1]),
                                         g.iota[:, 0:ITEMS].unsqueeze(2).broadcast_to([P, ITEMS, NB - 1]), ALU.is_le))
                own.link(v.tensor_reduce(blk_f[:], passed, AX.X, ALU.add))
                own.link(v.tensor_tensor(chk_f[:], g.iota[:, 0:ITEMS], blk_f[:], ALU.subtract))
                own.add(v.tensor_copy(g.blk_i[:], blk_f[:]))
                own.link(v.tensor_copy(g.chk_i[:], chk_f[:]))
                dve.wait_ge(e_done, 2)
                own.link(v.tensor_tensor(rec[:, :, SELF_AT:SELF_AT + H], sw[:], first[:].unsqueeze(2).broadcast_to([P, EC, H]), ALU.mult))
                v.engine_nop().then_inc(rec_done, 1)
                v.memset(g.acc_side[:], 0.0).then_inc(zeroed, 1)
                v.memset(g.big[:], 0.0).then_inc(zeroed, 1)
                dve.wait_ge(zeroed, 2)

            @block.scalar
            def _(act):
                act.wait_ge(e_in, 1)
                nc.scalar.activation(rec[:, :, W_AT:W_AT + H], ew[:], ACT.Exp).then_inc(e_done, 1)
                nc.scalar.activation(sw[:], sw[:], ACT.Exp).then_inc(e_done, 1)

            @block.tensor
            def _(pe):
                pe.wait_ge(cnt_in, 1)
                nc.tensor.matmul(cnt_ps[:], g.ones[:], counts[:], start=True, stop=True).then_inc(cnt_done, 1)
                for n in range(2):
                    pe.wait_ge(t_in, n + 1)
                    nc.tensor.transpose(tps[n][0:H, 0, :], tail4[:, 0, :], g.ident[:])
                    nc.tensor.transpose(tps[n][0:H, 1, :], tail4[:, 1, :], g.ident[:]).then_inc(t_done, 1)
                    pe.wait_ge(r_in, n + 1)
                    nc.tensor.transpose(cps[n][:], shifted[:], g.ident[0:H, 0:H]).then_inc(c_done, 1)

            @block.sync
            def _(sp):
                sp.wait_ge(rec_done, 1)
                sp.wait_ge(e_done, 2)
                sp.dma_start(g.rec.rearrange("(p n) r -> p n r", p=P), rec[:]).then_inc(rec_out, 16)
                sp.wait_ge(rec_out, 16)


GB = 4


def stage_messages(nc, g):
    with ExitStack() as ctx:
        sb = lambda n, s, d=F32: ctx.enter_context(nc.sbuf_tensor(n, s, d))
        ps = lambda n, s: ctx.enter_context(nc.psum_tensor(n, s, F32))
        rec = [sb(f"rec{q}", [P, SUB, REC]) for q in range(GB)]
        got = [sb(f"rows{q}", [P, SUB, D]) for q in range(GB)]
        hot = [sb(f"hot{i}", [P, SUB, H + 1, P]) for i in range(2)]
        msg = [ps(f"msg{i}", [P, D]) for i in range(2)]
        side = [ps(f"side{i}", [P, FIRST_AT + 1]) for i in range(2)]
        rec_in = new_sems(nc, g.ctx, *[f"rec_in{q}" for q in range(GB)])
        got_in = new_sems(nc, g.ctx, *[f"rows_in{q}" for q in range(GB)])
        hot_done, sums_done, added, gated = new_sems(nc, g.ctx, "hot_done", "sums_done", "added", "messages_gated")
        assert ITEMS % GB == 0
        turns = ITEMS // GB

        def each(eng, body):
            for q in range(GB):
                body(q, 0, q, True)
            with eng.Fori(1, turns) as t:
                for q in range(GB):
                    body(t * GB + q, t, q, False)

        with nc.Block() as block:
            @block.sync
            def _(sp):
                def load(i, t, q, first):
                    c = sp.value_load(g.chk_i[0:1, bass.ds(i, 1)], min_val=0, max_val=NC - 1)
                    if not first:
                        sp.wait_ge(sums_done, i - GB + 1)
                    sp.dma_start(rec[q][:], g.rec[bass.ds(c * CH, CH), :].rearrange("(p k) r -> p k r", k=SUB)).then_inc(rec_in[q], 16)
                each(sp, load)

            @block.gpsimd
            def _(pool):
                nc.gpsimd.memset(g.gate[0:1, 1:2], 0.0).then_inc(gated, 1)

                def gather(i, t, q, first):
                    if not first:
                        pool.wait_ge(sums_done, i - GB + 1)
                    pool.wait_ge(rec_in[q], 16 * (t + 1))
                    gate(nc, g, gated, i)
                    for k in range(SUB):
                        nc.gpsimd.indirect_dma_start(
                            got[q][:, k, :], None, g.xp[:, :],
                            bass.IndirectOffsetOnAxis(rec[q][:, k, SRC_AT:SRC_AT + 1].bitcast(I32), 0)).then_inc(got_in[q], 16)
                each(pool, gather)

            @block.vector
            def _(dve):
                def weigh(i, t, q, first):
                    b = dve.value_load(g.blk_i[0:1, bass.ds(i, 1)], min_val=0, max_val=NB - 1)
                    nodes = g.iota[:, bass.ds(b * P, P)]
                    dve.wait_ge(rec_in[q], 16 * (t + 1))
                    if not (first and q < 2):
                        dve.wait_ge(sums_done, i - 1)
                    for k in range(SUB):
                        node = rec[q][:, k, DST_AT:DST_AT + 1]
                        for h in range(H):
                            nc.vector.tensor_scalar(hot[q % 2][:, k, h, :], nodes, node, rec[q][:, k, h:h + 1],
                                                    ALU.is_equal, ALU.mult)
                        ins = nc.vector.tensor_scalar(hot[q % 2][:, k, H, :], nodes, node, None, ALU.is_equal)
                    ins.then_inc(hot_done, 1)

                def add(i, q, first):
                    b = dve.value_load(g.blk_i[0:1, bass.ds(i, 1)], min_val=0, max_val=NB - 1)
                    dve.wait_ge(sums_done, i + 1)
                    if not first:
                        dve.wait_ge(added, 2 * i)
                    at = g.big[:, bass.ds(b, 1), :].rearrange("p a n -> p (a n)")
                    nc.vector.tensor_tensor(at, at, msg[q % 2][:], ALU.add).then_inc(added, 1)
                    at = g.acc_side[:, bass.ds(b, 1), :].rearrange("p a n -> p (a n)")
                    nc.vector.tensor_tensor(at, at, side[q % 2][:], ALU.add).then_inc(added, 1)

                def step(i, t, q, first):
                    weigh(i, t, q, first)
                    if not (first and q == 0):
                        add(i - 1, (q - 1) % GB, first and q == 1)
                each(dve, step)
                add(ITEMS - 1, GB - 1, False)

            @block.tensor
            def _(pe):
                def sums(i, t, q, first):
                    pe.wait_ge(hot_done, i + 1)
                    pe.wait_ge(got_in[q], 16 * SUB * (t + 1))
                    if not (first and q < 2):
                        pe.wait_ge(added, 2 * (i - 1))
                    for h in range(H):
                        for k in range(SUB):
                            nc.tensor.matmul(msg[q % 2][:, h * C:(h + 1) * C], hot[q % 2][:, k, h, :],
                                             got[q][:, k, h * C:(h + 1) * C], start=(k == 0), stop=(k == SUB - 1))
                    for k in range(SUB):
                        t_ = nc.tensor.matmul(side[q % 2][:], hot[q % 2][:, k, H, :], rec[q][:, k, 0:FIRST_AT + 1],
                                              start=(k == 0), stop=(k == SUB - 1))
                    t_.then_inc(sums_done, 1)
                each(pe, sums)


def stage_residual(nc, g, x, bias, gate_w, out):
    with ExitStack() as ctx:
        sb = lambda n, s, d=F32: ctx.enter_context(nc.sbuf_tensor(n, s, d))
        ps = lambda n, s: ctx.enter_context(nc.psum_tensor(n, s, F32))
        pair = lambda n, s: [sb(f"{n}{i}", s) for i in range(2)]
        xb, xpb, x1, xn, xt = (pair(n, [P, D]) for n in ("r_x", "r_xp", "r_x1", "r_xn", "r_xt"))
        t = sb("r_t", [P, D])
        bias_b = sb("bias_b", [P, D])
        gw = sb("gate_rows", [X, D])
        gwt = sb("gate_t", [P, KT, X])
        wself, rz = sb("wself", [P, NB, H]), sb("rz", [P, NB, H])
        stats, mv, std, rstd = pair("r_stats", [P, 12]), pair("r_mv", [P, 2]), pair("r_std", [P, 1]), pair("r_rstd", [P, 1])
        eps = sb("r_eps", [P, 1])
        top, tot = sb("r_top", [P, NB]), sb("r_tot", [P, NB])
        tp = [ps(f"r_tp{i}", [P, D]) for i in range(2)]
        sp_ = [ps(f"r_sc{i}", [P, X]) for i in range(2)]
        gp = ps("gate_ps", [P, KT, X])
        (cons_in, own_dve, gp_done, gwt_done, x1_done, var_done, std_done, xn_done, tp_done, xt_done, sc_done,
         sc_copied, soft_in, soft_done, r_chain) = new_sems(
            nc, g.ctx, "r_consts_in", "residual_dve", "gate_ps_done", "gate_t_done", "x1_done", "r_var_done", "r_std_done",
            "r_xn_done", "r_tp_done", "r_xt_done", "r_sc_done", "r_sc_copied", "soft_in", "soft_done", "r_chain")
        loaded = new_sems(nc, g.ctx, "r_in0", "r_in1")
        stored = new_sems(nc, g.ctx, "r_out0", "r_out1")

        def each(eng, body):
            for i in range(2):
                body(i, i, 0, True)
            with eng.Fori(1, NB // 2) as n:
                for i in range(2):
                    body(n * 2 + i, i, n, False)
            body(NB - 1, 0, NB // 2, False)

        def last(b):
            return isinstance(b, int) and b == NB - 1

        with nc.Block() as block:
            @block.sync
            def _(sp):
                sp.dma_start(gw[:], gate_w).then_inc(cons_in, 16)
                sp.dma_start(bias_b[:], bias.unsqueeze(0).broadcast_to([P, D])).then_inc(cons_in, 16)

                def load(b, i, n, first):
                    if not first:
                        sp.wait_ge(x1_done, b - 1)
                    r = LAST if last(b) else P
                    sp.dma_start(xb[i][0:r, :], x[bass.ds(b * P, r), :]).then_inc(loaded[i], 16)
                    sp.dma_start(xpb[i][:], g.xp[bass.ds(b * P, P), :]).then_inc(loaded[i], 16)

                def store(b, i, n, first):
                    r = LAST if last(b) else P
                    sp.wait_ge(xn_done, b + 1)
                    sp.dma_start(out[bass.ds(b * P, r), :], x1[i][0:r, :]).then_inc(stored[i], 16)
                    sp.dma_start(g.xn1[bass.ds(b * P, r), :], xn[i][0:r, :]).then_inc(stored[i], 16)

                def both(b, i, n, first):
                    load(b, i, n, first)
                    if not (first and i == 0):
                        store(b - 1, 1 - i, n, first)
                each(sp, both)
                store(NB - 1, 0, NB // 2, False)
                sp.wait_ge(stored[0], 32 * ((NB + 1) // 2))
                sp.wait_ge(stored[1], 32 * (NB // 2))

            @block.vector
            def _(dve):
                v = nc.vector
                own = Links(dve, own_dve)
                own.add(v.memset(eps[:], EPS))
                have = g.acc_side[:, :, FIRST_AT:FIRST_AT + 1].broadcast_to([P, NB, H])
                own.link(v.tensor_tensor(wself[:], g.acc_side[:, :, SELF_AT:SELF_AT + H], have, ALU.subtract))
                own.link(v.tensor_scalar(wself[:], wself[:], 1.0, None, ALU.add))
                own.link(v.tensor_tensor(rz[:], g.acc_side[:, :, 0:H], wself[:], ALU.add))
                own.link(v.reciprocal(rz[:], rz[:]))
                dve.wait_ge(gp_done, 1)
                v.tensor_copy(gwt[:], gp[:]).then_inc(gwt_done, 1)
                dve.wait_ge(cons_in, 32)

                def residual(b, i, n, first):
                    base = b * 5
                    dve.wait_ge(loaded[i], 32 * (n + 1))
                    acc = g.big[:, bass.ds(b, 1), :].rearrange("p a n -> p (a n)")
                    own_w = wself[:, bass.ds(b, 1), :].rearrange("p a n -> p (a n)")
                    inv = rz[:, bass.ds(b, 1), :].rearrange("p a n -> p (a n)")
                    for h in range(H):
                        c = slice(h * C, (h + 1) * C)
                        ins = v.scalar_tensor_tensor(out=xpb[i][:, c], in0=xpb[i][:, c], scalar=own_w[:, h:h + 1],
                                                     in1=acc[:, c], op0=ALU.mult, op1=ALU.add)
                    ins.then_inc(r_chain, 1)
                    dve.wait_ge(r_chain, base + 1)
                    for h in range(H):
                        c = slice(h * C, (h + 1) * C)
                        ins = v.scalar_tensor_tensor(out=t[:, c], in0=xpb[i][:, c], scalar=inv[:, h:h + 1],
                                                     in1=bias_b[:, c], op0=ALU.mult, op1=ALU.add)
                    ins.then_inc(r_chain, 1)
                    dve.wait_ge(r_chain, base + 2)
                    if not first:
                        dve.wait_ge(stored[i], 32 * n)
                        dve.wait_ge(tp_done, b - 1)
                    v.scalar_tensor_tensor(out=x1[i][:], in0=t[:], scalar=0.0, in1=xb[i][:], op0=ALU.max,
                                           op1=ALU.add).then_inc(x1_done, 1)
                    dve.wait_ge(x1_done, b + 1)
                    v.bn_stats(stats[i][:, 0:6], x1[i][:, 0:512]).then_inc(r_chain, 1)
                    v.bn_stats(stats[i][:, 6:12], x1[i][:, 512:1024]).then_inc(r_chain, 1)
                    dve.wait_ge(r_chain, base + 4)
                    if not (first and i == 0):
                        copy_scores(b - 1, 1 - i)
                    v.bn_aggr(mv[i][:], stats[i][:]).then_inc(var_done, 1)
                    dve.wait_ge(var_done, b + 1)
                    dve.wait_ge(std_done, b + 1)
                    v.reciprocal(rstd[i][:], std[i][:]).then_inc(r_chain, 1)
                    dve.wait_ge(r_chain, base + 5)
                    v.tensor_scalar(xn[i][:], x1[i][:], mv[i][:, 0:1], rstd[i][:], ALU.subtract, ALU.mult).then_inc(xn_done, 1)

                def copy_scores(b, i):
                    dve.wait_ge(sc_done, b + 1)
                    v.tensor_copy(g.prob[:, bass.ds(b, 1), :].rearrange("p a n -> p (a n)"), sp_[i][:]).then_inc(sc_copied, 1)

                each(dve, residual)
                copy_scores(NB - 1, 0)
                dve.wait_ge(sc_copied, NB)
                wide = lambda a: a[:].unsqueeze(2).broadcast_to([P, NB, X])
                own.link(v.tensor_reduce(top[:], g.prob[:], AX.X, ALU.max))
                own.link(v.tensor_tensor(g.prob[:], g.prob[:], wide(top), ALU.subtract))
                v.tensor_copy(top[:], top[:]).then_inc(soft_in, 1)
                dve.wait_ge(soft_done, 1)
                own.link(v.tensor_reduce(tot[:], g.prob[:], AX.X, ALU.add))
                own.link(v.reciprocal(tot[:], tot[:]))
                own.link(v.tensor_tensor(g.prob[:], g.prob[:], wide(tot), ALU.mult))

            @block.scalar
            def _(act):
                def step(b, i, n, first):
                    act.wait_ge(var_done, b + 1)
                    nc.scalar.activation(std[i][:], mv[i][:, 1:2], ACT.Sqrt, bias=eps[:]).then_inc(std_done, 1)
                    act.wait_ge(tp_done, b + 1)
                    if not first:
                        act.wait_ge(sc_done, b - 1)
                    nc.scalar.copy(xt[i][:], tp[i][:]).then_inc(xt_done, 1)
                each(act, step)
                act.wait_ge(soft_in, 1)
                nc.scalar.activation(g.prob[:], g.prob[:], ACT.Exp).then_inc(soft_done, 1)

            @block.tensor
            def _(pe):
                pe.wait_ge(cons_in, 32)
                for k in range(KT):
                    m = nc.tensor.transpose(gp[:, k, :], gw[:, k * P:(k + 1) * P], g.ident[0:X, 0:X])
                m.then_inc(gp_done, 1)
                pe.wait_ge(gwt_done, 1)

                def step(b, i, n, first):
                    pe.wait_ge(xn_done, b + 1)
                    if not first:
                        pe.wait_ge(xt_done, b - 1)
                    for k in range(KT):
                        m = nc.tensor.transpose(tp[i][:, k * P:(k + 1) * P], xn[i][:, k * P:(k + 1) * P], g.ident[:])
                    m.then_inc(tp_done, 1)
                    pe.wait_ge(xt_done, b + 1)
                    if not first:
                        pe.wait_ge(sc_copied, b - 1)
                    for k in range(KT):
                        m = nc.tensor.matmul(sp_[i][:], xt[i][:, k * P:(k + 1) * P], gwt[:, k, :],
                                             start=(k == 0), stop=(k == KT - 1))
                    m.then_inc(sc_done, 1)
                each(pe, step)


SHIFTS = list(range(28, -1, -4))


def stage_select(nc, g):
    with ExitStack() as ctx:
        sb = lambda n, s, d=F32: ctx.enter_context(nc.sbuf_tensor(n, s, d))
        ps = lambda n, s: ctx.enter_context(nc.psum_tensor(n, s, F32))
        tid, valid = sb("tid", [P, NB]), sb("valid", [P, NB])
        rep = sb("rep", [P, NB, X, REP])
        prow, over, tie, rank = (sb(n, [P, NP]) for n in ("prow", "over", "tie", "rank"))
        pi, ji, pf = sb("sel_pi", [P, 1], I32), sb("sel_ji", [P, 1], I32), sb("sel_pf", [P, 1])
        steps = sb("sel_steps", [P, len(SHIFTS)], I32)
        gi, gf, same = sb("sel_gi", [P, P], I32), sb("sel_gf", [P, P]), sb("sel_same", [P, P])
        found, trial, dig = (sb(n, [P, 1], I32) for n in ("sel_found", "sel_trial", "sel_dig"))
        cnt, enough, digf = (sb(n, [P, 1]) for n in ("sel_cnt", "sel_enough", "sel_digf"))
        slot, slot_i = sb("slot", [P, NB, X]), sb("slot_i", [P, NB, X], I32)
        lo_i, hi_i = sb("lo_i", [P, NB, X], I32), sb("hi_i", [P, NB, X], I32)
        lo, hi = sb("lo", [P, NB, X]), sb("hi", [P, NB, X])
        mask = sb("mask", [P, NB, X, ST])
        val = sb("val", [P, NB * X, 2, ST])
        lo_hot = [sb(f"lo_hot{i}", [P, NB, P]) for i in range(2)]
        tp = [ps(f"sel_tp{i}", [P, 512]) for i in range(2)]
        vp = ps("sel_votes", [P, 1])
        lp = [ps(f"sel_list{i}", [P, 2 * ST]) for i in range(2)]
        own_dve, rep_done, tp_done, tp_copied, votes_in, votes_done, slot_done, hot_done, list_done, list_copied = new_sems(
            nc, g.ctx, "select_dve", "rep_done", "sel_tp_done", "sel_tp_copied", "votes_in", "votes_done", "slots_done",
            "lo_hot_done", "list_done", "list_copied")
        groups = [(n, min(4, NB - n)) for n in range(0, NB, 4)]
        with nc.Block() as block:
            @block.vector
            def _(dve):
                v = nc.vector
                own = Links(dve, own_dve)
                own.link(v.tensor_scalar(tid[:], g.iota[:, 0:NB], float(P), g.pcol[:], ALU.mult, ALU.add))
                own.link(v.tensor_scalar(valid[:], tid[:], float(N), None, ALU.is_lt))
                wide = lambda a: a[:].unsqueeze(2).broadcast_to([P, NB, X])
                own.link(v.tensor_tensor(g.prob[:], g.prob[:], wide(valid), ALU.mult))
                own.link(v.tensor_scalar(valid[:], valid[:], -1.0, None, ALU.add))
                own.link(v.tensor_tensor(g.prob[:], g.prob[:], wide(valid), ALU.add))
                own.link(v.tensor_copy(rep[:], g.prob[:].unsqueeze(3).broadcast_to([P, NB, X, REP])))
                v.engine_nop().then_inc(rep_done, 1)
                own.link(v.tensor_copy(pi[:], g.pcol[:]))
                own.link(v.tensor_scalar(ji[:], pi[:], REP - 1, None, ALU.bitwise_and))
                for n, s in enumerate(SHIFTS):
                    if n == 0:
                        own.link(v.tensor_scalar(steps[:, 0:1], ji[:], 3, s, ALU.bitwise_and, ALU.logical_shift_left))
                    else:
                        own.link(v.tensor_scalar(steps[:, n:n + 1], ji[:], s, None, ALU.logical_shift_left))
                own.link(v.tensor_scalar(pi[:], pi[:], REP.bit_length() - 1, None, ALU.logical_shift_right))
                own.link(v.tensor_copy(pf[:], pi[:]))
                own.link(v.tensor_copy(gi[:], g.iota[:, 0:P]))
                own.link(v.tensor_scalar(gi[:], gi[:], REP.bit_length() - 1, None, ALU.logical_shift_right))
                own.link(v.tensor_copy(gf[:], gi[:]))
                own.link(v.tensor_scalar(same[:], gf[:], pf[:], None, ALU.is_equal))
                own.link(v.memset(found[:], 0))

                for n, (b, k) in enumerate(groups):
                    dve.wait_ge(tp_done, n + 1)
                    v.tensor_copy(prow[:, b * P:(b + k) * P], tp[n % 2][:, 0:k * P]).then_inc(tp_copied, 1)
                dve.wait_ge(tp_copied, len(groups))

                for n, s in enumerate(SHIFTS):
                    own.link(v.tensor_tensor(trial[:], found[:], steps[:, n:n + 1], ALU.bitwise_or))
                    own.link(v.tensor_scalar(rank[:], prow[:], trial[:].bitcast(F32), None, ALU.is_ge, ALU.add, accum_out=cnt[:]))
                    own.link(v.tensor_scalar(enough[:], cnt[:], float(TOPK), None, ALU.is_ge))
                    v.engine_nop().then_inc(votes_in, 1)
                    dve.wait_ge(votes_done, n + 1)
                    own.link(v.tensor_scalar(digf[:], vp[:], 0.25 if n == 0 else 1.0, -1.0, ALU.mult, ALU.add))
                    own.link(v.tensor_copy(dig[:], digf[:]))
                    own.link(v.tensor_scalar(dig[:], dig[:], s, None, ALU.logical_shift_left))
                    own.link(v.tensor_tensor(found[:], found[:], dig[:], ALU.bitwise_or))

                thr = found[:].bitcast(F32)
                own.link(v.tensor_scalar(over[:], prow[:], thr, None, ALU.is_gt, ALU.add, accum_out=cnt[:]))
                own.add(v.tensor_scalar(cnt[:], cnt[:], -1.0, float(TOPK), ALU.mult, ALU.add))
                own.link(v.tensor_scalar(tie[:], prow[:], thr, None, ALU.is_equal))
                own.link(v.tensor_tensor_scan(rank[:], tie[:], tie[:], 0.0, ALU.add, ALU.max))
                own.link(v.scalar_tensor_tensor(out=tie[:], in0=rank[:], scalar=cnt[:], in1=tie[:], op0=ALU.is_le, op1=ALU.mult))
                own.link(v.tensor_tensor(over[:], over[:], tie[:], ALU.add))
                own.link(v.tensor_tensor_scan(rank[:], over[:], over[:], 0.0, ALU.add, ALU.max))
                own.link(v.tensor_tensor(rank[:], rank[:], over[:], ALU.mult))
                own.link(v.tensor_scalar(rank[:], rank[:], -1.0, None, ALU.add))
                v.engine_nop().then_inc(slot_done, 1)
                for n, (b, k) in enumerate(groups):
                    n += len(groups)
                    dve.wait_ge(tp_done, n + 1)
                    view = tp[n % 2][:, 0:k * P].rearrange("p (b x r) -> p b x r", x=X, r=REP)[:, :, :, 0]
                    v.tensor_copy(slot[:, b:b + k, :], view).then_inc(tp_copied, 1)
                dve.wait_ge(tp_copied, 2 * len(groups))
                own.link(v.tensor_copy(slot_i[:], slot[:]))
                own.add(v.tensor_scalar(lo_i[:], slot_i[:], P - 1, None, ALU.bitwise_and))
                own.link(v.tensor_scalar(hi_i[:], slot_i[:], P.bit_length() - 1, None, ALU.arith_shift_right))
                own.add(v.tensor_copy(lo[:], lo_i[:]))
                own.link(v.tensor_copy(hi[:], hi_i[:]))
                flat = lambda a: a.rearrange("p b x -> p (b x)").unsqueeze(2).broadcast_to([P, NB * X, ST])
                m = mask[:].rearrange("p b x t -> p (b x) t")
                own.link(v.tensor_tensor(m, flat(hi[:]), g.iota[:, 0:ST].unsqueeze(1).broadcast_to([P, NB * X, ST]), ALU.is_equal))
                own.add(v.tensor_tensor(val[:, :, 1, :], m, flat(g.prob[:]), ALU.mult))
                own.link(v.tensor_copy(rep[:, :, :, 0], tid[:].unsqueeze(2).broadcast_to([P, NB, X])))
                own.link(v.tensor_tensor(val[:, :, 0, :], m, flat(rep[:, :, :, 0]), ALU.mult))

                def hot(e, i, first):
                    if not first:
                        dve.wait_ge(list_done, e - 1)
                    v.tensor_tensor(lo_hot[i][:], lo[:, :, bass.ds(e, 1)].broadcast_to([P, NB, P]),
                                    g.iota[:, 0:P].unsqueeze(1).broadcast_to([P, NB, P]), ALU.is_equal).then_inc(hot_done, 1)

                def keep(e, i):
                    dve.wait_ge(list_done, e + 1)
                    v.tensor_copy(g.tok_i[:, bass.ds(e, 1), :].rearrange("p a t -> p (a t)"), lp[i][:, 0:ST]).then_inc(list_copied, 1)
                    v.tensor_copy(g.tok_p[:, bass.ds(e, 1), :].rearrange("p a t -> p (a t)"), lp[i][:, ST:2 * ST]).then_inc(list_copied, 1)

                hot(0, 0, True)
                hot(1, 1, True)
                with dve.Fori(1, X // 2) as n:
                    for i in range(2):
                        keep(n * 2 - 2 + i, i)
                        hot(n * 2 + i, i, False)
                keep(X - 2, 0)
                keep(X - 1, 1)
                dve.wait_ge(list_copied, 2 * X)

            @block.tensor
            def _(pe):
                for n, (b, k) in enumerate(groups):
                    if n == 0:
                        pe.wait_ge(rep_done, 1)
                    if n >= 2:
                        pe.wait_ge(tp_copied, n - 1)
                    for j in range(k):
                        m = nc.tensor.transpose(tp[n % 2][:, j * P:(j + 1) * P],
                                                rep[:, b + j, :, :].rearrange("p x r -> p (x r)"), g.ident[:])
                    m.then_inc(tp_done, 1)
                for n in range(len(SHIFTS)):
                    pe.wait_ge(votes_in, n + 1)
                    nc.tensor.matmul(vp[:], same[:], enough[:], start=True, stop=True).then_inc(votes_done, 1)
                for n, (b, k) in enumerate(groups):
                    n += len(groups)
                    if n == len(groups):
                        pe.wait_ge(slot_done, 1)
                    pe.wait_ge(tp_copied, n - 1)
                    for j in range(k):
                        m = nc.tensor.transpose(tp[n % 2][:, j * P:(j + 1) * P], rank[:, (b + j) * P:(b + j + 1) * P], g.ident[:])
                    m.then_inc(tp_done, 1)

                def lists(e, i, first):
                    pe.wait_ge(hot_done, e + 1)
                    if not first:
                        pe.wait_ge(list_copied, 2 * (e - 1))
                    for b in range(NB):
                        m = nc.tensor.matmul(lp[i][:], lo_hot[i][:, b, :],
                                             val[:, bass.ds(e + b * X, 1), :, :].rearrange("p a v t -> p (a v t)"),
                                             start=(b == 0), stop=(b == NB - 1))
                    m.then_inc(list_done, 1)
                lists(0, 0, True)
                lists(1, 1, True)
                with pe.Fori(1, X // 2) as n:
                    for i in range(2):
                        lists(n * 2 + i, i, False)


def stage_experts(nc, g, w1, w2, out):
    with ExitStack() as ctx:
        sb = lambda n, s, d=F32: ctx.enter_context(nc.sbuf_tensor(n, s, d))
        ps = lambda n, s: ctx.enter_context(nc.psum_tensor(n, s, F32))
        w1s = [sb(f"w1s{i}", [P, KT, FH]) for i in range(2)]
        w2s = [sb(f"w2s{i}", [P, FT, D]) for i in range(2)]
        xg = sb("xg", [P, ST, D])
        xt = sb("e_xt", [P, KT, TOPK])
        ht = sb("e_ht", [P, FT, TOPK])
        ob = [sb(f"e_out{i}", [P, D]) for i in range(2)]
        idx = [sb(f"e_idx{i}", [P, ST], I32) for i in range(2)]
        pr = [sb(f"e_pr{i}", [P, ST]) for i in range(2)]
        tp = [ps(f"e_tp{i}", [P, 4, P]) for i in range(2)]
        hp = [ps(f"e_hp{i}", [P, 512]) for i in range(2)]
        op = [ps(f"e_op{i}", [P, D]) for i in range(2)]
        idx_done, tp_done, tp_copied, h_done, h_copied, o_done, o_scaled, gated, padded = new_sems(
            nc, g.ctx, "e_idx_done", "e_tp_done", "e_tp_copied", "e_h_done", "e_h_copied",
            "e_o_done", "e_o_scaled", "experts_gated", "e_padded")
        w1_in = new_sems(nc, g.ctx, "w1_in0", "w1_in1")
        w2_in = new_sems(nc, g.ctx, "w2_in0", "w2_in1")
        xg_in = new_sems(nc, g.ctx, *[f"xg_in{t}" for t in range(ST)])
        o_out = new_sems(nc, g.ctx, "o_out0", "o_out1")
        size = lambda t: P if t < ST - 1 else SLAST
        halves = [(0, (TOPK + 1) // 2), ((TOPK + 1) // 2, TOPK)]
        UT = 2 * ST
        UH = FT * len(halves)
        uses = [(ST + 1) // 2, ST // 2]

        def each(eng, body):
            body(0, 0, 0, True, False)
            with eng.Fori(0, X // 2 - 1) as n:
                body(n * 2 + 1, 1, n, False, False)
                body(n * 2 + 2, 0, n + 1, False, False)
            body(X - 1, 1, X // 2 - 1, False, True)

        with nc.Block() as block:
            @block.sync
            def _(sp):
                for e in range(X):
                    i = e % 2
                    if e >= 2:
                        sp.wait_ge(h_done, UH * (e - 1))
                    sp.dma_start(w1s[i][:], w1[e].rearrange("(k p) f -> p k f", p=P)).then_inc(w1_in[i], 16)
                    if e >= 2:
                        sp.wait_ge(o_done, ST * (e - 1))
                    sp.dma_start(w2s[i][:], w2[e].rearrange("(k p) d -> p k d", p=P)).then_inc(w2_in[i], 16)

            @block.gpsimd
            def _(pool):
                nc.gpsimd.memset(g.gate[0:1, 1:2], 0.0).then_inc(gated, 1)

                def gather(e, i, turn):
                    pool.wait_ge(idx_done, 2 * e + 2)
                    if turn is not None:
                        pool.wait_ge(tp_done, UT * e)
                    gate(nc, g, gated, turn if turn is not None else 0)
                    for t in range(ST):
                        nc.gpsimd.indirect_dma_start(
                            xg[0:size(t), t, :], None, g.xn1[:, :],
                            bass.IndirectOffsetOnAxis(idx[i][0:size(t), t:t + 1], 0)).then_inc(xg_in[t], 16)

                def scatter(e, i, n, first, last):
                    base = e * (ST + 1) + 1
                    if not last:
                        gather(e + 1, 1 - i, base)
                    for t in range(ST):
                        if t == 0 and not first:
                            for j in range(2):
                                pool.wait_ge(o_out[j], 16 * uses[j] * e)
                        pool.wait_ge(o_scaled, ST * e + t + 1)
                        gate(nc, g, gated, base + t + (0 if last else 1))
                        nc.gpsimd.indirect_dma_start(
                            out[:, :], bass.IndirectOffsetOnAxis(idx[i][0:size(t), t:t + 1], 0), ob[t % 2][0:size(t), :],
                            None, bounds_check=N - 1, oob_is_err=True, compute_op=ALU.add).then_inc(o_out[t % 2], 16)
                pool.wait_ge(padded, 1)
                gather(0, 0, None)
                each(pool, scatter)
                for j in range(2):
                    pool.wait_ge(o_out[j], 16 * uses[j] * X)

            @block.vector
            def _(dve):
                v = nc.vector

                def lists(e, i, first):
                    if not first:
                        for j in range(2):
                            dve.wait_ge(o_out[j], 16 * uses[j] * (e - 1))
                    v.tensor_copy(idx[i][:], g.tok_i[:, bass.ds(e, 1), :].rearrange("p a t -> p (a t)")).then_inc(idx_done, 1)
                    v.tensor_copy(pr[i][:], g.tok_p[:, bass.ds(e, 1), :].rearrange("p a t -> p (a t)")).then_inc(idx_done, 1)

                def scale(e, i, n, first, last):
                    if not last:
                        lists(e + 1, 1 - i, first)
                    dve.wait_ge(idx_done, 2 * e + 2)
                    for t in range(ST):
                        j = t % 2
                        dve.wait_ge(o_done, ST * e + t + 1)
                        if not (first and t < 2):
                            dve.wait_ge(o_out[j], 16 * (uses[j] * e + t // 2))
                        v.tensor_scalar(ob[j][0:size(t), :], op[j][0:size(t), :], pr[i][0:size(t), t:t + 1], None,
                                        ALU.mult).then_inc(o_scaled, 1)
                v.memset(xg[:, ST - 1, :], 0.0).then_inc(padded, 1)
                lists(0, 0, True)
                each(dve, scale)

            @block.scalar
            def _(act):
                def turn(e, first):
                    if not first:
                        act.wait_ge(h_done, UH * e)
                    for u in range(UT):
                        t, k = u // 2, (u % 2) * 4
                        act.wait_ge(tp_done, UT * e + u + 1)
                        nc.scalar.copy(xt[:, k:k + 4, t * P:t * P + size(t)], tp[u % 2][:, :, 0:size(t)]).then_inc(tp_copied, 1)

                def step(e, i, n, first, last):
                    if not first:
                        act.wait_ge(o_done, ST * e)
                    for u in range(UH):
                        f, (a, b) = u // 2, halves[u % 2]
                        act.wait_ge(h_done, UH * e + u + 1)
                        nc.scalar.activation(ht[:, f, a:b], hp[u % 2][:, 0:b - a], ACT.Gelu).then_inc(h_copied, 1)
                    if not last:
                        turn(e + 1, False)
                turn(0, True)
                each(act, step)

            @block.tensor
            def _(pe):
                def turn(e, first):
                    for u in range(UT):
                        t, k = u // 2, (u % 2) * 4
                        if u % 2 == 0:
                            pe.wait_ge(xg_in[t], 16 * (e + 1))
                        if not (first and u < 2):
                            pe.wait_ge(tp_copied, UT * e + u - 1)
                        for j in range(4):
                            m = nc.tensor.transpose(tp[u % 2][:, j, :], xg[:, t, (k + j) * P:(k + j + 1) * P], g.ident[:])
                        m.then_inc(tp_done, 1)

                def step(e, i, n, first, last):
                    pe.wait_ge(tp_copied, UT * (e + 1))
                    pe.wait_ge(w1_in[i], 16 * (n + 1))
                    for u in range(UH):
                        f, (a, b) = u // 2, halves[u % 2]
                        if not (first and u < 2):
                            pe.wait_ge(h_copied, UH * e + u - 1)
                        for k in range(KT):
                            m = nc.tensor.matmul(hp[u % 2][:, 0:b - a], w1s[i][:, k, f * P:(f + 1) * P], xt[:, k, a:b],
                                                 start=(k == 0), stop=(k == KT - 1))
                        m.then_inc(h_done, 1)
                    if not last:
                        turn(e + 1, False)
                    pe.wait_ge(h_copied, UH * (e + 1))
                    pe.wait_ge(w2_in[i], 16 * (n + 1))
                    for t in range(ST):
                        if not (first and t < 2):
                            pe.wait_ge(o_scaled, ST * e + max(t - 1, 0))
                        for n_ in range(2):
                            for f in range(FT):
                                m = nc.tensor.matmul(op[t % 2][0:size(t), n_ * 512:(n_ + 1) * 512],
                                                     ht[:, f, t * P:t * P + size(t)], w2s[i][:, f, n_ * 512:(n_ + 1) * 512],
                                                     start=(f == 0), stop=(f == FT - 1))
                        m.then_inc(o_done, 1)
                turn(0, True)
                each(pe, step)


def build(nc, x, src, dst, W, att_src, att_dst, bias, gate_w, w1, w2, out):
    from_dram = lambda n, s, d=F32: nc.dram_tensor(n, s, d).ap()
    with ExitStack() as top:
        g = Core()
        g.ctx = top
        g.a_src = from_dram("a_src_table", (NP, H))
        g.a_both = from_dram("a_both_table", (NP, 2 * H))
        g.xp = from_dram("xp_rows", (NP, D))
        g.rec = from_dram("edge_records", (NC * CH, REC))
        g.xn1 = from_dram("xn1_rows", (N, D))
        setup(nc, top, g)
        keep = lambda c, n, s, d=F32: c.enter_context(nc.sbuf_tensor(n, s, d))
        g.prob = keep(top, "prob", [P, NB, X])
        g.tok_i = keep(top, "tok_i", [P, X, ST], I32)
        g.tok_p = keep(top, "tok_p", [P, X, ST])
        with ExitStack() as gnn:
            g.big = keep(gnn, "big", [P, NB, D])
            g.acc_side = keep(gnn, "acc_side", [P, NB, 2 * H + 1])
            g.blk_i = keep(gnn, "blk_i", [P, ITEMS], I32)
            g.chk_i = keep(gnn, "chk_i", [P, ITEMS], I32)
            with ExitStack() as mid:
                g.dst_i = keep(mid, "dst_i", [P, EC + 2], I32)
                g.src_i = keep(mid, "src_i", [P, EC], I32)
                g.dst_f = keep(mid, "dst_f", [P, EC + 2])
                g.edge_a = keep(mid, "edge_a", [P, EC, 3 * H])
                with ExitStack() as first:
                    g.w = keep(first, "w_proj", [P, KT, D])
                    g.atab = keep(first, "atab", [P, NB, 2 * H])
                    atab_out, = new_sems(nc, top, "atab_out")
                    stage_nodes(nc, g, atab_out, x, W, att_src, att_dst)
                    stage_project(nc, g, atab_out, src, dst)
                stage_weights(nc, g)
            stage_messages(nc, g)
            stage_residual(nc, g, x, bias, gate_w, out)
        stage_select(nc, g)
        stage_experts(nc, g, w1, w2, out)


_INS = ["x", "src", "dst", "L0_gnn_W", "L0_gnn_att_src", "L0_gnn_att_dst", "L0_gnn_bias", "L0_ffn_gate_w",
        "L0_ffn_w1", "L0_ffn_w2"]


def kernel(**inputs):
    import numpy as np
    import concourse.bacc as bacc
    from concourse.bass_utils import run_bass_kernel_spmd

    nc = bacc.Bacc("TRN2", target_bir_lowering=False, num_devices=1)
    arrays, args = {}, []
    for name in _INS:
        a = np.ascontiguousarray(inputs[name])
        arrays[f"in_{name}"] = a
        args.append(nc.dram_tensor(f"in_{name}", a.shape, mybir.dt.from_np(a.dtype), kind="ExternalInput").ap())
    args.append(nc.dram_tensor("out_rows", (N, D), F32, kind="ExternalOutput").ap())
    build(nc, *args)
    r = run_bass_kernel_spmd(nc, [arrays], core_ids=[0])
    return r.results[0]["out_rows"]
```

```python
from contextlib import ExitStack

import concourse.bass as bass
from concourse import mybir

F32 = mybir.dt.float32
I32 = mybir.dt.int32
F32R = mybir.dt.float32r
BF16 = mybir.dt.bfloat16
ALU = mybir.AluOpType
ACT = mybir.ActivationFunctionType
AX = mybir.AxisListType

P = 128
N = 3125
D = 1024
KT = D // P
NB = -(-N // P)
LAST = N - (NB - 1) * P
NP = NB * P
H = 4
C = D // H
E = 50000
SUB = 2
CH = SUB * P
NC = -(-E // (8 * P)) * 8 // SUB
EC = NC * CH // P
PADS = NC * CH - E
ELAST = E - (P - 1) * EC
PATH = 55
ITEMS = NC + NB - 1
REC = 12
W_AT, SELF_AT, FIRST_AT, DST_AT, SRC_AT = 0, 4, 8, 9, 11
SLOPE = 0.2
EPS = 1e-5
NEG = -1e38
X = 8
FH = 512
FT = FH // P
TOPK = 2 * N // X
ST = -(-TOPK // P)
SLAST = TOPK - (ST - 1) * P
REP = P // X


class Links:

    def __init__(self, eng, sem):
        self.eng, self.sem, self.n = eng, sem, 0

    def add(self, ins):
        ins.then_inc(self.sem, 1)
        self.n += 1

    def wait(self):
        self.eng.wait_ge(self.sem, self.n)

    def link(self, ins):
        self.add(ins)
        self.wait()


class Core:
    pass


def new_sems(nc, ctx, *names):
    return [ctx.enter_context(nc.semaphore(n)) for n in names]


def gate(nc, g, sem, turn):
    nc.gpsimd.wait_ge(sem, turn + 1)
    nc.gpsimd.tensor_tensor(g.gate[0:1, 1:2], g.gate[0:1, 0:1], g.gate[0:1, 0:1], ALU.add).then_inc(sem, 1)


def rows(b):
    return P if b < NB - 1 else LAST


def setup(nc, ctx, g):
    sb = lambda n, s, d=F32: ctx.enter_context(nc.sbuf_tensor(n, s, d))
    g.iota = sb("iota", [P, NP])
    g.ident = sb("ident", [P, P])
    g.gate = sb("gate", [P, 2])
    g.pcol = sb("pcol", [P, 1])
    iota_done, consts_done = new_sems(nc, ctx, "iota_done", "consts_done")
    with nc.sbuf_tensor("iota_int", [P, NP], I32) as ints, nc.sbuf_tensor("pcol_int", [P, 1], I32) as pint, nc.Block() as block:
        @block.gpsimd
        def _(pool):
            nc.gpsimd.iota(ints[:], [[1, NP]], base=0, channel_multiplier=0).then_inc(iota_done, 1)
            nc.gpsimd.iota(pint[:], [[0, 1]], base=0, channel_multiplier=1).then_inc(iota_done, 1)

        @block.vector
        def _(dve):
            own = Links(dve, consts_done)
            own.add(nc.vector.memset(g.gate[:], 0.0))
            dve.wait_ge(iota_done, 2)
            own.add(nc.vector.tensor_copy(g.iota[:], ints[:]))
            own.link(nc.vector.tensor_copy(g.pcol[:], pint[:]))
            own.link(nc.vector.tensor_scalar(g.ident[:], g.iota[:, 0:P], g.pcol[:], None, ALU.is_equal))


XR = 4
LG = 13
DW = D + 2 * H
DG = DW // 3


def in_rings(eng, body):
    for q in range(XR):
        body(q, q, 0, True)
    with eng.Fori(1, NB // XR) as n:
        for q in range(XR):
            body(n * XR + q, q, n, False)
    for b in range(NB // XR * XR, NB):
        body(b, b % XR, b // XR, False)


def stage_nodes(nc, g, x, src, dst, W, att_src, att_dst):
    flat = g.big[:].rearrange("p b d -> p (b d)")
    used = [0]

    def piece(cols):
        used[0] += cols
        assert used[0] <= NB * D
        return flat[:, used[0] - cols:used[0]]

    with ExitStack() as ctx:
        sb = lambda n, s, d=F32: ctx.enter_context(nc.sbuf_tensor(n, s, d))
        ps = lambda n, s: ctx.enter_context(nc.psum_tensor(n, s, F32))
        raw = piece(KT * D).rearrange("p (k n) -> p k n", k=KT)
        xr = [piece(D) for _ in range(XR)]
        xn = [piece(D) for _ in range(2)]
        xo = [piece(DW) for _ in range(2)]
        prod = [piece(D) for _ in range(2)]
        att = xo
        rawf = raw.rearrange("p k n -> p (k n)")
        lines = rawf[:, 0:LG * EC].rearrange("p (b n) -> p b n", b=LG)
        below = rawf[:, 0:LG * P].rearrange("p (b n) -> p b n", b=LG)
        passed = rawf[:, 0:PATH * (NB - 1)].rearrange("p (i k) -> p i k", k=NB - 1)
        wh, wl = sb("w_high", [P, KT, DW], F32R), sb("w_low", [P, KT, DW], F32R)
        xh = [sb(f"x_high{i}", [P, D], F32R) for i in range(2)]
        xl = [sb(f"x_low{i}", [P, D], F32R) for i in range(2)]
        stats = [sb(f"ln_stats{i}", [P, 12]) for i in range(2)]
        mv = [sb(f"ln_mv{i}", [P, 2]) for i in range(2)]
        std = [sb(f"ln_std{i}", [P, 1]) for i in range(2)]
        rstd = [sb(f"ln_rstd{i}", [P, 1]) for i in range(2)]
        eps, hold = sb("ln_eps", [P, 1]), sb("ln_hold", [1, 1])
        wa = sb("wa", [P, KT, 2 * H])
        row_at, node, before = sb("row_at", [P, NB]), sb("node", [P, NB]), sb("before", [P, NB])
        row_i = sb("row_i", [P, NB], I32)
        heads, heads_b = piece(P)[0:1, :], piece(P)
        start, after = sb("start", [P, NB]), sb("after", [P, NB])
        tail = sb("tail_const", [1, 1])
        junk = piece(EC)
        ones = piece(P)
        counts, step_at = sb("counts", [P, NB - 1]), sb("step_at", [P, NB - 1])
        cnt_i = sb("cnt_i", [P, NB - 1], I32)
        blk_f, chk_f = piece(ITEMS), piece(ITEMS)
        tp = [ps(f"tp{i}", [P, 512]) for i in range(2)]
        pp = [ps(f"pp{i}", [P, 3, 512]) for i in range(2)]
        cnt_ps = pp[0][:, 0, 0:NB - 1]
        (att_in, own_dve, prod_done, prod_read, wa_done, wh_done, wl_done, stats_done, var_done, std_done,
         rstd_done, xn_done, tp_done, high_done, low_done, pp_done, xo_done, atab_done, edges_in, fills, zeroed,
         dst_done, dst_out, heads_in, heads_done, row_done, lines_read, start_done, start_out, after_in, cnt_in,
         cnt_done, cnt_read) = new_sems(
            nc, g.ctx, "att_in", "nodes_dve", "prod_done", "prod_read", "wa_done", "w_high_done", "w_low_done",
            "stats_done", "var_done", "std_done", "rstd_done", "xn_done", "tp_done", "x_high_done", "x_low_done",
            "pp_done", "xo_done", "atab_done", "edges_in", "edge_fills", "laid_zeroed", "dst_done", "dst_out",
            "heads_in", "heads_done", "row_done", "lines_read", "start_done", "start_out", "after_in", "cnt_in",
            "cnt_done", "cnt_read")
        x_in = new_sems(nc, g.ctx, *[f"x_in{q}" for q in range(XR)])
        xp_out = new_sems(nc, g.ctx, "xp_out0", "xp_out1")
        w_in = new_sems(nc, g.ctx, "w_in0", "w_in1")
        lines_in = new_sems(nc, g.ctx, "lines_in0", "lines_in1")
        line_groups = [(0, LG), (LG, NB)]
        dst_i = piece(EC + 2).bitcast(I32)
        cur = g.dst_f[:, 1:EC + 1]
        with nc.Block() as block:
            @block.sync
            def _(sp):
                def load(b, q, n, first):
                    if not first:
                        sp.wait_ge(xn_done, b - XR + 1)
                    r = LAST if isinstance(b, int) and b == NB - 1 else P
                    sp.dma_start(xr[q][0:r, :], x[bass.ds(b * P, r), :]).then_inc(x_in[q], 16)

                def store(b, i):
                    sp.wait_ge(xo_done, b + 1)
                    sp.dma_start(g.xp[bass.ds(b * P, P), :], xo[i][:, 0:D]).then_inc(xp_out[i], 16)

                def both(b, q, n, first):
                    load(b, q, n, first)
                    if not first:
                        store(b - XR, q % 2)
                load(0, 0, 0, True)
                sp.dma_start(raw[:, 0:KT // 2, :], W[0:D // 2, :].rearrange("(k p) n -> p k n", p=P)).then_inc(w_in[0], 16)
                load(1, 1, 0, True)
                sp.dma_start(raw[:, KT // 2:KT, :], W[D // 2:D, :].rearrange("(k p) n -> p k n", p=P)).then_inc(w_in[1], 16)
                sp.wait_ge(fills, 2)
                sp.dma_start(dst_i[0:1, 1:EC + 2], dst[0:EC + 1].unsqueeze(0)).then_inc(edges_in, 16)
                sp.dma_start(dst_i[1:P - 1, :], bass.AP(dst.tensor, EC - 1, [[EC, P - 2], [1, EC + 2]])).then_inc(edges_in, 16)
                sp.dma_start(dst_i[P - 1:P, 0:ELAST + 1], dst[(P - 1) * EC - 1:E].unsqueeze(0)).then_inc(edges_in, 16)
                sp.dma_start(g.src_i[0:P - 1, :], src[0:(P - 1) * EC].rearrange("(p n) -> p n", p=P - 1)).then_inc(edges_in, 16)
                sp.dma_start(g.src_i[P - 1:P, 0:ELAST], src[(P - 1) * EC:E].unsqueeze(0)).then_inc(edges_in, 16)
                for q in range(2, XR):
                    load(q, q, 0, True)
                sp.wait_ge(dst_done, 1)
                sp.dma_start(g.lines[:, :], cur).then_inc(dst_out, 16)
                sp.wait_ge(dst_out, 16)
                sp.dma_start(heads, g.lines[:, 0:1].rearrange("p a -> a p"), allow_slow_non_contiguous=True).then_inc(heads_in, 16)
                with sp.Fori(1, NB // XR) as n:
                    for q in range(XR):
                        both(n * XR + q, q, n, False)
                sp.wait_ge(start_done, 2)
                sp.dma_start(g.starts[0:NP].rearrange("(b p) -> p b", p=P), start[:], allow_slow_non_contiguous=True).then_inc(start_out, 16)
                sp.dma_start(g.starts[NP:NP + 1].unsqueeze(0), tail[:]).then_inc(start_out, 16)
                sp.wait_ge(start_out, 32)
                sp.dma_start(after[:], g.starts[1:NP + 1].rearrange("(b p) -> p b", p=P), allow_slow_non_contiguous=True).then_inc(after_in, 16)
                for b in range(NB // XR * XR, NB):
                    both(b, b % XR, b // XR, False)
                for b in range(NB - XR, NB):
                    store(b, b % 2)
                sp.wait_ge(xp_out[0], 16 * ((NB + 1) // 2))
                sp.wait_ge(xp_out[1], 16 * (NB // 2))

            @block.gpsimd
            def _(pool):
                pool.wait_ge(att_in, 32)
                for n in range(2 * KT):
                    pool.wait_ge(w_in[n // KT], 16)
                    if n >= 2:
                        pool.wait_ge(prod_read, n - 1)
                    nc.gpsimd.tensor_tensor(prod[n % 2], raw[:, n // 2, :], att[n % 2][:, 0:D], ALU.mult).then_inc(prod_done, 1)
                pool.wait_ge(heads_in, 16)
                nc.gpsimd.partition_broadcast(heads_b, heads, P).then_inc(heads_done, 1)
                pool.wait_ge(row_done, 1)
                for n, (lo, hi) in enumerate(line_groups):
                    if n:
                        pool.wait_ge(lines_read, lo)
                    for b in range(lo, hi):
                        nc.gpsimd.indirect_dma_start(lines[:, b - lo, :], None, g.lines[:, :],
                                                     bass.IndirectOffsetOnAxis(row_i[:, b:b + 1], 0)).then_inc(lines_in[n], 16)

            @block.vector
            def _(dve):
                v = nc.vector
                own = Links(dve, own_dve)
                v.memset(dst_i, NP + P).then_inc(fills, 1)
                v.memset(g.src_i[:], 0).then_inc(fills, 1)
                own.add(v.memset(eps[:], EPS))
                own.add(v.memset(ones, 1.0))
                v.memset(tail[:], float(E)).then_inc(start_done, 1)
                own.add(v.memset(xn[0], 0.0))
                own.link(v.tensor_scalar(node[:], g.iota[:, 0:NB], float(P), g.pcol[:], ALU.mult, ALU.add))

                def normalise(b, q, n, first):
                    i = q % 2
                    dve.wait_ge(x_in[q], 16 * (n + 1))
                    for j in range(2):
                        v.bn_stats(stats[i][:, j * 6:j * 6 + 6], xr[q][:, j * 512:(j + 1) * 512]).then_inc(stats_done, 1)
                    dve.wait_ge(stats_done, 2 * (b + 1))
                    if isinstance(b, int) and b == 0:
                        v.memset(hold[:], 0.0).then_inc(fills, 1)
                    else:
                        low(b - 1, 1 - i, first and q < 3)
                    v.bn_aggr(mv[i][:], stats[i][:]).then_inc(var_done, 1)
                    dve.wait_ge(std_done, b + 1)
                    v.reciprocal(rstd[i][:], std[i][:]).then_inc(rstd_done, 1)
                    dve.wait_ge(rstd_done, b + 1)
                    if not (first and q < 2):
                        dve.wait_ge(tp_done, 2 * (b - 1))
                    v.tensor_scalar(xn[i], xr[q], mv[i][:, 0:1], rstd[i][:], ALU.subtract, ALU.mult).then_inc(xn_done, 1)

                def low(b, i, first):
                    for j in range(2):
                        dve.wait_ge(high_done, 2 * b + j + 1)
                        c = slice(j * 512, (j + 1) * 512)
                        v.tensor_tensor(xl[i][:, c], tp[j][:], xh[i][:, c].bitcast(F32), ALU.subtract).then_inc(low_done, 1)

                dve.wait_ge(edges_in, 16 * 5)
                v.tensor_copy(g.dst_f[:], dst_i).then_inc(dst_done, 1)
                normalise(0, 0, 0, True)
                dve.wait_ge(dst_done, 1)
                own.add(v.tensor_tensor(g.first[:], cur, g.dst_f[:, 0:EC], ALU.not_equal))
                own.add(v.tensor_tensor(g.last[:], cur, g.dst_f[:, 2:EC + 2], ALU.not_equal))
                for k in range(KT):
                    dve.wait_ge(wh_done, k + 1)
                    v.tensor_tensor(wl[:, k, 0:D], raw[:, k, :], wh[:, k, 0:D].bitcast(F32), ALU.subtract).then_inc(wl_done, 1)
                    for m in (2 * k, 2 * k + 1):
                        dve.wait_ge(prod_done, m + 1)
                        v.tensor_reduce(wa[:, k, (m % 2) * H:(m % 2 + 1) * H],
                                        prod[m % 2].rearrange("p (h c) -> p h c", h=H), AX.X, ALU.add).then_inc(prod_read, 1)
                dve.wait_ge(prod_read, 2 * KT)
                own.link(v.tensor_copy(wh[:, :, D:DW], wa[:]))
                v.tensor_tensor(wl[:, :, D:DW], wa[:], wh[:, :, D:DW].bitcast(F32), ALU.subtract).then_inc(wa_done, 1)
                for k in range(1, NB):
                    own.link(v.tensor_scalar(junk, cur, float(k * P), None, ALU.is_lt, ALU.add, accum_out=counts[:, k - 1:k]))
                v.engine_nop().then_inc(cnt_in, 1)
                dve.wait_ge(cnt_done, 1)
                own.link(v.tensor_scalar(step_at[:], cnt_ps, float(E - 1), None, ALU.min))
                v.engine_nop().then_inc(cnt_read, 1)
                normalise(1, 1, 0, True)
                dve.wait_ge(heads_done, 1)
                dve.wait_ge(wl_done, KT)
                for lo, hi in ((0, LG), (LG, NB)):
                    k = hi - lo
                    own.link(v.tensor_tensor(below[:, 0:k, :], heads_b.unsqueeze(1).broadcast_to([P, k, P]),
                                             node[:, lo:hi].unsqueeze(2).broadcast_to([P, k, P]), ALU.is_lt))
                    own.link(v.tensor_reduce(row_at[:, lo:hi], below[:, 0:k, :], AX.X, ALU.add))
                own.link(v.tensor_scalar(row_at[:], row_at[:], -1.0, 0.0, ALU.add, ALU.max))
                v.tensor_copy(row_i[:], row_at[:]).then_inc(row_done, 1)
                for q, (lo, hi) in zip((2, 3), line_groups):
                    normalise(q, q, 0, True)
                    dve.wait_ge(lines_in[q - 2], 16 * (hi - lo))
                    for b in range(lo, hi):
                        v.tensor_scalar(junk, lines[:, b - lo, :], node[:, b:b + 1], None, ALU.is_lt, ALU.add,
                                        accum_out=before[:, b:b + 1]).then_inc(lines_read, 1)
                        dve.wait_ge(lines_read, b + 1)
                v.scalar_tensor_tensor(out=start[:], in0=row_at[:], scalar=float(EC), in1=before[:], op0=ALU.mult,
                                       op1=ALU.add).then_inc(start_done, 1)
                own.link(v.tensor_copy(cnt_i[:], step_at[:]))
                own.link(v.tensor_scalar(cnt_i[:], cnt_i[:], CH.bit_length() - 1, None, ALU.logical_shift_right))
                own.link(v.tensor_copy(counts[:], cnt_i[:]))
                own.link(v.tensor_tensor(step_at[:], counts[:], g.iota[:, 1:NB], ALU.add))
                with dve.Fori(1, NB // XR) as n:
                    for q in range(XR):
                        normalise(n * XR + q, q, n, False)
                for b in range(NB // XR * XR, NB):
                    normalise(b, b % XR, b // XR, False)
                low(NB - 1, (NB - 1) % 2, False)
                for a in range(0, ITEMS, PATH):
                    own.link(v.tensor_tensor(passed, step_at[:].unsqueeze(1).broadcast_to([P, PATH, NB - 1]),
                                             g.iota[:, a:a + PATH].unsqueeze(2).broadcast_to([P, PATH, NB - 1]), ALU.is_le))
                    own.link(v.tensor_reduce(blk_f[:, a:a + PATH], passed, AX.X, ALU.add))
                own.link(v.tensor_tensor(chk_f, g.iota[:, 0:ITEMS], blk_f, ALU.subtract))
                own.add(v.tensor_copy(g.blk_i[:], blk_f))
                own.link(v.tensor_copy(g.chk_i[:], chk_f))
                dve.wait_ge(after_in, 16)
                dve.wait_ge(start_out, 32)
                own.link(v.tensor_tensor(after[:], start[:], after[:], ALU.is_equal))
                own.link(v.scalar_tensor_tensor(out=start[:], in0=after[:], scalar=float(2 * NC * CH), in1=start[:],
                                                op0=ALU.mult, op1=ALU.add))
                own.link(v.tensor_copy(g.start_i[:], start[:]))

            @block.scalar
            def _(act):
                for i, a in enumerate((att_src, att_dst)):
                    act.dma_start(att[i][:, 0:D], a.rearrange("h c -> (h c)").unsqueeze(0).broadcast_to([P, D])).then_inc(att_in, 16)

                def deviation(b, i):
                    act.wait_ge(var_done, b + 1)
                    nc.scalar.activation(std[i][:], mv[i][:, 1:2], ACT.Sqrt, bias=eps[:]).then_inc(std_done, 1)

                def high(b, i, first):
                    if not first:
                        act.wait_ge(pp_done, b - 1)
                    for j in range(2):
                        act.wait_ge(tp_done, 2 * b + j + 1)
                        nc.scalar.copy(xh[i][:, j * 512:(j + 1) * 512], tp[j][:]).then_inc(high_done, 1)

                def out(b, i, turn):
                    act.wait_ge(pp_done, b + 1)
                    if turn is not None:
                        act.wait_ge(xp_out[i], 16 * turn)
                    nc.scalar.copy(xo[i].rearrange("p (g n) -> p g n", g=3), pp[i][:, :, 0:DG]).then_inc(xo_done, 1)
                    nc.scalar.copy(g.atab[:, bass.ds(b, 1), :].rearrange("p a n -> p (a n)"),
                                   pp[i][:, 2, DG - 2 * H:DG]).then_inc(atab_done, 1)

                def step(b, q, n, first):
                    high(b, q % 2, first and q < 2)
                    if not (isinstance(b, int) and b == NB - 1):
                        deviation(b + 1, (q + 1) % 2)
                    if not (first and q == 0):
                        turn = None if first and q < 3 else (n * 2 + (q - 1) // 2)
                        out(b - 1, (q + 1) % 2, turn)
                deviation(0, 0)
                for k in range(KT):
                    act.wait_ge(w_in[k // (KT // 2)], 16)
                    nc.scalar.copy(wh[:, k, 0:D], raw[:, k, :]).then_inc(wh_done, 1)
                in_rings(act, step)
                out(NB - 1, (NB - 1) % 2, (NB - 1) // 2)

            @block.tensor
            def _(pe):
                def transposes(b, i, first):
                    pe.wait_ge(xn_done, b + 1)
                    if not first:
                        pe.wait_ge(low_done, 2 * b)
                    for j in range(2):
                        for k in range(KT // 2):
                            c = j * 512 + k * P
                            t = nc.tensor.transpose(tp[j][:, k * P:(k + 1) * P], xn[i][:, c:c + P], g.ident[:])
                        t.then_inc(tp_done, 1)

                def project(b, i, first):
                    pe.wait_ge(low_done, 2 * (b + 1))
                    if not first:
                        pe.wait_ge(atab_done, b - 1)
                    passes = [(w, s) for w, s in ((wh, xh), (wl, xh), (wh, xl))]
                    for n in range(3):
                        if isinstance(b, int) and b == 0:
                            pe.wait_ge(wa_done if n == 2 else wl_done, 1 if n == 2 else KT)
                        for m, (w, s) in enumerate(passes):
                            for k in range(KT):
                                t = nc.tensor.matmul(pp[i][:, n, 0:DG], s[i][:, k * P:(k + 1) * P],
                                                     w[:, k, n * DG:(n + 1) * DG], start=(m == 0 and k == 0),
                                                     stop=(m == len(passes) - 1 and k == KT - 1))
                    t.then_inc(pp_done, 1)

                def step(b, q, n, first):
                    if not (isinstance(b, int) and b == NB - 1):
                        transposes(b + 1, (q + 1) % 2, False)
                    project(b, q % 2, first and q < 2)
                transposes(0, 0, True)
                pe.wait_ge(cnt_in, 1)
                nc.tensor.matmul(cnt_ps, ones, counts[:], start=True, stop=True).then_inc(cnt_done, 1)
                pe.wait_ge(cnt_read, 1)
                in_rings(pe, step)


BATCH = 4
RING = 7
PIECE = EC // RING


def stage_scores(nc, g):
    flat = g.big[:].rearrange("p b d -> p (b d)")
    used = [0]

    def piece(cols, d=F32):
        used[0] += cols
        assert used[0] <= NB * D
        return flat[:, used[0] - cols:used[0]].bitcast(d)

    with ExitStack() as ctx:
        sb = lambda n, s, d=F32: ctx.enter_context(nc.sbuf_tensor(n, s, d))
        ps = lambda n, s: ctx.enter_context(nc.psum_tensor(n, s, F32))
        low_t = sb("low_t", [PIECE * 2, 4, P], BF16)
        spread = [sb(f"spread{i}", [P, PIECE, P], BF16) for i in range(3)]
        part = [sb(f"table{i}", [P, NB, H], BF16) for i in range(3)]
        rest = sb("table_rest", [P, NB, H])
        hot = [sb(f"low_hot{i}", [P, BATCH, P], BF16) for i in range(2)]
        high = piece(EC * NB).rearrange("p (n b) -> p n b", b=NB)
        picked = [piece(BATCH * H * NB).rearrange("p (n b h) -> p n b h", b=NB, h=H) for _ in range(2)]
        zeros = piece(EC * 2 * H).rearrange("p (n r) -> p n r", r=2 * H)
        row2 = sb("fill_row2", [2 * H, 2, P])
        run, shifted = sb("fill_run", [2 * H, P]), sb("fill_shifted", [2 * H, P])
        ends = sb("fill_ends", [P, 2, 2 * H])
        carry = sb("fill_carry", [P, 2 * H])
        same, unseen = sb("same", [P, EC]), sb("unseen", [P, EC])
        pick_ps = [ps(f"pick_ps{i}", [P, BATCH, NB * H]) for i in range(2)]
        lps = ps("low_ps", [PIECE * 2, 4, P])
        tps = ps("fill_rows", [2 * H, 2, P])
        cps = ps("fill_cols", [P, 2 * H])
        part_i = sb("address_part", [P, EC], I32)
        src_lo, src_hi = sb("src_lo", [P, EC]), sb("src_hi", [P, EC])
        (own_dve, src_lo_done, lt_done, lt_copied, low_out, zero_done, zero_out, laid, laid_in, table_done, hot_done, pick_done,
         picked_done, edge_s_done, ends_in, ends_done, run_in, carry_done) = new_sems(
            nc, g.ctx, "scores_dve", "src_lo_done", "low_t_done", "low_t_copied", "low_out", "zero_done", "zero_out", "laid", "laid_in",
            "table_done", "low_hot_done", "pick_done", "picked_done", "edge_s_done", "ends_in", "ends_done", "run_in",
            "carry_done")
        spread_in = new_sems(nc, g.ctx, *[f"spread_in{i}" for i in range(3)])
        QC = EC // 4
        STEPS = PIECE // BATCH
        assert QC <= 2 * PIECE
        assert PIECE % BATCH == 0 and STEPS % 2 == 0
        with nc.Block() as block:
            @block.sync
            def _(sp):
                sp.wait_ge(zero_done, 1)
                sp.dma_start(g.laid.rearrange("(p n) r -> p n r", p=P), zeros).then_inc(zero_out, 16)
                sp.wait_ge(lt_copied, 1)
                sp.dma_start(g.low.rearrange("(t c) p -> c t p", t=4), low_t[0:QC, :, :]).then_inc(low_out, 16)
                sp.wait_ge(low_out, 16)
                for r in range(RING):
                    if r >= 3:
                        sp.wait_ge(hot_done, (r - 2) * STEPS)
                    if r == 5:
                        sp.wait_ge(laid, 16 * NB)
                        sp.dma_start(g.edge_d[:], g.laid.rearrange("(p n) r -> p n r", p=P)).then_inc(laid_in, 16)
                    sp.dma_start(spread[r % 3][:].rearrange("p n e -> p (n e)"),
                                 g.low[r * PIECE:(r + 1) * PIECE, :].rearrange("c p -> (c p)").unsqueeze(0)
                                 .broadcast_to([P, PIECE * P])).then_inc(spread_in[r % 3], 16)

            @block.gpsimd
            def _(pool):
                pool.wait_ge(zero_out, 16)
                for b in range(NB):
                    nc.gpsimd.indirect_dma_start(
                        g.laid[:, :], bass.IndirectOffsetOnAxis(g.start_i[:, b:b + 1], 0), g.atab[:, b, :], None,
                        bounds_check=NC * CH - 1, oob_is_err=False).then_inc(laid, 16)

            @block.vector
            def _(dve):
                v = nc.vector
                own = Links(dve, own_dve)
                v.memset(zeros, 0.0).then_inc(zero_done, 1)
                own.link(v.tensor_scalar(part_i[:], g.src_i[:], P - 1, None, ALU.bitwise_and))
                v.tensor_copy(src_lo[:], part_i[:]).then_inc(src_lo_done, 1)
                dve.wait_ge(src_lo_done, 1)
                own.link(v.tensor_scalar(part_i[:], g.src_i[:], P.bit_length() - 1, None, ALU.logical_shift_right))
                own.link(v.tensor_copy(src_hi[:], part_i[:]))
                dve.wait_ge(lt_done, 1)
                v.tensor_copy(low_t[0:QC, :, :], lps[0:QC, :, :]).then_inc(lt_copied, 1)
                own.link(v.tensor_copy(part[0][:], g.atab[:, :, 0:H]))
                own.link(v.tensor_tensor(rest[:], g.atab[:, :, 0:H], part[0][:], ALU.subtract))
                own.link(v.tensor_copy(part[1][:], rest[:]))
                own.link(v.tensor_tensor(rest[:], rest[:], part[1][:], ALU.subtract))
                v.tensor_copy(part[2][:], rest[:]).then_inc(table_done, 1)
                own.link(v.tensor_tensor(high, src_hi[:].unsqueeze(2).broadcast_to([P, EC, NB]),
                                         g.iota[:, 0:NB].unsqueeze(1).broadcast_to([P, EC, NB]), ALU.is_equal))

                def low_hot(s, i, ring, at, first):
                    if not first:
                        dve.wait_ge(pick_done, s - 1)
                    v.tensor_scalar(hot[i][:], spread[ring][:, bass.ds(at, BATCH), :], g.pcol[:], None,
                                    ALU.is_equal).then_inc(hot_done, 1)

                def pick(s, i, first=False):
                    dve.wait_ge(pick_done, s + 1)
                    if not first:
                        dve.wait_ge(edge_s_done, s - 1)
                    v.tensor_tensor(picked[i], pick_ps[i][:].rearrange("p n (b h) -> p n b h", h=H),
                                    high[:, bass.ds(s * BATCH, BATCH), :].unsqueeze(3).broadcast_to([P, BATCH, NB, H]),
                                    ALU.mult).then_inc(picked_done, 1)

                def total(s, i):
                    dve.wait_ge(picked_done, s + 1)
                    v.tensor_reduce(g.edge_s[:, bass.ds(s * BATCH, BATCH), :],
                                    picked[i].rearrange("p n b h -> p n h b"), AX.X, ALU.add).then_inc(edge_s_done, 1)

                for r in range(RING):
                    dve.wait_ge(spread_in[r % 3], 16 * (r // 3 + 1))
                    base = r * STEPS

                    def batch(s, i, at, late):
                        low_hot(s, i, r % 3, at, late < 2)
                        if late >= 1:
                            pick(s - 1, 1 - i, late < 3)
                        if late >= 2:
                            total(s - 2, i)
                    peeled = 4 if r == 0 else 0
                    for n in range(peeled):
                        batch(n, n % 2, n * BATCH, n)
                    with dve.Fori(peeled // 2, STEPS // 2) as n:
                        for i in range(2):
                            batch(n * 2 + (base + i), i, n * (2 * BATCH) + i * BATCH, 4)
                S = RING * STEPS
                pick(S - 1, 1)
                total(S - 2, 0)
                total(S - 1, 1)
                dve.wait_ge(laid_in, 16)
                own.link(v.tensor_scalar(same[:], g.first[:], -1.0, 1.0, ALU.mult, ALU.add))
                own.add(v.tensor_tensor_scan(unseen[:], same[:], same[:], 1.0, ALU.mult, ALU.min))
                for r in range(2 * H):
                    own.add(v.tensor_tensor_scan(g.edge_d[:, :, r], same[:], g.edge_d[:, :, r], 0.0, ALU.mult, ALU.add))
                own.wait()
                own.add(v.tensor_copy(ends[:, 0, :], g.edge_d[:, EC - 1, :]))
                own.link(v.tensor_copy(ends[:, 1, :], unseen[:, EC - 1:EC].broadcast_to([P, 2 * H])))
                v.engine_nop().then_inc(ends_in, 1)
                dve.wait_ge(ends_done, 1)
                own.link(v.tensor_copy(row2[:], tps[:]))
                own.add(v.memset(shifted[:], 0.0))
                own.link(v.tensor_tensor_scan(run[:], row2[:, 1, :], row2[:, 0, :], 0.0, ALU.mult, ALU.add))
                own.link(v.tensor_copy(shifted[:, 1:P], run[:, 0:P - 1]))
                v.engine_nop().then_inc(run_in, 1)
                dve.wait_ge(carry_done, 1)
                own.link(v.tensor_copy(carry[:], cps[:]))
                for r in range(2 * H):
                    own.add(v.scalar_tensor_tensor(out=g.edge_d[:, :, r], in0=unseen[:], scalar=carry[:, r:r + 1],
                                                   in1=g.edge_d[:, :, r], op0=ALU.mult, op1=ALU.add))
                own.wait()

            @block.tensor
            def _(pe):
                pe.wait_ge(src_lo_done, 1)
                for t in range(4):
                    m = nc.tensor.transpose(lps[0:QC, t, :], src_lo[:, t * QC:(t + 1) * QC], g.ident[:])
                m.then_inc(lt_done, 1)
                pe.wait_ge(table_done, 1)

                def pick(s, i, first):
                    pe.wait_ge(hot_done, s + 1)
                    if not first:
                        pe.wait_ge(picked_done, s - 1)
                    for c in range(BATCH):
                        for k in range(3):
                            m = nc.tensor.matmul(pick_ps[i][:, c, :], hot[i][:, c, :],
                                                 part[k][:].rearrange("p b h -> p (b h)"), start=(k == 0), stop=(k == 2))
                    m.then_inc(pick_done, 1)
                for i in range(2):
                    pick(i, i, True)
                with pe.Fori(1, RING * STEPS // 2) as n:
                    for i in range(2):
                        pick(n * 2 + i, i, False)
                pe.wait_ge(ends_in, 1)
                nc.tensor.transpose(tps[:, 0, :], ends[:, 0, :], g.ident[:])
                nc.tensor.transpose(tps[:, 1, :], ends[:, 1, :], g.ident[:]).then_inc(ends_done, 1)
                pe.wait_ge(run_in, 1)
                nc.tensor.transpose(cps[:], shifted[:], g.ident[0:2 * H, 0:2 * H]).then_inc(carry_done, 1)


def stage_weights(nc, g):
    with ExitStack() as ctx:
        sb = lambda n, s, d=F32: ctx.enter_context(nc.sbuf_tensor(n, s, d))
        ps = lambda n, s: ctx.enter_context(nc.psum_tensor(n, s, F32))
        rec = sb("rec_all", [P, EC, REC])
        first, last = g.first, g.last
        nf, nl, seen_f, seen_l = (sb(n, [P, EC]) for n in ("nf", "nl", "seen_f", "seen_l"))
        fmax, bmax = sb("fmax", [P, EC, H]), sb("bmax", [P, EC, H])
        ew, mw, sw = sb("ew", [P, EC, H]), sb("mw", [P, EC, H]), sb("sw", [P, EC, H])
        tail4 = sb("tail4", [P, 2, H])
        rowt = sb("rowt", [H, 2, P])
        run = sb("run", [H, P])
        shifted = sb("shifted", [H, P])
        carry = sb("carry", [P, 2, H])
        tps = [ps(f"row_ps{i}", [P, 2, P]) for i in range(2)]
        cps = [ps(f"col_ps{i}", [P, H]) for i in range(2)]
        own_dve, t_in, t_done, r_in, c_done, e_in, e_done, rec_done, rec_out, zeroed = new_sems(
            nc, g.ctx, "weights_dve", "tails_in", "tails_done", "runs_in", "carried_back",
            "exps_in", "exps_done", "rec_done", "rec_out", "acc_zeroed")
        a_s, d_s, d_d = g.edge_s[:], g.edge_d[:, :, 0:H], g.edge_d[:, :, H:2 * H]
        with nc.Block() as block:
            @block.vector
            def _(dve):
                own = Links(dve, own_dve)
                v = nc.vector
                cur = g.dst_f[:, 1:EC + 1]
                own.add(v.tensor_scalar(nf[:], first[:], NEG, None, ALU.mult))
                own.add(v.tensor_scalar(nl[:], last[:], NEG, None, ALU.mult))
                own.add(v.tensor_tensor_scan(seen_f[:], first[:], first[:], 0.0, ALU.max, ALU.max))
                own.add(v.tensor_tensor_scan(seen_l[:, ::-1], last[:, ::-1], last[:, ::-1], 0.0, ALU.max, ALU.max))
                own.wait()
                own.add(v.tensor_scalar(seen_f[:], seen_f[:], NEG, None, ALU.mult))
                own.add(v.tensor_scalar(seen_l[:], seen_l[:], NEG, None, ALU.mult))
                own.wait()

                def carried(n, out, inp, seg, seen, tail, back):
                    rev = slice(None, None, -1) if back else slice(None)
                    for h in range(H):
                        own.add(v.tensor_tensor_scan(out[:, rev, h], seg[:, rev], inp[:, rev, h], NEG, ALU.add, ALU.max))
                    own.wait()
                    own.add(v.tensor_copy(tail4[:, 0, :], out[:, tail, :]))
                    own.link(v.tensor_copy(tail4[:, 1, :], seen[:, tail:tail + 1].broadcast_to([P, H])))
                    v.engine_nop().then_inc(t_in, 1)
                    dve.wait_ge(t_done, n + 1)
                    own.link(v.tensor_copy(rowt[:], tps[n][0:H, :, :]))
                    own.add(v.memset(shifted[:], NEG))
                    own.link(v.tensor_tensor_scan(run[:, rev], rowt[:, 1, rev], rowt[:, 0, rev], NEG, ALU.add, ALU.max))
                    if back:
                        own.link(v.tensor_copy(shifted[:, 0:P - 1], run[:, 1:P]))
                    else:
                        own.link(v.tensor_copy(shifted[:, 1:P], run[:, 0:P - 1]))
                    v.engine_nop().then_inc(r_in, 1)
                    dve.wait_ge(c_done, n + 1)
                    own.link(v.tensor_copy(carry[:, n, :], cps[n][:]))
                    for h in range(H):
                        own.add(v.scalar_tensor_tensor(out=out[:, :, h], in0=seen[:], scalar=carry[:, n, h:h + 1],
                                                       in1=out[:, :, h], op0=ALU.add, op1=ALU.max))
                    own.wait()

                carried(0, fmax, a_s, nf, seen_f, EC - 1, False)
                carried(1, bmax, fmax, nl, seen_l, 0, True)
                own.add(v.tensor_tensor(mw[:], bmax[:], d_s, ALU.max))
                own.add(v.tensor_tensor(ew[:], a_s, d_d, ALU.add))
                own.add(v.tensor_tensor(sw[:], d_s, d_d, ALU.add))
                own.wait()
                own.link(v.tensor_tensor(mw[:], mw[:], d_d, ALU.add))
                for t in (mw, ew, sw):
                    own.add(v.scalar_tensor_tensor(out=t[:], in0=t[:], scalar=SLOPE, in1=t[:], op0=ALU.mult, op1=ALU.max))
                own.wait()
                own.add(v.tensor_tensor(ew[:], ew[:], mw[:], ALU.subtract))
                own.link(v.tensor_tensor(sw[:], sw[:], mw[:], ALU.subtract))
                v.engine_nop().then_inc(e_in, 1)
                own.add(v.tensor_copy(rec[:, :, FIRST_AT:FIRST_AT + 1], first[:].unsqueeze(2)))
                own.add(v.tensor_copy(rec[:, :, DST_AT:DST_AT + 1], cur.unsqueeze(2)))
                own.add(v.memset(rec[:, :, DST_AT + 1:DST_AT + 2], 0.0))
                own.add(v.tensor_copy(rec[:, :, SRC_AT:SRC_AT + 1].bitcast(I32), g.src_i[:].unsqueeze(2)))
                dve.wait_ge(e_done, 2)
                own.link(v.tensor_tensor(rec[:, :, SELF_AT:SELF_AT + H], sw[:], first[:].unsqueeze(2).broadcast_to([P, EC, H]), ALU.mult))
                v.engine_nop().then_inc(rec_done, 1)
                v.memset(g.acc_side[:], 0.0).then_inc(zeroed, 1)
                v.memset(g.big[:], 0.0).then_inc(zeroed, 1)
                dve.wait_ge(zeroed, 2)

            @block.scalar
            def _(act):
                act.wait_ge(e_in, 1)
                nc.scalar.activation(rec[:, :, W_AT:W_AT + H], ew[:], ACT.Exp).then_inc(e_done, 1)
                nc.scalar.activation(sw[:], sw[:], ACT.Exp).then_inc(e_done, 1)

            @block.tensor
            def _(pe):
                for n in range(2):
                    pe.wait_ge(t_in, n + 1)
                    nc.tensor.transpose(tps[n][0:H, 0, :], tail4[:, 0, :], g.ident[:])
                    nc.tensor.transpose(tps[n][0:H, 1, :], tail4[:, 1, :], g.ident[:]).then_inc(t_done, 1)
                    pe.wait_ge(r_in, n + 1)
                    nc.tensor.transpose(cps[n][:], shifted[:], g.ident[0:H, 0:H]).then_inc(c_done, 1)

            @block.sync
            def _(sp):
                sp.wait_ge(rec_done, 1)
                sp.wait_ge(e_done, 2)
                sp.dma_start(g.rec.rearrange("(p n) r -> p n r", p=P), rec[:]).then_inc(rec_out, 16)
                sp.wait_ge(rec_out, 16)


GB = 4


HB = 4
LAG = 2


def stage_messages(nc, g):
    with ExitStack() as ctx:
        sb = lambda n, s, d=F32: ctx.enter_context(nc.sbuf_tensor(n, s, d))
        ps = lambda n, s: ctx.enter_context(nc.psum_tensor(n, s, F32))
        rec = [sb(f"rec{q}", [P, SUB, REC]) for q in range(GB)]
        got = [sb(f"rows{q}", [P, SUB, D]) for q in range(GB)]
        one = [sb(f"one{i}", [P, SUB, P]) for i in range(HB)]
        hot = [sb(f"hot{i}", [P, SUB, H, P]) for i in range(HB)]
        msg = [ps(f"msg{i}", [P, D]) for i in range(2)]
        side = [ps(f"side{i}", [P, FIRST_AT + 1]) for i in range(2)]
        rec_in = new_sems(nc, g.ctx, *[f"rec_in{q}" for q in range(GB)])
        got_in = new_sems(nc, g.ctx, *[f"rows_in{q}" for q in range(GB)])
        one_done, hot_done, sums_done, added, gated = new_sems(
            nc, g.ctx, "one_done", "hot_done", "sums_done", "added", "messages_gated")
        assert ITEMS % GB == 0 and GB % HB == 0
        turns = ITEMS // GB

        def each(eng, body):
            for q in range(GB):
                body(q, 0, q, True)
            with eng.Fori(1, turns) as t:
                for q in range(GB):
                    body(t * GB + q, t, q, False)

        with nc.Block() as block:
            @block.sync
            def _(sp):
                def load(i, t, q, first):
                    c = sp.value_load(g.chk_i[0:1, bass.ds(i, 1)], min_val=0, max_val=NC - 1)
                    if not first:
                        sp.wait_ge(sums_done, i - GB + 1)
                    sp.dma_start(rec[q][:], g.rec[bass.ds(c * CH, CH), :].rearrange("(p k) r -> p k r", k=SUB)).then_inc(rec_in[q], 16)
                each(sp, load)

            @block.gpsimd
            def _(pool):
                nc.gpsimd.memset(g.gate[0:1, 1:2], 0.0).then_inc(gated, 1)

                def gather(i, t, q, first):
                    if not first:
                        pool.wait_ge(sums_done, i - GB + 1)
                    pool.wait_ge(rec_in[q], 16 * (t + 1))
                    gate(nc, g, gated, i)
                    for k in range(SUB):
                        nc.gpsimd.indirect_dma_start(
                            got[q][:, k, :], None, g.xp[:, :],
                            bass.IndirectOffsetOnAxis(rec[q][:, k, SRC_AT:SRC_AT + 1].bitcast(I32), 0)).then_inc(got_in[q], 16)
                each(pool, gather)

            @block.scalar
            def _(act):
                def weights(i, t, q, first):
                    if not (first and q < HB):
                        act.wait_ge(sums_done, i - HB + 1)
                    for k in range(SUB):
                        act.wait_ge(one_done, SUB * i + k + 1)
                        for h in range(H):
                            ins = nc.scalar.activation(hot[q % HB][:, k, h, :], one[q % HB][:, k, :], ACT.Copy,
                                                       scale=rec[q][:, k, h:h + 1])
                    ins.then_inc(hot_done, 1)
                each(act, weights)

            @block.vector
            def _(dve):
                def weigh(i, t, q, first):
                    b = dve.value_load(g.blk_i[0:1, bass.ds(i, 1)], min_val=0, max_val=NB - 1)
                    nodes = g.iota[:, bass.ds(b * P, P)]
                    dve.wait_ge(rec_in[q], 16 * (t + 1))
                    if not (first and q < HB):
                        dve.wait_ge(sums_done, i - HB + 1)
                    for k in range(SUB):
                        nc.vector.tensor_scalar(one[q % HB][:, k, :], nodes, rec[q][:, k, DST_AT:DST_AT + 1], None,
                                                ALU.is_equal).then_inc(one_done, 1)

                def add(i, q, first):
                    b = dve.value_load(g.blk_i[0:1, bass.ds(i, 1)], min_val=0, max_val=NB - 1)
                    dve.wait_ge(sums_done, i + 1)
                    if not first:
                        dve.wait_ge(added, 2 * i)
                    at = g.big[:, bass.ds(b, 1), :].rearrange("p a n -> p (a n)")
                    nc.vector.tensor_tensor(at, at, msg[q % 2][:], ALU.add).then_inc(added, 1)
                    at = g.acc_side[:, bass.ds(b, 1), :].rearrange("p a n -> p (a n)")
                    nc.vector.tensor_tensor(at, at, side[q % 2][:], ALU.add).then_inc(added, 1)

                def step(i, t, q, first):
                    weigh(i, t, q, first)
                    if not (first and q < LAG):
                        add(i - LAG, (q - LAG) % GB, first and q == LAG)
                each(dve, step)
                for q in range(GB - LAG, GB):
                    add(ITEMS - GB + q, q, False)

            @block.tensor
            def _(pe):
                def sums(i, t, q, first):
                    pe.wait_ge(hot_done, i + 1)
                    pe.wait_ge(got_in[q], 16 * SUB * (t + 1))
                    if not (first and q < 2):
                        pe.wait_ge(added, 2 * (i - 1))
                    for h in range(H):
                        for k in range(SUB):
                            nc.tensor.matmul(msg[q % 2][:, h * C:(h + 1) * C], hot[q % HB][:, k, h, :],
                                             got[q][:, k, h * C:(h + 1) * C], start=(k == 0), stop=(k == SUB - 1))
                    for k in range(SUB):
                        t_ = nc.tensor.matmul(side[q % 2][:], one[q % HB][:, k, :], rec[q][:, k, 0:FIRST_AT + 1],
                                              start=(k == 0), stop=(k == SUB - 1))
                    t_.then_inc(sums_done, 1)
                each(pe, sums)


def stage_residual(nc, g, x, bias, gate_w, out):
    with ExitStack() as ctx:
        sb = lambda n, s, d=F32: ctx.enter_context(nc.sbuf_tensor(n, s, d))
        ps = lambda n, s: ctx.enter_context(nc.psum_tensor(n, s, F32))
        pair = lambda n, s: [sb(f"{n}{i}", s) for i in range(2)]
        xb, xpb, x1, xn, xt = (pair(n, [P, D]) for n in ("r_x", "r_xp", "r_x1", "r_xn", "r_xt"))
        t = sb("r_t", [P, D])
        bias_b = sb("bias_b", [P, D])
        gw = sb("gate_rows", [X, D])
        gwt = sb("gate_t", [P, KT, X])
        wself, rz = sb("wself", [P, NB, H]), sb("rz", [P, NB, H])
        stats, mv, std, rstd = pair("r_stats", [P, 12]), pair("r_mv", [P, 2]), pair("r_std", [P, 1]), pair("r_rstd", [P, 1])
        eps = sb("r_eps", [P, 1])
        top, tot = sb("r_top", [P, NB]), sb("r_tot", [P, NB])
        tp = [ps(f"r_tp{i}", [P, D]) for i in range(2)]
        sp_ = [ps(f"r_sc{i}", [P, X]) for i in range(2)]
        gp = ps("gate_ps", [P, KT, X])
        (cons_in, own_dve, gp_done, gwt_done, x1_done, var_done, std_done, xn_done, tp_done, xt_done, sc_done,
         sc_copied, soft_in, soft_done, r_chain) = new_sems(
            nc, g.ctx, "r_consts_in", "residual_dve", "gate_ps_done", "gate_t_done", "x1_done", "r_var_done", "r_std_done",
            "r_xn_done", "r_tp_done", "r_xt_done", "r_sc_done", "r_sc_copied", "soft_in", "soft_done", "r_chain")
        loaded = new_sems(nc, g.ctx, "r_in0", "r_in1")
        stored = new_sems(nc, g.ctx, "r_out0", "r_out1")

        def each(eng, body):
            for i in range(2):
                body(i, i, 0, True)
            with eng.Fori(1, NB // 2) as n:
                for i in range(2):
                    body(n * 2 + i, i, n, False)
            body(NB - 1, 0, NB // 2, False)

        def last(b):
            return isinstance(b, int) and b == NB - 1

        with nc.Block() as block:
            @block.sync
            def _(sp):
                sp.dma_start(gw[:], gate_w).then_inc(cons_in, 16)
                sp.dma_start(bias_b[:], bias.unsqueeze(0).broadcast_to([P, D])).then_inc(cons_in, 16)

                def load(b, i, n, first):
                    if not first:
                        sp.wait_ge(x1_done, b - 1)
                    r = LAST if last(b) else P
                    sp.dma_start(xb[i][0:r, :], x[bass.ds(b * P, r), :]).then_inc(loaded[i], 16)
                    sp.dma_start(xpb[i][:], g.xp[bass.ds(b * P, P), :]).then_inc(loaded[i], 16)

                def store(b, i, n, first):
                    r = LAST if last(b) else P
                    sp.wait_ge(xn_done, b + 1)
                    sp.dma_start(out[bass.ds(b * P, r), :], x1[i][0:r, :]).then_inc(stored[i], 16)
                    sp.dma_start(g.xn1[bass.ds(b * P, r), :], xn[i][0:r, :]).then_inc(stored[i], 16)

                def both(b, i, n, first):
                    load(b, i, n, first)
                    if not (first and i == 0):
                        store(b - 1, 1 - i, n, first)
                each(sp, both)
                store(NB - 1, 0, NB // 2, False)
                sp.wait_ge(stored[0], 32 * ((NB + 1) // 2))
                sp.wait_ge(stored[1], 32 * (NB // 2))

            @block.vector
            def _(dve):
                v = nc.vector
                own = Links(dve, own_dve)
                own.add(v.memset(eps[:], EPS))
                have = g.acc_side[:, :, FIRST_AT:FIRST_AT + 1].broadcast_to([P, NB, H])
                own.link(v.tensor_tensor(wself[:], g.acc_side[:, :, SELF_AT:SELF_AT + H], have, ALU.subtract))
                own.link(v.tensor_scalar(wself[:], wself[:], 1.0, None, ALU.add))
                own.link(v.tensor_tensor(rz[:], g.acc_side[:, :, 0:H], wself[:], ALU.add))
                own.link(v.reciprocal(rz[:], rz[:]))
                dve.wait_ge(gp_done, 1)
                v.tensor_copy(gwt[:], gp[:]).then_inc(gwt_done, 1)
                dve.wait_ge(cons_in, 32)

                def residual(b, i, n, first):
                    base = b * 5
                    dve.wait_ge(loaded[i], 32 * (n + 1))
                    acc = g.big[:, bass.ds(b, 1), :].rearrange("p a n -> p (a n)")
                    own_w = wself[:, bass.ds(b, 1), :].rearrange("p a n -> p (a n)")
                    inv = rz[:, bass.ds(b, 1), :].rearrange("p a n -> p (a n)")
                    for h in range(H):
                        c = slice(h * C, (h + 1) * C)
                        ins = v.scalar_tensor_tensor(out=xpb[i][:, c], in0=xpb[i][:, c], scalar=own_w[:, h:h + 1],
                                                     in1=acc[:, c], op0=ALU.mult, op1=ALU.add)
                    ins.then_inc(r_chain, 1)
                    dve.wait_ge(r_chain, base + 1)
                    for h in range(H):
                        c = slice(h * C, (h + 1) * C)
                        ins = v.scalar_tensor_tensor(out=t[:, c], in0=xpb[i][:, c], scalar=inv[:, h:h + 1],
                                                     in1=bias_b[:, c], op0=ALU.mult, op1=ALU.add)
                    ins.then_inc(r_chain, 1)
                    dve.wait_ge(r_chain, base + 2)
                    if not first:
                        dve.wait_ge(stored[i], 32 * n)
                        dve.wait_ge(tp_done, b - 1)
                    v.scalar_tensor_tensor(out=x1[i][:], in0=t[:], scalar=0.0, in1=xb[i][:], op0=ALU.max,
                                           op1=ALU.add).then_inc(x1_done, 1)
                    dve.wait_ge(x1_done, b + 1)
                    v.bn_stats(stats[i][:, 0:6], x1[i][:, 0:512]).then_inc(r_chain, 1)
                    v.bn_stats(stats[i][:, 6:12], x1[i][:, 512:1024]).then_inc(r_chain, 1)
                    dve.wait_ge(r_chain, base + 4)
                    if not (first and i == 0):
                        copy_scores(b - 1, 1 - i)
                    v.bn_aggr(mv[i][:], stats[i][:]).then_inc(var_done, 1)
                    dve.wait_ge(var_done, b + 1)
                    dve.wait_ge(std_done, b + 1)
                    v.reciprocal(rstd[i][:], std[i][:]).then_inc(r_chain, 1)
                    dve.wait_ge(r_chain, base + 5)
                    v.tensor_scalar(xn[i][:], x1[i][:], mv[i][:, 0:1], rstd[i][:], ALU.subtract, ALU.mult).then_inc(xn_done, 1)

                def copy_scores(b, i):
                    dve.wait_ge(sc_done, b + 1)
                    v.tensor_copy(g.prob[:, bass.ds(b, 1), :].rearrange("p a n -> p (a n)"), sp_[i][:]).then_inc(sc_copied, 1)

                each(dve, residual)
                copy_scores(NB - 1, 0)
                dve.wait_ge(sc_copied, NB)
                wide = lambda a: a[:].unsqueeze(2).broadcast_to([P, NB, X])
                own.link(v.tensor_reduce(top[:], g.prob[:], AX.X, ALU.max))
                own.link(v.tensor_tensor(g.prob[:], g.prob[:], wide(top), ALU.subtract))
                v.tensor_copy(top[:], top[:]).then_inc(soft_in, 1)
                dve.wait_ge(soft_done, 1)
                own.link(v.tensor_reduce(tot[:], g.prob[:], AX.X, ALU.add))
                own.link(v.reciprocal(tot[:], tot[:]))
                own.link(v.tensor_tensor(g.prob[:], g.prob[:], wide(tot), ALU.mult))

            @block.scalar
            def _(act):
                def step(b, i, n, first):
                    act.wait_ge(var_done, b + 1)
                    nc.scalar.activation(std[i][:], mv[i][:, 1:2], ACT.Sqrt, bias=eps[:]).then_inc(std_done, 1)
                    act.wait_ge(tp_done, b + 1)
                    if not first:
                        act.wait_ge(sc_done, b - 1)
                    nc.scalar.copy(xt[i][:], tp[i][:]).then_inc(xt_done, 1)
                each(act, step)
                act.wait_ge(soft_in, 1)
                nc.scalar.activation(g.prob[:], g.prob[:], ACT.Exp).then_inc(soft_done, 1)

            @block.tensor
            def _(pe):
                pe.wait_ge(cons_in, 32)
                for k in range(KT):
                    m = nc.tensor.transpose(gp[:, k, :], gw[:, k * P:(k + 1) * P], g.ident[0:X, 0:X])
                m.then_inc(gp_done, 1)
                pe.wait_ge(gwt_done, 1)

                def step(b, i, n, first):
                    pe.wait_ge(xn_done, b + 1)
                    if not first:
                        pe.wait_ge(xt_done, b - 1)
                    for k in range(KT):
                        m = nc.tensor.transpose(tp[i][:, k * P:(k + 1) * P], xn[i][:, k * P:(k + 1) * P], g.ident[:])
                    m.then_inc(tp_done, 1)
                    pe.wait_ge(xt_done, b + 1)
                    if not first:
                        pe.wait_ge(sc_copied, b - 1)
                    for k in range(KT):
                        m = nc.tensor.matmul(sp_[i][:], xt[i][:, k * P:(k + 1) * P], gwt[:, k, :],
                                             start=(k == 0), stop=(k == KT - 1))
                    m.then_inc(sc_done, 1)
                each(pe, step)


SHIFTS = list(range(28, -1, -4))


def stage_select(nc, g):
    with ExitStack() as ctx:
        sb = lambda n, s, d=F32: ctx.enter_context(nc.sbuf_tensor(n, s, d))
        ps = lambda n, s: ctx.enter_context(nc.psum_tensor(n, s, F32))
        tid, valid = sb("tid", [P, NB]), sb("valid", [P, NB])
        rep = sb("rep", [P, NB, X, REP])
        prow, over, tie, rank = (sb(n, [P, NP]) for n in ("prow", "over", "tie", "rank"))
        pi, ji, pf = sb("sel_pi", [P, 1], I32), sb("sel_ji", [P, 1], I32), sb("sel_pf", [P, 1])
        steps = sb("sel_steps", [P, len(SHIFTS)], I32)
        gi, gf, same = sb("sel_gi", [P, P], I32), sb("sel_gf", [P, P]), sb("sel_same", [P, P])
        found, trial, dig = (sb(n, [P, 1], I32) for n in ("sel_found", "sel_trial", "sel_dig"))
        cnt, enough, digf = (sb(n, [P, 1]) for n in ("sel_cnt", "sel_enough", "sel_digf"))
        slot, slot_i = sb("slot", [P, NB, X]), sb("slot_i", [P, NB, X], I32)
        lo_i, hi_i = sb("lo_i", [P, NB, X], I32), sb("hi_i", [P, NB, X], I32)
        lo, hi = sb("lo", [P, NB, X]), sb("hi", [P, NB, X])
        mask = sb("mask", [P, NB, X, ST])
        val = sb("val", [P, NB * X, 2, ST])
        lo_hot = [sb(f"lo_hot{i}", [P, NB, P]) for i in range(2)]
        tp = [ps(f"sel_tp{i}", [P, 512]) for i in range(2)]
        vp = ps("sel_votes", [P, 1])
        lp = [ps(f"sel_list{i}", [P, 2 * ST]) for i in range(2)]
        own_dve, rep_done, tp_done, tp_copied, votes_in, votes_done, slot_done, hot_done, list_done, list_copied = new_sems(
            nc, g.ctx, "select_dve", "rep_done", "sel_tp_done", "sel_tp_copied", "votes_in", "votes_done", "slots_done",
            "lo_hot_done", "list_done", "list_copied")
        groups = [(n, min(4, NB - n)) for n in range(0, NB, 4)]
        with nc.Block() as block:
            @block.vector
            def _(dve):
                v = nc.vector
                own = Links(dve, own_dve)
                own.link(v.tensor_scalar(tid[:], g.iota[:, 0:NB], float(P), g.pcol[:], ALU.mult, ALU.add))
                own.link(v.tensor_scalar(valid[:], tid[:], float(N), None, ALU.is_lt))
                wide = lambda a: a[:].unsqueeze(2).broadcast_to([P, NB, X])
                own.link(v.tensor_tensor(g.prob[:], g.prob[:], wide(valid), ALU.mult))
                own.link(v.tensor_scalar(valid[:], valid[:], -1.0, None, ALU.add))
                own.link(v.tensor_tensor(g.prob[:], g.prob[:], wide(valid), ALU.add))
                own.link(v.tensor_copy(rep[:], g.prob[:].unsqueeze(3).broadcast_to([P, NB, X, REP])))
                v.engine_nop().then_inc(rep_done, 1)
                own.link(v.tensor_copy(pi[:], g.pcol[:]))
                own.link(v.tensor_scalar(ji[:], pi[:], REP - 1, None, ALU.bitwise_and))
                for n, s in enumerate(SHIFTS):
                    if n == 0:
                        own.link(v.tensor_scalar(steps[:, 0:1], ji[:], 3, s, ALU.bitwise_and, ALU.logical_shift_left))
                    else:
                        own.link(v.tensor_scalar(steps[:, n:n + 1], ji[:], s, None, ALU.logical_shift_left))
                own.link(v.tensor_scalar(pi[:], pi[:], REP.bit_length() - 1, None, ALU.logical_shift_right))
                own.link(v.tensor_copy(pf[:], pi[:]))
                own.link(v.tensor_copy(gi[:], g.iota[:, 0:P]))
                own.link(v.tensor_scalar(gi[:], gi[:], REP.bit_length() - 1, None, ALU.logical_shift_right))
                own.link(v.tensor_copy(gf[:], gi[:]))
                own.link(v.tensor_scalar(same[:], gf[:], pf[:], None, ALU.is_equal))
                own.link(v.memset(found[:], 0))

                for n, (b, k) in enumerate(groups):
                    dve.wait_ge(tp_done, n + 1)
                    v.tensor_copy(prow[:, b * P:(b + k) * P], tp[n % 2][:, 0:k * P]).then_inc(tp_copied, 1)
                dve.wait_ge(tp_copied, len(groups))

                for n, s in enumerate(SHIFTS):
                    own.link(v.tensor_tensor(trial[:], found[:], steps[:, n:n + 1], ALU.bitwise_or))
                    own.link(v.tensor_scalar(rank[:], prow[:], trial[:].bitcast(F32), None, ALU.is_ge, ALU.add, accum_out=cnt[:]))
                    own.link(v.tensor_scalar(enough[:], cnt[:], float(TOPK), None, ALU.is_ge))
                    v.engine_nop().then_inc(votes_in, 1)
                    dve.wait_ge(votes_done, n + 1)
                    own.link(v.tensor_scalar(digf[:], vp[:], 0.25 if n == 0 else 1.0, -1.0, ALU.mult, ALU.add))
                    own.link(v.tensor_copy(dig[:], digf[:]))
                    own.link(v.tensor_scalar(dig[:], dig[:], s, None, ALU.logical_shift_left))
                    own.link(v.tensor_tensor(found[:], found[:], dig[:], ALU.bitwise_or))

                thr = found[:].bitcast(F32)
                own.link(v.tensor_scalar(over[:], prow[:], thr, None, ALU.is_gt, ALU.add, accum_out=cnt[:]))
                own.add(v.tensor_scalar(cnt[:], cnt[:], -1.0, float(TOPK), ALU.mult, ALU.add))
                own.link(v.tensor_scalar(tie[:], prow[:], thr, None, ALU.is_equal))
                own.link(v.tensor_tensor_scan(rank[:], tie[:], tie[:], 0.0, ALU.add, ALU.max))
                own.link(v.scalar_tensor_tensor(out=tie[:], in0=rank[:], scalar=cnt[:], in1=tie[:], op0=ALU.is_le, op1=ALU.mult))
                own.link(v.tensor_tensor(over[:], over[:], tie[:], ALU.add))
                own.link(v.tensor_tensor_scan(rank[:], over[:], over[:], 0.0, ALU.add, ALU.max))
                own.link(v.tensor_tensor(rank[:], rank[:], over[:], ALU.mult))
                own.link(v.tensor_scalar(rank[:], rank[:], -1.0, None, ALU.add))
                v.engine_nop().then_inc(slot_done, 1)
                for n, (b, k) in enumerate(groups):
                    n += len(groups)
                    dve.wait_ge(tp_done, n + 1)
                    view = tp[n % 2][:, 0:k * P].rearrange("p (b x r) -> p b x r", x=X, r=REP)[:, :, :, 0]
                    v.tensor_copy(slot[:, b:b + k, :], view).then_inc(tp_copied, 1)
                dve.wait_ge(tp_copied, 2 * len(groups))
                own.link(v.tensor_copy(slot_i[:], slot[:]))
                own.add(v.tensor_scalar(lo_i[:], slot_i[:], P - 1, None, ALU.bitwise_and))
                own.link(v.tensor_scalar(hi_i[:], slot_i[:], P.bit_length() - 1, None, ALU.arith_shift_right))
                own.add(v.tensor_copy(lo[:], lo_i[:]))
                own.link(v.tensor_copy(hi[:], hi_i[:]))
                flat = lambda a: a.rearrange("p b x -> p (b x)").unsqueeze(2).broadcast_to([P, NB * X, ST])
                m = mask[:].rearrange("p b x t -> p (b x) t")
                own.link(v.tensor_tensor(m, flat(hi[:]), g.iota[:, 0:ST].unsqueeze(1).broadcast_to([P, NB * X, ST]), ALU.is_equal))
                own.add(v.tensor_tensor(val[:, :, 1, :], m, flat(g.prob[:]), ALU.mult))
                own.link(v.tensor_copy(rep[:, :, :, 0], tid[:].unsqueeze(2).broadcast_to([P, NB, X])))
                own.link(v.tensor_tensor(val[:, :, 0, :], m, flat(rep[:, :, :, 0]), ALU.mult))

                def hot(e, i, first):
                    if not first:
                        dve.wait_ge(list_done, e - 1)
                    v.tensor_tensor(lo_hot[i][:], lo[:, :, bass.ds(e, 1)].broadcast_to([P, NB, P]),
                                    g.iota[:, 0:P].unsqueeze(1).broadcast_to([P, NB, P]), ALU.is_equal).then_inc(hot_done, 1)

                def keep(e, i):
                    dve.wait_ge(list_done, e + 1)
                    v.tensor_copy(g.tok_i[:, bass.ds(e, 1), :].rearrange("p a t -> p (a t)"), lp[i][:, 0:ST]).then_inc(list_copied, 1)
                    v.tensor_copy(g.tok_p[:, bass.ds(e, 1), :].rearrange("p a t -> p (a t)"), lp[i][:, ST:2 * ST]).then_inc(list_copied, 1)

                hot(0, 0, True)
                hot(1, 1, True)
                with dve.Fori(1, X // 2) as n:
                    for i in range(2):
                        keep(n * 2 - 2 + i, i)
                        hot(n * 2 + i, i, False)
                keep(X - 2, 0)
                keep(X - 1, 1)
                dve.wait_ge(list_copied, 2 * X)

            @block.tensor
            def _(pe):
                for n, (b, k) in enumerate(groups):
                    if n == 0:
                        pe.wait_ge(rep_done, 1)
                    if n >= 2:
                        pe.wait_ge(tp_copied, n - 1)
                    for j in range(k):
                        m = nc.tensor.transpose(tp[n % 2][:, j * P:(j + 1) * P],
                                                rep[:, b + j, :, :].rearrange("p x r -> p (x r)"), g.ident[:])
                    m.then_inc(tp_done, 1)
                for n in range(len(SHIFTS)):
                    pe.wait_ge(votes_in, n + 1)
                    nc.tensor.matmul(vp[:], same[:], enough[:], start=True, stop=True).then_inc(votes_done, 1)
                for n, (b, k) in enumerate(groups):
                    n += len(groups)
                    if n == len(groups):
                        pe.wait_ge(slot_done, 1)
                    pe.wait_ge(tp_copied, n - 1)
                    for j in range(k):
                        m = nc.tensor.transpose(tp[n % 2][:, j * P:(j + 1) * P], rank[:, (b + j) * P:(b + j + 1) * P], g.ident[:])
                    m.then_inc(tp_done, 1)

                def lists(e, i, first):
                    pe.wait_ge(hot_done, e + 1)
                    if not first:
                        pe.wait_ge(list_copied, 2 * (e - 1))
                    for b in range(NB):
                        m = nc.tensor.matmul(lp[i][:], lo_hot[i][:, b, :],
                                             val[:, bass.ds(e + b * X, 1), :, :].rearrange("p a v t -> p (a v t)"),
                                             start=(b == 0), stop=(b == NB - 1))
                    m.then_inc(list_done, 1)
                lists(0, 0, True)
                lists(1, 1, True)
                with pe.Fori(1, X // 2) as n:
                    for i in range(2):
                        lists(n * 2 + i, i, False)


def stage_experts(nc, g, w1, w2, out):
    with ExitStack() as ctx:
        sb = lambda n, s, d=F32: ctx.enter_context(nc.sbuf_tensor(n, s, d))
        ps = lambda n, s: ctx.enter_context(nc.psum_tensor(n, s, F32))
        w1s = [sb(f"w1s{i}", [P, KT, FH]) for i in range(2)]
        w2s = [sb(f"w2s{i}", [P, FT, D]) for i in range(2)]
        xg = sb("xg", [P, ST, D])
        xt = sb("e_xt", [P, KT, TOPK])
        ht = sb("e_ht", [P, FT, TOPK])
        ob = [sb(f"e_out{i}", [P, D]) for i in range(2)]
        idx = [sb(f"e_idx{i}", [P, ST], I32) for i in range(2)]
        pr = [sb(f"e_pr{i}", [P, ST]) for i in range(2)]
        tp = [ps(f"e_tp{i}", [P, 4, P]) for i in range(2)]
        hp = [ps(f"e_hp{i}", [P, 512]) for i in range(2)]
        op = [ps(f"e_op{i}", [P, D]) for i in range(2)]
        idx_done, tp_done, tp_copied, h_done, h_copied, o_done, o_scaled, gated, padded = new_sems(
            nc, g.ctx, "e_idx_done", "e_tp_done", "e_tp_copied", "e_h_done", "e_h_copied",
            "e_o_done", "e_o_scaled", "experts_gated", "e_padded")
        w1_in = new_sems(nc, g.ctx, "w1_in0", "w1_in1")
        w2_in = new_sems(nc, g.ctx, "w2_in0", "w2_in1")
        xg_in = new_sems(nc, g.ctx, *[f"xg_in{t}" for t in range(ST)])
        o_out = new_sems(nc, g.ctx, "o_out0", "o_out1")
        size = lambda t: P if t < ST - 1 else SLAST
        halves = [(0, (TOPK + 1) // 2), ((TOPK + 1) // 2, TOPK)]
        UT = 2 * ST
        UH = FT * len(halves)
        uses = [(ST + 1) // 2, ST // 2]

        def each(eng, body):
            body(0, 0, 0, True, False)
            with eng.Fori(0, X // 2 - 1) as n:
                body(n * 2 + 1, 1, n, False, False)
                body(n * 2 + 2, 0, n + 1, False, False)
            body(X - 1, 1, X // 2 - 1, False, True)

        with nc.Block() as block:
            @block.sync
            def _(sp):
                for e in range(X):
                    i = e % 2
                    if e >= 2:
                        sp.wait_ge(h_done, UH * (e - 1))
                    sp.dma_start(w1s[i][:], w1[e].rearrange("(k p) f -> p k f", p=P)).then_inc(w1_in[i], 16)
                    if e >= 2:
                        sp.wait_ge(o_done, ST * (e - 1))
                    sp.dma_start(w2s[i][:], w2[e].rearrange("(k p) d -> p k d", p=P)).then_inc(w2_in[i], 16)

            @block.gpsimd
            def _(pool):
                nc.gpsimd.memset(g.gate[0:1, 1:2], 0.0).then_inc(gated, 1)

                def gather(e, i, turn):
                    pool.wait_ge(idx_done, 2 * e + 2)
                    if turn is not None:
                        pool.wait_ge(tp_done, UT * e)
                    gate(nc, g, gated, turn if turn is not None else 0)
                    for t in range(ST):
                        nc.gpsimd.indirect_dma_start(
                            xg[0:size(t), t, :], None, g.xn1[:, :],
                            bass.IndirectOffsetOnAxis(idx[i][0:size(t), t:t + 1], 0)).then_inc(xg_in[t], 16)

                def scatter(e, i, n, first, last):
                    base = e * (ST + 1) + 1
                    if not last:
                        gather(e + 1, 1 - i, base)
                    for t in range(ST):
                        if t == 0 and not first:
                            for j in range(2):
                                pool.wait_ge(o_out[j], 16 * uses[j] * e)
                        pool.wait_ge(o_scaled, ST * e + t + 1)
                        gate(nc, g, gated, base + t + (0 if last else 1))
                        nc.gpsimd.indirect_dma_start(
                            out[:, :], bass.IndirectOffsetOnAxis(idx[i][0:size(t), t:t + 1], 0), ob[t % 2][0:size(t), :],
                            None, bounds_check=N - 1, oob_is_err=True, compute_op=ALU.add).then_inc(o_out[t % 2], 16)
                pool.wait_ge(padded, 1)
                gather(0, 0, None)
                each(pool, scatter)
                for j in range(2):
                    pool.wait_ge(o_out[j], 16 * uses[j] * X)

            @block.vector
            def _(dve):
                v = nc.vector

                def lists(e, i, first):
                    if not first:
                        for j in range(2):
                            dve.wait_ge(o_out[j], 16 * uses[j] * (e - 1))
                    v.tensor_copy(idx[i][:], g.tok_i[:, bass.ds(e, 1), :].rearrange("p a t -> p (a t)")).then_inc(idx_done, 1)
                    v.tensor_copy(pr[i][:], g.tok_p[:, bass.ds(e, 1), :].rearrange("p a t -> p (a t)")).then_inc(idx_done, 1)

                def scale(e, i, n, first, last):
                    if not last:
                        lists(e + 1, 1 - i, first)
                    dve.wait_ge(idx_done, 2 * e + 2)
                    for t in range(ST):
                        j = t % 2
                        dve.wait_ge(o_done, ST * e + t + 1)
                        if not (first and t < 2):
                            dve.wait_ge(o_out[j], 16 * (uses[j] * e + t // 2))
                        v.tensor_scalar(ob[j][0:size(t), :], op[j][0:size(t), :], pr[i][0:size(t), t:t + 1], None,
                                        ALU.mult).then_inc(o_scaled, 1)
                v.memset(xg[:, ST - 1, :], 0.0).then_inc(padded, 1)
                lists(0, 0, True)
                each(dve, scale)

            @block.scalar
            def _(act):
                def turn(e, first):
                    if not first:
                        act.wait_ge(h_done, UH * e)
                    for u in range(UT):
                        t, k = u // 2, (u % 2) * 4
                        act.wait_ge(tp_done, UT * e + u + 1)
                        nc.scalar.copy(xt[:, k:k + 4, t * P:t * P + size(t)], tp[u % 2][:, :, 0:size(t)]).then_inc(tp_copied, 1)

                def step(e, i, n, first, last):
                    if not first:
                        act.wait_ge(o_done, ST * e)
                    for u in range(UH):
                        f, (a, b) = u // 2, halves[u % 2]
                        act.wait_ge(h_done, UH * e + u + 1)
                        nc.scalar.activation(ht[:, f, a:b], hp[u % 2][:, 0:b - a], ACT.Gelu).then_inc(h_copied, 1)
                    if not last:
                        turn(e + 1, False)
                turn(0, True)
                each(act, step)

            @block.tensor
            def _(pe):
                def turn(e, first):
                    for u in range(UT):
                        t, k = u // 2, (u % 2) * 4
                        if u % 2 == 0:
                            pe.wait_ge(xg_in[t], 16 * (e + 1))
                        if not (first and u < 2):
                            pe.wait_ge(tp_copied, UT * e + u - 1)
                        for j in range(4):
                            m = nc.tensor.transpose(tp[u % 2][:, j, :], xg[:, t, (k + j) * P:(k + j + 1) * P], g.ident[:])
                        m.then_inc(tp_done, 1)

                def step(e, i, n, first, last):
                    pe.wait_ge(tp_copied, UT * (e + 1))
                    pe.wait_ge(w1_in[i], 16 * (n + 1))
                    for u in range(UH):
                        f, (a, b) = u // 2, halves[u % 2]
                        if not (first and u < 2):
                            pe.wait_ge(h_copied, UH * e + u - 1)
                        for k in range(KT):
                            m = nc.tensor.matmul(hp[u % 2][:, 0:b - a], w1s[i][:, k, f * P:(f + 1) * P], xt[:, k, a:b],
                                                 start=(k == 0), stop=(k == KT - 1))
                        m.then_inc(h_done, 1)
                    if not last:
                        turn(e + 1, False)
                    pe.wait_ge(h_copied, UH * (e + 1))
                    pe.wait_ge(w2_in[i], 16 * (n + 1))
                    for t in range(ST):
                        if not (first and t < 2):
                            pe.wait_ge(o_scaled, ST * e + max(t - 1, 0))
                        for n_ in range(2):
                            for f in range(FT):
                                m = nc.tensor.matmul(op[t % 2][0:size(t), n_ * 512:(n_ + 1) * 512],
                                                     ht[:, f, t * P:t * P + size(t)], w2s[i][:, f, n_ * 512:(n_ + 1) * 512],
                                                     start=(f == 0), stop=(f == FT - 1))
                        m.then_inc(o_done, 1)
                turn(0, True)
                each(pe, step)


def build(nc, x, src, dst, W, att_src, att_dst, bias, gate_w, w1, w2, out):
    from_dram = lambda n, s, d=F32: nc.dram_tensor(n, s, d).ap()
    with ExitStack() as top:
        g = Core()
        g.ctx = top
        g.lines = from_dram("dst_lines", (P, EC))
        g.starts = from_dram("edge_starts", (NP + 1,))
        g.laid = from_dram("laid_scores", (NC * CH, 2 * H))
        g.low = from_dram("low_addresses", (EC, P), BF16)
        g.xp = from_dram("xp_rows", (NP, D))
        g.rec = from_dram("edge_records", (NC * CH, REC))
        g.xn1 = from_dram("xn1_rows", (N, D))
        setup(nc, top, g)
        keep = lambda c, n, s, d=F32: c.enter_context(nc.sbuf_tensor(n, s, d))
        g.prob = keep(top, "prob", [P, NB, X])
        with ExitStack() as gnn:
            g.big = keep(gnn, "big", [P, NB, D])
            g.acc_side = keep(gnn, "acc_side", [P, NB, 2 * H + 1])
            g.blk_i = keep(gnn, "blk_i", [P, ITEMS], I32)
            g.chk_i = keep(gnn, "chk_i", [P, ITEMS], I32)
            with ExitStack() as mid:
                g.first, g.last = keep(mid, "first", [P, EC]), keep(mid, "last", [P, EC])
                g.src_i = keep(mid, "src_i", [P, EC], I32)
                g.dst_f = keep(mid, "dst_f", [P, EC + 2])
                g.start_i = keep(mid, "start_i", [P, NB], I32)
                g.atab = keep(mid, "atab", [P, NB, 2 * H])
                stage_nodes(nc, g, x, src, dst, W, att_src, att_dst)
                g.edge_s = keep(mid, "edge_s", [P, EC, H])
                g.edge_d = keep(mid, "edge_d", [P, EC, 2 * H])
                stage_scores(nc, g)
                stage_weights(nc, g)
            stage_messages(nc, g)
            stage_residual(nc, g, x, bias, gate_w, out)
        g.tok_i = keep(top, "tok_i", [P, X, ST], I32)
        g.tok_p = keep(top, "tok_p", [P, X, ST])
        stage_select(nc, g)
        stage_experts(nc, g, w1, w2, out)


_INS = ["x", "src", "dst", "L0_gnn_W", "L0_gnn_att_src", "L0_gnn_att_dst", "L0_gnn_bias", "L0_ffn_gate_w",
        "L0_ffn_w1", "L0_ffn_w2"]


def kernel(**inputs):
    import numpy as np
    import concourse.bacc as bacc
    from concourse.bass_utils import run_bass_kernel_spmd

    nc = bacc.Bacc("TRN2", target_bir_lowering=False, num_devices=1)
    arrays, args = {}, []
    for name in _INS:
        a = np.ascontiguousarray(inputs[name])
        arrays[f"in_{name}"] = a
        args.append(nc.dram_tensor(f"in_{name}", a.shape, mybir.dt.from_np(a.dtype), kind="ExternalInput").ap())
    args.append(nc.dram_tensor("out_rows", (N, D), F32, kind="ExternalOutput").ap())
    build(nc, *args)
    r = run_bass_kernel_spmd(nc, [arrays], core_ids=[0])
    return r.results[0]["out_rows"]
```

```python
from contextlib import ExitStack

import concourse.bass as bass
from concourse import mybir

F32 = mybir.dt.float32
I32 = mybir.dt.int32
F32R = mybir.dt.float32r
BF16 = mybir.dt.bfloat16
ALU = mybir.AluOpType
ACT = mybir.ActivationFunctionType
AX = mybir.AxisListType

P = 128
N = 3125
D = 1024
KT = D // P
NB = -(-N // P)
LAST = N - (NB - 1) * P
NP = NB * P
H = 4
C = D // H
E = 50000
SUB = 2
CH = SUB * P
NC = -(-E // (8 * P)) * 8 // SUB
EC = NC * CH // P
ELAST = E - (P - 1) * EC
PATH = 55
ITEMS = NC + NB - 1
REC = 20
W_AT, DST_AT, SRC_AT, SUMMED_AT = 0, 4, 5, 6
PARTS = 3
SUMMED = 2 * PARTS * H + 2
SELF_AT, FIRST_AT = PARTS * H, 2 * PARTS * H
SLOPE = 0.2
EPS = 1e-5
NEG = -1e38
X = 8
FH = 512
FT = FH // P
TOPK = 2 * N // X
ST = -(-TOPK // P)
SLAST = TOPK - (ST - 1) * P
REP = P // X


class Links:

    def __init__(self, eng, sem):
        self.eng, self.sem, self.n = eng, sem, 0

    def add(self, ins):
        ins.then_inc(self.sem, 1)
        self.n += 1

    def wait(self):
        self.eng.wait_ge(self.sem, self.n)

    def link(self, ins):
        self.add(ins)
        self.wait()


class Core:
    pass


def new_sems(nc, ctx, *names):
    made = [nc.alloc_semaphore(n) for n in names]
    ctx.extend(made)
    return made


def clear_sems(nc, used):
    with nc.Block() as block:
        @block.gpsimd
        def _(pool):
            nc.clear_and_free_semaphores(used)
    used.clear()


def gate(nc, g, sem, turn):
    nc.gpsimd.wait_ge(sem, turn + 1)
    nc.gpsimd.tensor_tensor(g.gate[0:1, 1:2], g.gate[0:1, 0:1], g.gate[0:1, 0:1], ALU.add).then_inc(sem, 1)


def setup(nc, ctx, g):
    sb = lambda n, s, d=F32: ctx.enter_context(nc.sbuf_tensor(n, s, d))
    g.iota = sb("iota", [P, NP])
    g.ident = sb("ident", [P, P])
    g.gate = sb("gate", [P, 2])
    g.pcol = sb("pcol", [P, 1])
    iota_done, consts_done = new_sems(nc, g.ctx, "iota_done", "consts_done")
    with nc.sbuf_tensor("iota_int", [P, NP], I32) as ints, nc.sbuf_tensor("pcol_int", [P, 1], I32) as pint, nc.Block() as block:
        @block.gpsimd
        def _(pool):
            nc.gpsimd.iota(ints[:], [[1, NP]], base=0, channel_multiplier=0).then_inc(iota_done, 1)
            nc.gpsimd.iota(pint[:], [[0, 1]], base=0, channel_multiplier=1).then_inc(iota_done, 1)

        @block.vector
        def _(dve):
            own = Links(dve, consts_done)
            own.add(nc.vector.memset(g.gate[:], 0.0))
            dve.wait_ge(iota_done, 2)
            own.add(nc.vector.tensor_copy(g.iota[:], ints[:]))
            own.link(nc.vector.tensor_copy(g.pcol[:], pint[:]))
            own.link(nc.vector.tensor_scalar(g.ident[:], g.iota[:, 0:P], g.pcol[:], None, ALU.is_equal))


def stage_order(nc, g, src, dst):
    with ExitStack() as ctx:
        sb = lambda n, s, d=F32: ctx.enter_context(nc.sbuf_tensor(n, s, d))
        ps = lambda n, s: ctx.enter_context(nc.psum_tensor(n, s, F32))
        dst_i, src_i = sb("o_dst_i", [P, EC + 1], I32), sb("o_src_i", [P, EC], I32)
        dst_f = sb("o_dst_f", [P, EC + 1])
        falls, fell = sb("o_falls", [P, EC]), sb("o_fell", [P, 1])
        ones = sb("o_ones", [P, P])
        flag = sb("o_flag", [P, 1], I32)
        per, base, total, junk = (sb(n, [P, NP]) for n in ("o_per", "o_base", "o_total", "o_junk"))
        lower = sb("o_lower", [P, P])
        place_f, place = sb("o_place_f", [P, 1]), sb("o_place", [P, 1], I32)
        one_dst, one_src = sb("o_one_dst", [P, 1], I32), sb("o_one_src", [P, 1], I32)
        fell_ps = ps("o_fell_ps", [P, 1])
        tot_ps, low_ps = ps("o_total_ps", [P, 512]), ps("o_lower_ps", [P, 512])
        (filled, edges_in, own_dve, fell_in, fell_done, edges_out, counted, counts_in, summed, summed_read, step_dve,
         placed, scattered, gated) = new_sems(
            nc, g.ctx, "o_filled", "o_edges_in", "order_dve", "o_fell_in", "o_fell_done", "o_edges_out", "o_counted",
            "o_counts_in", "o_summed", "o_summed_read", "o_step_dve", "o_placed", "o_scattered", "o_gated")
        with nc.Block() as block:
            @block.sync
            def _(sp):
                sp.wait_ge(filled, 2)
                sp.dma_start(dst_i[0:P - 1, :], bass.AP(dst.tensor, 0, [[EC, P - 1], [1, EC + 1]])).then_inc(edges_in, 16)
                sp.dma_start(dst_i[P - 1:P, 0:ELAST], dst[(P - 1) * EC:E].unsqueeze(0)).then_inc(edges_in, 16)
                sp.dma_start(src_i[0:P - 1, :], src[0:(P - 1) * EC].rearrange("(p n) -> p n", p=P - 1)).then_inc(edges_in, 16)
                sp.dma_start(src_i[P - 1:P, 0:ELAST], src[(P - 1) * EC:E].unsqueeze(0)).then_inc(edges_in, 16)
                sp.wait_ge(edges_in, 16 * 4)
                sp.dma_start(g.dst_s.rearrange("(p n) a -> p (n a)", p=P), dst_i[:, 0:EC]).then_inc(edges_out, 16)
                sp.dma_start(g.src_s.rearrange("(p n) a -> p (n a)", p=P), src_i[:]).then_inc(edges_out, 16)
                sp.wait_ge(edges_out, 32)

            @block.vector
            def _(dve):
                v = nc.vector
                own = Links(dve, own_dve)
                v.memset(dst_i[:], NP + P).then_inc(filled, 1)
                v.memset(src_i[:], 0).then_inc(filled, 1)
                own.add(v.memset(ones[:], 1.0))
                dve.wait_ge(edges_in, 16 * 4)
                own.link(v.tensor_copy(dst_f[:], dst_i[:]))
                own.link(v.tensor_tensor(falls[:], dst_f[:, 0:EC], dst_f[:, 1:EC + 1], ALU.is_gt))
                own.link(v.tensor_reduce(fell[:], falls[:], AX.X, ALU.add))
                v.engine_nop().then_inc(fell_in, 1)
                dve.wait_ge(fell_done, 1)
                own.link(v.tensor_scalar(flag[:], fell_ps[:], 1.0, None, ALU.min))

            @block.tensor
            def _(pe):
                pe.wait_ge(fell_in, 1)
                nc.tensor.matmul(fell_ps[:], ones[:], fell[:], start=True, stop=True).then_inc(fell_done, 1)

        chunks = [(a, min(a + 512, NP)) for a in range(0, NP, 512)]
        with nc.Block() as block:
            @block.vector
            def _(dve):
                v = nc.vector
                with dve.If(dve.value_load(flag[0:1, 0:1], min_val=0, max_val=1) > 0):
                    v.memset(g.gate[0:1, 1:2], 0.0).then_inc(gated, 1)
                    v.memset(per[:], 0.0).then_inc(counted, 1)
                    dve.wait_ge(counted, 1)
                    with dve.Fori(0, EC) as j:
                        v.scalar_tensor_tensor(out=per[:], in0=g.iota[:], scalar=dst_f[:, bass.ds(j, 1)], in1=per[:],
                                               op0=ALU.is_equal, op1=ALU.add).then_inc(counted, 1)
                        dve.wait_ge(counted, j + 2)
                    v.tensor_scalar(lower[:], g.iota[:, 0:P], g.pcol[:], None, ALU.is_gt).then_inc(counts_in, 1)
                    for n, (a, b) in enumerate(chunks):
                        dve.wait_ge(summed, n + 1)
                        v.tensor_copy(total[:, a:b], tot_ps[:, 0:b - a]).then_inc(summed_read, 1)
                        v.tensor_copy(base[:, a:b], low_ps[:, 0:b - a]).then_inc(summed_read, 1)
                    dve.wait_ge(summed_read, 2 * len(chunks))
                    v.tensor_tensor_scan(junk[:], total[:], total[:], 0.0, ALU.add, ALU.max).then_inc(counts_in, 1)
                    dve.wait_ge(counts_in, 2)
                    v.tensor_tensor(junk[:], junk[:], total[:], ALU.subtract).then_inc(counts_in, 1)
                    dve.wait_ge(counts_in, 3)
                    v.tensor_tensor(base[:], base[:], junk[:], ALU.add).then_inc(counts_in, 1)
                    dve.wait_ge(counts_in, 4)
                    with dve.Fori(0, EC) as j:
                        node = dst_f[:, bass.ds(j, 1)]
                        v.scalar_tensor_tensor(out=junk[:], in0=g.iota[:], scalar=node, in1=base[:], op0=ALU.is_equal,
                                               op1=ALU.mult, accum_out=place_f[:]).then_inc(step_dve, 1)
                        dve.wait_ge(step_dve, j * 4 + 1)
                        v.scalar_tensor_tensor(out=base[:], in0=g.iota[:], scalar=node, in1=base[:], op0=ALU.is_equal,
                                               op1=ALU.add).then_inc(step_dve, 1)
                        v.tensor_scalar(junk[:, 0:1], node, float(NP), float(2 * NC * CH), ALU.is_ge, ALU.mult).then_inc(step_dve, 1)
                        dve.wait_ge(step_dve, j * 4 + 3)
                        v.tensor_tensor(place[:], place_f[:], junk[:, 0:1], ALU.add).then_inc(step_dve, 1)
                        v.tensor_copy(one_dst[:], dst_i[:, bass.ds(j, 1)]).then_inc(placed, 1)
                        v.tensor_copy(one_src[:], src_i[:, bass.ds(j, 1)]).then_inc(placed, 1)
                        dve.wait_ge(step_dve, j * 4 + 4)
                        dve.wait_ge(scattered, j * 32 + 32)

            @block.tensor
            def _(pe):
                with pe.If(pe.value_load(flag[0:1, 0:1], min_val=0, max_val=1) > 0):
                    pe.wait_ge(counts_in, 1)
                    for n, (a, b) in enumerate(chunks):
                        if n:
                            pe.wait_ge(summed_read, 2 * n)
                        nc.tensor.matmul(tot_ps[:, 0:b - a], ones[:], per[:, a:b], start=True, stop=True)
                        nc.tensor.matmul(low_ps[:, 0:b - a], lower[:], per[:, a:b], start=True, stop=True).then_inc(summed, 1)

            @block.gpsimd
            def _(pool):
                with pool.If(pool.value_load(flag[0:1, 0:1], min_val=0, max_val=1) > 0):
                    with pool.Fori(0, EC) as j:
                        pool.wait_ge(step_dve, j * 4 + 4)
                        pool.wait_ge(placed, j * 2 + 2)
                        gate(nc, g, gated, j)
                        for table, one in ((g.dst_s, one_dst), (g.src_s, one_src)):
                            nc.gpsimd.indirect_dma_start(table[:, :], bass.IndirectOffsetOnAxis(place[:], 0), one[:], None,
                                                         bounds_check=E - 1, oob_is_err=False).then_inc(scattered, 16)


XR = 4
LG = 13
DW = D + 2 * H
DG = DW // 3


def in_rings(eng, body):
    for q in range(XR):
        body(q, q, 0, True)
    with eng.Fori(1, NB // XR) as n:
        for q in range(XR):
            body(n * XR + q, q, n, False)
    for b in range(NB // XR * XR, NB):
        body(b, b % XR, b // XR, False)


def stage_nodes(nc, g, x, W, att_src, att_dst):
    flat = g.big[:].rearrange("p b d -> p (b d)")
    used = [0]

    def piece(cols):
        used[0] += cols
        assert used[0] <= NB * D
        return flat[:, used[0] - cols:used[0]]

    with ExitStack() as ctx:
        sb = lambda n, s, d=F32: ctx.enter_context(nc.sbuf_tensor(n, s, d))
        ps = lambda n, s: ctx.enter_context(nc.psum_tensor(n, s, F32))
        raw = piece(KT * D).rearrange("p (k n) -> p k n", k=KT)
        xr = [piece(D) for _ in range(XR)]
        xn = [piece(D) for _ in range(2)]
        xo = [piece(DW) for _ in range(2)]
        prod = [piece(D) for _ in range(2)]
        product = piece(D)
        att = xo
        rawf = raw.rearrange("p k n -> p (k n)")
        lines = rawf[:, 0:LG * EC].rearrange("p (b n) -> p b n", b=LG)
        below = rawf[:, 0:LG * P].rearrange("p (b n) -> p b n", b=LG)
        passed = rawf[:, 0:PATH * (NB - 1)].rearrange("p (i k) -> p i k", k=NB - 1)
        wh, wl = sb("w_high", [P, KT, DW], F32R), sb("w_low", [P, KT, DW], F32R)
        xh = [sb(f"x_high{i}", [P, D], F32R) for i in range(2)]
        xl = [sb(f"x_low{i}", [P, D], F32R) for i in range(2)]
        stats = [sb(f"ln_stats{i}", [P, 12]) for i in range(2)]
        mv = [sb(f"ln_mv{i}", [P, 2]) for i in range(2)]
        std = [sb(f"ln_std{i}", [P, 1]) for i in range(2)]
        rstd = [sb(f"ln_rstd{i}", [P, 1]) for i in range(2)]
        eps, hold = sb("ln_eps", [P, 1]), sb("ln_hold", [1, 1])
        wa = sb("wa", [P, KT, 2 * H])
        row_at, node, before = sb("row_at", [P, NB]), sb("node", [P, NB]), sb("before", [P, NB])
        row_i = sb("row_i", [P, NB], I32)
        heads, heads_b = piece(P)[0:1, :], piece(P)
        start, after = sb("start", [P, NB]), sb("after", [P, NB])
        tail = sb("tail_const", [1, 1])
        junk = piece(EC)
        ones = piece(P)
        counts, step_at = sb("counts", [P, NB - 1]), sb("step_at", [P, NB - 1])
        cnt_i = sb("cnt_i", [P, NB - 1], I32)
        blk_f, chk_f = piece(ITEMS), piece(ITEMS)
        tp = [ps(f"tp{i}", [P, 512]) for i in range(2)]
        pp = [ps(f"pp{i}", [P, 3, 512]) for i in range(2)]
        cnt_ps = tp[0][:, 0:NB - 1]
        (att_in, own_dve, wa_parts, prod_done, prod_read, wa_done, wh_done, wl_done, stats_done, var_done, std_done,
         rstd_done, xn_done, tp_done, high_done, low_done, pp_done, xo_done, atab_done, edges_in, fills,
         dst_done, dst_out, heads_in, heads_done, row_done, lines_read, start_done, start_out, after_in, cnt_in,
         cnt_done) = new_sems(
            nc, g.ctx, "att_in", "nodes_dve", "wa_parts", "prod_done", "prod_read", "wa_done", "w_high_done", "w_low_done",
            "stats_done", "var_done", "std_done", "rstd_done", "xn_done", "tp_done", "x_high_done", "x_low_done",
            "pp_done", "xo_done", "atab_done", "edges_in", "edge_fills", "dst_done", "dst_out",
            "heads_in", "heads_done", "row_done", "lines_read", "start_done", "start_out", "after_in", "cnt_in",
            "cnt_done")
        x_in = new_sems(nc, g.ctx, *[f"x_in{q}" for q in range(XR)])
        xp_out = new_sems(nc, g.ctx, "xp_out0", "xp_out1")
        w_in = new_sems(nc, g.ctx, "w_in0", "w_in1")
        lines_in = new_sems(nc, g.ctx, "lines_in0", "lines_in1")
        line_groups = [(0, LG), (LG, NB)]
        dst_i = piece(EC + 2).bitcast(I32)
        dst_s = g.dst_s.tensor
        cur = g.dst_f[:, 1:EC + 1]
        with nc.Block() as block:
            @block.sync
            def _(sp):
                def load(b, q, n, first):
                    if not first:
                        sp.wait_ge(xn_done, b - XR + 1)
                    r = LAST if isinstance(b, int) and b == NB - 1 else P
                    sp.dma_start(xr[q][0:r, :], x[bass.ds(b * P, r), :]).then_inc(x_in[q], 16)

                def store(b, i):
                    sp.wait_ge(xo_done, b + 1)
                    sp.dma_start(g.xp[bass.ds(b * P, P), :], xo[i][:, 0:D]).then_inc(xp_out[i], 16)

                def both(b, q, n, first):
                    load(b, q, n, first)
                    if not first:
                        store(b - XR, q % 2)
                load(0, 0, 0, True)
                sp.dma_start(raw[:, 0:KT // 2, :], W[0:D // 2, :].rearrange("(k p) n -> p k n", p=P)).then_inc(w_in[0], 16)
                load(1, 1, 0, True)
                sp.dma_start(raw[:, KT // 2:KT, :], W[D // 2:D, :].rearrange("(k p) n -> p k n", p=P)).then_inc(w_in[1], 16)
                sp.wait_ge(fills, 1)
                sp.dma_start(dst_i[0:1, 1:EC + 2], bass.AP(dst_s, 0, [[EC, 1], [1, EC + 1]])).then_inc(edges_in, 16)
                sp.dma_start(dst_i[1:P - 1, :], bass.AP(dst_s, EC - 1, [[EC, P - 2], [1, EC + 2]])).then_inc(edges_in, 16)
                sp.dma_start(dst_i[P - 1:P, 0:EC + 1], bass.AP(dst_s, (P - 1) * EC - 1, [[EC, 1], [1, EC + 1]])).then_inc(edges_in, 16)
                sp.dma_start(g.src_i[:], g.src_s.rearrange("(p n) a -> p (n a)", p=P)).then_inc(edges_in, 16)
                for q in range(2, XR):
                    load(q, q, 0, True)
                sp.wait_ge(dst_done, 1)
                sp.dma_start(g.lines[:, :], cur).then_inc(dst_out, 16)
                sp.wait_ge(dst_out, 16)
                sp.dma_start(heads, g.lines[:, 0:1].rearrange("p a -> a p"), allow_slow_non_contiguous=True).then_inc(heads_in, 16)
                with sp.Fori(1, NB // XR) as n:
                    for q in range(XR):
                        both(n * XR + q, q, n, False)
                sp.wait_ge(start_done, 2)
                sp.dma_start(g.starts[0:NP].rearrange("(b p) -> p b", p=P), start[:], allow_slow_non_contiguous=True).then_inc(start_out, 16)
                sp.dma_start(g.starts[NP:NP + 1].unsqueeze(0), tail[:]).then_inc(start_out, 16)
                sp.wait_ge(start_out, 32)
                sp.dma_start(after[:], g.starts[1:NP + 1].rearrange("(b p) -> p b", p=P), allow_slow_non_contiguous=True).then_inc(after_in, 16)
                for b in range(NB // XR * XR, NB):
                    both(b, b % XR, b // XR, False)
                for b in range(NB - XR, NB):
                    store(b, b % 2)
                sp.wait_ge(xp_out[0], 16 * ((NB + 1) // 2))
                sp.wait_ge(xp_out[1], 16 * (NB // 2))

            @block.gpsimd
            def _(pool):
                pool.wait_ge(att_in, 32)
                for k in range(KT):
                    pool.wait_ge(w_in[k // (KT // 2)], 16)
                    if k >= 2:
                        pool.wait_ge(prod_read, k - 1)
                    nc.gpsimd.tensor_tensor(prod[k % 2], raw[:, k, :], att[0][:, 0:D], ALU.mult).then_inc(prod_done, 1)
                pool.wait_ge(heads_in, 16)
                nc.gpsimd.partition_broadcast(heads_b, heads, P).then_inc(heads_done, 1)
                pool.wait_ge(row_done, 1)
                for n, (lo, hi) in enumerate(line_groups):
                    if n:
                        pool.wait_ge(lines_read, lo)
                    for b in range(lo, hi):
                        nc.gpsimd.indirect_dma_start(lines[:, b - lo, :], None, g.lines[:, :],
                                                     bass.IndirectOffsetOnAxis(row_i[:, b:b + 1], 0)).then_inc(lines_in[n], 16)

            @block.vector
            def _(dve):
                v = nc.vector
                own = Links(dve, own_dve)
                v.memset(dst_i, NP + P).then_inc(fills, 1)
                own.add(v.memset(eps[:], EPS))
                own.add(v.memset(ones, 1.0))
                v.memset(tail[:], float(E)).then_inc(start_done, 1)
                own.add(v.memset(xn[0], 0.0))
                own.link(v.tensor_scalar(node[:], g.iota[:, 0:NB], float(P), g.pcol[:], ALU.mult, ALU.add))

                def normalise(b, q, n, first):
                    i = q % 2
                    dve.wait_ge(x_in[q], 16 * (n + 1))
                    for j in range(2):
                        v.bn_stats(stats[i][:, j * 6:j * 6 + 6], xr[q][:, j * 512:(j + 1) * 512]).then_inc(stats_done, 1)
                    dve.wait_ge(stats_done, 2 * (b + 1))
                    if isinstance(b, int) and b == 0:
                        v.memset(hold[:], 0.0).then_inc(fills, 1)
                    else:
                        low(b - 1, 1 - i, first and q < 3)
                    v.bn_aggr(mv[i][:], stats[i][:]).then_inc(var_done, 1)
                    dve.wait_ge(std_done, b + 1)
                    v.reciprocal(rstd[i][:], std[i][:]).then_inc(rstd_done, 1)
                    dve.wait_ge(rstd_done, b + 1)
                    if not (first and q < 2):
                        dve.wait_ge(tp_done, 2 * (b - 1))
                    v.tensor_scalar(xn[i], xr[q], mv[i][:, 0:1], rstd[i][:], ALU.subtract, ALU.mult).then_inc(xn_done, 1)

                def low(b, i, first):
                    for j in range(2):
                        dve.wait_ge(high_done, 2 * b + j + 1)
                        c = slice(j * 512, (j + 1) * 512)
                        v.tensor_tensor(xl[i][:, c], tp[j][:], xh[i][:, c].bitcast(F32), ALU.subtract).then_inc(low_done, 1)

                dve.wait_ge(edges_in, 16 * 4)
                v.tensor_copy(g.dst_f[:], dst_i).then_inc(dst_done, 1)
                normalise(0, 0, 0, True)
                dve.wait_ge(dst_done, 1)
                own.add(v.tensor_tensor(g.first[:], cur, g.dst_f[:, 0:EC], ALU.not_equal))
                own.add(v.tensor_tensor(g.last[:], cur, g.dst_f[:, 2:EC + 2], ALU.not_equal))
                for k in range(KT):
                    dve.wait_ge(wh_done, k + 1)
                    v.tensor_tensor(wl[:, k, 0:D], raw[:, k, :], wh[:, k, 0:D].bitcast(F32), ALU.subtract).then_inc(wl_done, 1)
                dve.wait_ge(att_in, 32)
                for k in range(KT):
                    for h in range(H):
                        c = slice(h * C, (h + 1) * C)
                        v.scalar_tensor_tensor(out=product[:, c], in0=raw[:, k, c], scalar=1.0, in1=att[1][:, c], op0=ALU.mult,
                                               op1=ALU.mult, accum_out=wa[:, k, H + h:H + h + 1]).then_inc(wa_parts, 1)
                    dve.wait_ge(wa_parts, (k + 1) * H)
                    dve.wait_ge(prod_done, k + 1)
                    v.tensor_reduce(wa[:, k, 0:H], prod[k % 2].rearrange("p (h c) -> p h c", h=H), AX.X, ALU.add).then_inc(prod_read, 1)
                dve.wait_ge(prod_read, KT)
                own.link(v.tensor_copy(wh[:, :, D:DW], wa[:]))
                v.tensor_tensor(wl[:, :, D:DW], wa[:], wh[:, :, D:DW].bitcast(F32), ALU.subtract).then_inc(wa_done, 1)
                normalise(1, 1, 0, True)
                dve.wait_ge(heads_done, 1)
                dve.wait_ge(wl_done, KT)
                for lo, hi in ((0, LG), (LG, NB)):
                    k = hi - lo
                    own.link(v.tensor_tensor(below[:, 0:k, :], heads_b.unsqueeze(1).broadcast_to([P, k, P]),
                                             node[:, lo:hi].unsqueeze(2).broadcast_to([P, k, P]), ALU.is_lt))
                    own.link(v.tensor_reduce(row_at[:, lo:hi], below[:, 0:k, :], AX.X, ALU.add))
                own.link(v.tensor_scalar(row_at[:], row_at[:], -1.0, 0.0, ALU.add, ALU.max))
                v.tensor_copy(row_i[:], row_at[:]).then_inc(row_done, 1)
                for q, (lo, hi) in zip((2, 3), line_groups):
                    normalise(q, q, 0, True)
                    dve.wait_ge(lines_in[q - 2], 16 * (hi - lo))
                    for b in range(lo, hi):
                        v.tensor_scalar(junk, lines[:, b - lo, :], node[:, b:b + 1], None, ALU.is_lt, ALU.add,
                                        accum_out=before[:, b:b + 1]).then_inc(lines_read, 1)
                        dve.wait_ge(lines_read, b + 1)
                v.scalar_tensor_tensor(out=start[:], in0=row_at[:], scalar=float(EC), in1=before[:], op0=ALU.mult,
                                       op1=ALU.add).then_inc(start_done, 1)
                with dve.Fori(1, NB // XR) as n:
                    for q in range(XR):
                        normalise(n * XR + q, q, n, False)
                for b in range(NB // XR * XR, NB):
                    normalise(b, b % XR, b // XR, False)
                for k in range(1, NB):
                    own.link(v.tensor_scalar(junk, cur, float(k * P), None, ALU.is_lt, ALU.add, accum_out=counts[:, k - 1:k]))
                v.engine_nop().then_inc(cnt_in, 1)
                low(NB - 1, (NB - 1) % 2, False)
                dve.wait_ge(cnt_done, 1)
                own.link(v.tensor_scalar(step_at[:], cnt_ps, float(E - 1), None, ALU.min))
                own.link(v.tensor_copy(cnt_i[:], step_at[:]))
                own.link(v.tensor_scalar(cnt_i[:], cnt_i[:], CH.bit_length() - 1, None, ALU.logical_shift_right))
                own.link(v.tensor_copy(counts[:], cnt_i[:]))
                own.link(v.tensor_tensor(step_at[:], counts[:], g.iota[:, 1:NB], ALU.add))
                for a in range(0, ITEMS, PATH):
                    own.link(v.tensor_tensor(passed, step_at[:].unsqueeze(1).broadcast_to([P, PATH, NB - 1]),
                                             g.iota[:, a:a + PATH].unsqueeze(2).broadcast_to([P, PATH, NB - 1]), ALU.is_le))
                    own.link(v.tensor_reduce(blk_f[:, a:a + PATH], passed, AX.X, ALU.add))
                own.link(v.tensor_tensor(chk_f, g.iota[:, 0:ITEMS], blk_f, ALU.subtract))
                own.add(v.tensor_copy(g.blk_i[:], blk_f))
                own.link(v.tensor_copy(g.chk_i[:], chk_f))
                dve.wait_ge(after_in, 16)
                dve.wait_ge(start_out, 32)
                own.link(v.tensor_tensor(after[:], start[:], after[:], ALU.is_equal))
                own.link(v.scalar_tensor_tensor(out=start[:], in0=after[:], scalar=float(2 * NC * CH), in1=start[:],
                                                op0=ALU.mult, op1=ALU.add))
                own.link(v.tensor_copy(g.start_i[:], start[:]))

            @block.scalar
            def _(act):
                for i, a in enumerate((att_src, att_dst)):
                    act.dma_start(att[i][:, 0:D], a.rearrange("h c -> (h c)").unsqueeze(0).broadcast_to([P, D])).then_inc(att_in, 16)

                def deviation(b, i):
                    act.wait_ge(var_done, b + 1)
                    nc.scalar.activation(std[i][:], mv[i][:, 1:2], ACT.Sqrt, bias=eps[:]).then_inc(std_done, 1)

                def high(b, i, first):
                    if not first:
                        act.wait_ge(pp_done, b - 1)
                    for j in range(2):
                        act.wait_ge(tp_done, 2 * b + j + 1)
                        nc.scalar.copy(xh[i][:, j * 512:(j + 1) * 512], tp[j][:]).then_inc(high_done, 1)

                def out(b, i, turn):
                    act.wait_ge(pp_done, b + 1)
                    if turn is not None:
                        act.wait_ge(xp_out[i], 16 * turn)
                    nc.scalar.copy(xo[i].rearrange("p (g n) -> p g n", g=3), pp[i][:, :, 0:DG]).then_inc(xo_done, 1)
                    nc.scalar.copy(g.atab[:, bass.ds(b, 1), :].rearrange("p a n -> p (a n)"),
                                   pp[i][:, 2, DG - 2 * H:DG]).then_inc(atab_done, 1)

                def step(b, q, n, first):
                    high(b, q % 2, first and q < 2)
                    if not (isinstance(b, int) and b == NB - 1):
                        deviation(b + 1, (q + 1) % 2)
                    if not (first and q == 0):
                        turn = None if first and q < 3 else (n * 2 + (q - 1) // 2)
                        out(b - 1, (q + 1) % 2, turn)
                deviation(0, 0)
                for k in range(KT):
                    act.wait_ge(w_in[k // (KT // 2)], 16)
                    nc.scalar.copy(wh[:, k, 0:D], raw[:, k, :]).then_inc(wh_done, 1)
                in_rings(act, step)
                out(NB - 1, (NB - 1) % 2, (NB - 1) // 2)

            @block.tensor
            def _(pe):
                def transposes(b, i, first):
                    pe.wait_ge(xn_done, b + 1)
                    if not first:
                        pe.wait_ge(low_done, 2 * b)
                    for j in range(2):
                        for k in range(KT // 2):
                            c = j * 512 + k * P
                            t = nc.tensor.transpose(tp[j][:, k * P:(k + 1) * P], xn[i][:, c:c + P], g.ident[:])
                        t.then_inc(tp_done, 1)

                def project(b, i, first):
                    pe.wait_ge(low_done, 2 * (b + 1))
                    if not first:
                        pe.wait_ge(atab_done, b - 1)
                    if isinstance(b, int) and b == NB - 1:
                        pe.wait_ge(cnt_in, 1)
                        nc.tensor.matmul(cnt_ps, ones, counts[:], start=True, stop=True).then_inc(cnt_done, 1)
                    passes = [(w, s) for w, s in ((wh, xh), (wl, xh), (wh, xl))]
                    for n in range(3):
                        if isinstance(b, int) and b == 0:
                            pe.wait_ge(wa_done if n == 2 else wl_done, 1 if n == 2 else KT)
                        for m, (w, s) in enumerate(passes):
                            for k in range(KT):
                                t = nc.tensor.matmul(pp[i][:, n, 0:DG], s[i][:, k * P:(k + 1) * P],
                                                     w[:, k, n * DG:(n + 1) * DG], start=(m == 0 and k == 0),
                                                     stop=(m == len(passes) - 1 and k == KT - 1))
                    t.then_inc(pp_done, 1)

                def step(b, q, n, first):
                    if not (isinstance(b, int) and b == NB - 1):
                        transposes(b + 1, (q + 1) % 2, False)
                    project(b, q % 2, first and q < 2)
                transposes(0, 0, True)
                in_rings(pe, step)


BATCH = 4
RING = 7
PIECE = EC // RING


def stage_scores(nc, g):
    flat = g.big[:].rearrange("p b d -> p (b d)")
    used = [0]

    def piece(cols, d=F32):
        used[0] += cols
        assert used[0] <= NB * D
        return flat[:, used[0] - cols:used[0]].bitcast(d)

    with ExitStack() as ctx:
        sb = lambda n, s, d=F32: ctx.enter_context(nc.sbuf_tensor(n, s, d))
        ps = lambda n, s: ctx.enter_context(nc.psum_tensor(n, s, F32))
        low_t = sb("low_t", [PIECE * 2, 4, P], BF16)
        spread = [sb(f"spread{i}", [P, PIECE, P], BF16) for i in range(3)]
        part = [sb(f"table{i}", [P, NB, H], BF16) for i in range(3)]
        rest = sb("table_rest", [P, NB, H])
        hot = [sb(f"low_hot{i}", [P, BATCH, P], BF16) for i in range(2)]
        high = piece(EC * NB).rearrange("p (n b) -> p n b", b=NB)
        picked = [piece(BATCH * H * NB).rearrange("p (n b h) -> p n b h", b=NB, h=H) for _ in range(2)]
        zeros = piece(EC * 2 * H).rearrange("p (n r) -> p n r", r=2 * H)
        row2 = sb("fill_row2", [2 * H, 2, P])
        run, shifted = sb("fill_run", [2 * H, P]), sb("fill_shifted", [2 * H, P])
        ends = sb("fill_ends", [P, 2, 2 * H])
        carry = sb("fill_carry", [P, 2 * H])
        same, unseen = sb("same", [P, EC]), sb("unseen", [P, EC])
        pick_ps = [ps(f"pick_ps{i}", [P, BATCH, NB * H]) for i in range(2)]
        lps = ps("low_ps", [PIECE * 2, 4, P])
        tps = ps("fill_rows", [2 * H, 2, P])
        cps = ps("fill_cols", [P, 2 * H])
        part_i = sb("address_part", [P, EC], I32)
        src_lo, src_hi = sb("src_lo", [P, EC]), sb("src_hi", [P, EC])
        (own_dve, src_lo_done, lt_done, lt_copied, low_out, zero_done, zero_out, laid, laid_in, table_done, hot_done, pick_done,
         picked_done, edge_s_done, ends_in, ends_done, run_in, carry_done) = new_sems(
            nc, g.ctx, "scores_dve", "src_lo_done", "low_t_done", "low_t_copied", "low_out", "zero_done", "zero_out", "laid", "laid_in",
            "table_done", "low_hot_done", "pick_done", "picked_done", "edge_s_done", "ends_in", "ends_done", "run_in",
            "carry_done")
        spread_in = new_sems(nc, g.ctx, *[f"spread_in{i}" for i in range(3)])
        QC = EC // 4
        STEPS = PIECE // BATCH
        assert QC <= 2 * PIECE
        assert PIECE % BATCH == 0 and STEPS % 2 == 0
        with nc.Block() as block:
            @block.sync
            def _(sp):
                sp.wait_ge(zero_done, 1)
                sp.dma_start(g.laid.rearrange("(p n) r -> p n r", p=P), zeros).then_inc(zero_out, 16)
                sp.wait_ge(lt_copied, 1)
                sp.dma_start(g.low.rearrange("(t c) p -> c t p", t=4), low_t[0:QC, :, :]).then_inc(low_out, 16)
                sp.wait_ge(low_out, 16)
                for r in range(RING):
                    if r >= 3:
                        sp.wait_ge(hot_done, (r - 2) * STEPS)
                    if r == 5:
                        sp.wait_ge(laid, 16 * NB)
                        sp.dma_start(g.edge_d[:], g.laid.rearrange("(p n) r -> p n r", p=P)).then_inc(laid_in, 16)
                    sp.dma_start(spread[r % 3][:].rearrange("p n e -> p (n e)"),
                                 g.low[r * PIECE:(r + 1) * PIECE, :].rearrange("c p -> (c p)").unsqueeze(0)
                                 .broadcast_to([P, PIECE * P])).then_inc(spread_in[r % 3], 16)

            @block.gpsimd
            def _(pool):
                pool.wait_ge(zero_out, 16)
                for b in range(NB):
                    nc.gpsimd.indirect_dma_start(
                        g.laid[:, :], bass.IndirectOffsetOnAxis(g.start_i[:, b:b + 1], 0), g.atab[:, b, :], None,
                        bounds_check=NC * CH - 1, oob_is_err=False).then_inc(laid, 16)

            @block.vector
            def _(dve):
                v = nc.vector
                own = Links(dve, own_dve)
                v.memset(zeros, 0.0).then_inc(zero_done, 1)
                own.link(v.tensor_scalar(part_i[:], g.src_i[:], P - 1, None, ALU.bitwise_and))
                v.tensor_copy(src_lo[:], part_i[:]).then_inc(src_lo_done, 1)
                dve.wait_ge(src_lo_done, 1)
                own.link(v.tensor_scalar(part_i[:], g.src_i[:], P.bit_length() - 1, None, ALU.logical_shift_right))
                own.link(v.tensor_copy(src_hi[:], part_i[:]))
                dve.wait_ge(lt_done, 1)
                v.tensor_copy(low_t[0:QC, :, :], lps[0:QC, :, :]).then_inc(lt_copied, 1)
                own.link(v.tensor_copy(part[0][:], g.atab[:, :, 0:H]))
                own.link(v.tensor_tensor(rest[:], g.atab[:, :, 0:H], part[0][:], ALU.subtract))
                own.link(v.tensor_copy(part[1][:], rest[:]))
                own.link(v.tensor_tensor(rest[:], rest[:], part[1][:], ALU.subtract))
                v.tensor_copy(part[2][:], rest[:]).then_inc(table_done, 1)
                own.link(v.tensor_tensor(high, src_hi[:].unsqueeze(2).broadcast_to([P, EC, NB]),
                                         g.iota[:, 0:NB].unsqueeze(1).broadcast_to([P, EC, NB]), ALU.is_equal))

                def low_hot(s, i, ring, at, first):
                    if not first:
                        dve.wait_ge(pick_done, s - 1)
                    v.tensor_scalar(hot[i][:], spread[ring][:, bass.ds(at, BATCH), :], g.pcol[:], None,
                                    ALU.is_equal).then_inc(hot_done, 1)

                def pick(s, i, first=False):
                    dve.wait_ge(pick_done, s + 1)
                    if not first:
                        dve.wait_ge(edge_s_done, s - 1)
                    v.tensor_tensor(picked[i], pick_ps[i][:].rearrange("p n (b h) -> p n b h", h=H),
                                    high[:, bass.ds(s * BATCH, BATCH), :].unsqueeze(3).broadcast_to([P, BATCH, NB, H]),
                                    ALU.mult).then_inc(picked_done, 1)

                def total(s, i):
                    dve.wait_ge(picked_done, s + 1)
                    v.tensor_reduce(g.edge_s[:, bass.ds(s * BATCH, BATCH), :],
                                    picked[i].rearrange("p n b h -> p n h b"), AX.X, ALU.add).then_inc(edge_s_done, 1)

                for r in range(RING):
                    dve.wait_ge(spread_in[r % 3], 16 * (r // 3 + 1))
                    base = r * STEPS

                    def batch(s, i, at, late):
                        low_hot(s, i, r % 3, at, late < 2)
                        if late >= 1:
                            pick(s - 1, 1 - i, late < 3)
                        if late >= 2:
                            total(s - 2, i)
                    peeled = 4 if r == 0 else 0
                    for n in range(peeled):
                        batch(n, n % 2, n * BATCH, n)
                    with dve.Fori(peeled // 2, STEPS // 2) as n:
                        for i in range(2):
                            batch(n * 2 + (base + i), i, n * (2 * BATCH) + i * BATCH, 4)
                S = RING * STEPS
                pick(S - 1, 1)
                total(S - 2, 0)
                total(S - 1, 1)
                dve.wait_ge(laid_in, 16)
                own.link(v.tensor_scalar(same[:], g.first[:], -1.0, 1.0, ALU.mult, ALU.add))
                own.add(v.tensor_tensor_scan(unseen[:], same[:], same[:], 1.0, ALU.mult, ALU.min))
                for r in range(2 * H):
                    own.add(v.tensor_tensor_scan(g.edge_d[:, :, r], same[:], g.edge_d[:, :, r], 0.0, ALU.mult, ALU.add))
                own.wait()
                own.add(v.tensor_copy(ends[:, 0, :], g.edge_d[:, EC - 1, :]))
                own.link(v.tensor_copy(ends[:, 1, :], unseen[:, EC - 1:EC].broadcast_to([P, 2 * H])))
                v.engine_nop().then_inc(ends_in, 1)
                dve.wait_ge(ends_done, 1)
                own.link(v.tensor_copy(row2[:], tps[:]))
                own.add(v.memset(shifted[:], 0.0))
                own.link(v.tensor_tensor_scan(run[:], row2[:, 1, :], row2[:, 0, :], 0.0, ALU.mult, ALU.add))
                own.link(v.tensor_copy(shifted[:, 1:P], run[:, 0:P - 1]))
                v.engine_nop().then_inc(run_in, 1)
                dve.wait_ge(carry_done, 1)
                own.link(v.tensor_copy(carry[:], cps[:]))
                for r in range(2 * H):
                    own.add(v.scalar_tensor_tensor(out=g.edge_d[:, :, r], in0=unseen[:], scalar=carry[:, r:r + 1],
                                                   in1=g.edge_d[:, :, r], op0=ALU.mult, op1=ALU.add))
                own.wait()

            @block.tensor
            def _(pe):
                pe.wait_ge(src_lo_done, 1)
                for t in range(4):
                    m = nc.tensor.transpose(lps[0:QC, t, :], src_lo[:, t * QC:(t + 1) * QC], g.ident[:])
                m.then_inc(lt_done, 1)
                pe.wait_ge(table_done, 1)

                def pick(s, i, first):
                    pe.wait_ge(hot_done, s + 1)
                    if not first:
                        pe.wait_ge(picked_done, s - 1)
                    for c in range(BATCH):
                        for k in range(3):
                            m = nc.tensor.matmul(pick_ps[i][:, c, :], hot[i][:, c, :],
                                                 part[k][:].rearrange("p b h -> p (b h)"), start=(k == 0), stop=(k == 2))
                    m.then_inc(pick_done, 1)
                for i in range(2):
                    pick(i, i, True)
                with pe.Fori(1, RING * STEPS // 2) as n:
                    for i in range(2):
                        pick(n * 2 + i, i, False)
                pe.wait_ge(ends_in, 1)
                nc.tensor.transpose(tps[:, 0, :], ends[:, 0, :], g.ident[:])
                nc.tensor.transpose(tps[:, 1, :], ends[:, 1, :], g.ident[:]).then_inc(ends_done, 1)
                pe.wait_ge(run_in, 1)
                nc.tensor.transpose(cps[:], shifted[:], g.ident[0:2 * H, 0:2 * H]).then_inc(carry_done, 1)


def stage_weights(nc, g):
    with ExitStack() as ctx:
        sb = lambda n, s, d=F32: ctx.enter_context(nc.sbuf_tensor(n, s, d))
        ps = lambda n, s: ctx.enter_context(nc.psum_tensor(n, s, F32))
        rec = sb("rec_all", [P, EC, REC])
        first, last = g.first, g.last
        nf, nl, seen_f, seen_l = (sb(n, [P, EC]) for n in ("nf", "nl", "seen_f", "seen_l"))
        fmax, bmax = sb("fmax", [P, EC, H]), sb("bmax", [P, EC, H])
        mw, sw = sb("mw", [P, EC, H]), sb("sw", [P, EC, H])
        ew = fmax
        tail4 = sb("tail4", [P, 2, H])
        rowt = sb("rowt", [H, 2, P])
        run = sb("run", [H, P])
        shifted = sb("shifted", [H, P])
        carry = sb("carry", [P, 2, H])
        tps = [ps(f"row_ps{i}", [P, 2, P]) for i in range(2)]
        cps = [ps(f"col_ps{i}", [P, H]) for i in range(2)]
        own_dve, t_in, t_done, r_in, c_done, e_in, e_done, rec_done, rec_out, zeroed = new_sems(
            nc, g.ctx, "weights_dve", "tails_in", "tails_done", "runs_in", "carried_back",
            "exps_in", "exps_done", "rec_done", "rec_out", "acc_zeroed")
        rec_halves = [(0, EC // 2), (EC // 2, EC)]
        a_s, d_s, d_d = g.edge_s[:], g.edge_d[:, :, 0:H], g.edge_d[:, :, H:2 * H]
        with nc.Block() as block:
            @block.vector
            def _(dve):
                own = Links(dve, own_dve)
                v = nc.vector
                cur = g.dst_f[:, 1:EC + 1]
                own.add(v.tensor_scalar(nf[:], first[:], NEG, None, ALU.mult))
                own.add(v.tensor_scalar(nl[:], last[:], NEG, None, ALU.mult))
                own.add(v.tensor_tensor_scan(seen_f[:], first[:], first[:], 0.0, ALU.max, ALU.max))
                own.add(v.tensor_tensor_scan(seen_l[:, ::-1], last[:, ::-1], last[:, ::-1], 0.0, ALU.max, ALU.max))
                own.wait()
                own.add(v.tensor_scalar(seen_f[:], seen_f[:], NEG, None, ALU.mult))
                own.add(v.tensor_scalar(seen_l[:], seen_l[:], NEG, None, ALU.mult))
                own.wait()

                def carried(n, out, inp, seg, seen, tail, back):
                    rev = slice(None, None, -1) if back else slice(None)
                    for h in range(H):
                        own.add(v.tensor_tensor_scan(out[:, rev, h], seg[:, rev], inp[:, rev, h], NEG, ALU.add, ALU.max))
                    own.wait()
                    own.add(v.tensor_copy(tail4[:, 0, :], out[:, tail, :]))
                    own.link(v.tensor_copy(tail4[:, 1, :], seen[:, tail:tail + 1].broadcast_to([P, H])))
                    v.engine_nop().then_inc(t_in, 1)
                    dve.wait_ge(t_done, n + 1)
                    own.link(v.tensor_copy(rowt[:], tps[n][0:H, :, :]))
                    own.add(v.memset(shifted[:], NEG))
                    own.link(v.tensor_tensor_scan(run[:, rev], rowt[:, 1, rev], rowt[:, 0, rev], NEG, ALU.add, ALU.max))
                    if back:
                        own.link(v.tensor_copy(shifted[:, 0:P - 1], run[:, 1:P]))
                    else:
                        own.link(v.tensor_copy(shifted[:, 1:P], run[:, 0:P - 1]))
                    v.engine_nop().then_inc(r_in, 1)
                    dve.wait_ge(c_done, n + 1)
                    own.link(v.tensor_copy(carry[:, n, :], cps[n][:]))
                    for h in range(H):
                        own.add(v.scalar_tensor_tensor(out=out[:, :, h], in0=seen[:], scalar=carry[:, n, h:h + 1],
                                                       in1=out[:, :, h], op0=ALU.add, op1=ALU.max))
                    own.wait()

                carried(0, fmax, a_s, nf, seen_f, EC - 1, False)
                carried(1, bmax, fmax, nl, seen_l, 0, True)
                own.add(v.tensor_tensor(mw[:], bmax[:], d_s, ALU.max))
                own.add(v.tensor_tensor(ew[:], a_s, d_d, ALU.add))
                own.add(v.tensor_tensor(sw[:], d_s, d_d, ALU.add))
                own.wait()
                own.link(v.tensor_tensor(mw[:], mw[:], d_d, ALU.add))
                for t in (mw, ew, sw):
                    own.add(v.scalar_tensor_tensor(out=t[:], in0=t[:], scalar=SLOPE, in1=t[:], op0=ALU.mult, op1=ALU.max))
                own.wait()
                own.add(v.tensor_tensor(ew[:], ew[:], mw[:], ALU.subtract))
                own.link(v.tensor_tensor(sw[:], sw[:], mw[:], ALU.subtract))
                v.engine_nop().then_inc(e_in, 1)
                summed = rec[:, :, SUMMED_AT:SUMMED_AT + SUMMED // 2].bitcast(BF16)
                own.add(v.tensor_copy(summed[:, :, FIRST_AT:FIRST_AT + 1], first[:].unsqueeze(2)))
                own.add(v.memset(summed[:, :, FIRST_AT + 1:FIRST_AT + 2], 0.0))
                own.add(v.tensor_copy(rec[:, :, DST_AT:DST_AT + 1], cur.unsqueeze(2)))
                own.add(v.memset(rec[:, :, SUMMED_AT + SUMMED // 2:REC], 0.0))
                own.add(v.tensor_copy(rec[:, :, SRC_AT:SRC_AT + 1].bitcast(I32), g.src_i[:].unsqueeze(2)))
                dve.wait_ge(e_done, 2)
                own.add(v.tensor_tensor(sw[:], sw[:], first[:].unsqueeze(2).broadcast_to([P, EC, H]), ALU.mult))
                own.link(v.tensor_copy(ew[:], rec[:, :, W_AT:W_AT + H]))
                for a, b in rec_halves:
                    for n in range(PARTS):
                        parts = [summed[:, a:b, at + n * H:at + (n + 1) * H] for at in (0, SELF_AT)]
                        for t, part in zip((ew, sw), parts):
                            own.add(v.tensor_copy(part, t[:, a:b, :]))
                        own.wait()
                        if n < PARTS - 1:
                            for t, part in zip((ew, sw), parts):
                                own.add(v.tensor_tensor(t[:, a:b, :], t[:, a:b, :], part, ALU.subtract))
                            own.wait()
                    v.engine_nop().then_inc(rec_done, 1)

            @block.gpsimd
            def _(pool):
                nc.gpsimd.memset(g.acc_side[:], 0.0).then_inc(zeroed, 1)
                nc.gpsimd.memset(g.big[:], 0.0).then_inc(zeroed, 1)
                pool.wait_ge(zeroed, 2)

            @block.scalar
            def _(act):
                act.wait_ge(e_in, 1)
                nc.scalar.activation(rec[:, :, W_AT:W_AT + H], ew[:], ACT.Exp).then_inc(e_done, 1)
                nc.scalar.activation(sw[:], sw[:], ACT.Exp).then_inc(e_done, 1)

            @block.tensor
            def _(pe):
                for n in range(2):
                    pe.wait_ge(t_in, n + 1)
                    nc.tensor.transpose(tps[n][0:H, 0, :], tail4[:, 0, :], g.ident[:])
                    nc.tensor.transpose(tps[n][0:H, 1, :], tail4[:, 1, :], g.ident[:]).then_inc(t_done, 1)
                    pe.wait_ge(r_in, n + 1)
                    nc.tensor.transpose(cps[n][:], shifted[:], g.ident[0:H, 0:H]).then_inc(c_done, 1)

            @block.sync
            def _(sp):
                sp.wait_ge(e_done, 2)
                for n, (a, b) in enumerate(rec_halves):
                    sp.wait_ge(rec_done, n + 1)
                    sp.dma_start(g.rec.rearrange("(p n) r -> p n r", p=P)[:, a:b, :], rec[:, a:b, :]).then_inc(rec_out, 16)
                sp.wait_ge(rec_out, 16 * len(rec_halves))


GB = 4


HB = 4
LAG = 2


def stage_messages(nc, g):
    with ExitStack() as ctx:
        sb = lambda n, s, d=F32: ctx.enter_context(nc.sbuf_tensor(n, s, d))
        ps = lambda n, s: ctx.enter_context(nc.psum_tensor(n, s, F32))
        rec = [sb(f"rec{q}", [P, SUB, REC]) for q in range(GB)]
        got = [sb(f"rows{q}", [P, SUB, D]) for q in range(GB)]
        one = [sb(f"one{i}", [P, SUB, P], BF16) for i in range(HB)]
        hot = [sb(f"hot{i}", [P, SUB, H, P]) for i in range(HB)]
        msg = [ps(f"msg{i}", [P, D]) for i in range(2)]
        side = [ps(f"side{i}", [P, SUMMED]) for i in range(2)]
        rec_in = new_sems(nc, g.ctx, *[f"rec_in{q}" for q in range(GB)])
        got_in = new_sems(nc, g.ctx, *[f"rows_in{q}" for q in range(GB)])
        one_done, hot_done, sums_done, added, gated = new_sems(
            nc, g.ctx, "one_done", "hot_done", "sums_done", "added", "messages_gated")
        assert ITEMS % GB == 0 and GB % HB == 0
        turns = ITEMS // GB

        def each(eng, body):
            for q in range(GB):
                body(q, 0, q, True)
            with eng.Fori(1, turns) as t:
                for q in range(GB):
                    body(t * GB + q, t, q, False)

        with nc.Block() as block:
            @block.sync
            def _(sp):
                def load(i, t, q, first):
                    c = sp.value_load(g.chk_i[0:1, bass.ds(i, 1)], min_val=0, max_val=NC - 1)
                    if not first:
                        sp.wait_ge(sums_done, i - GB + 1)
                    sp.dma_start(rec[q][:], g.rec[bass.ds(c * CH, CH), :].rearrange("(p k) r -> p k r", k=SUB)).then_inc(rec_in[q], 16)
                each(sp, load)

            @block.gpsimd
            def _(pool):
                nc.gpsimd.memset(g.gate[0:1, 1:2], 0.0).then_inc(gated, 1)

                def gather(i, t, q, first):
                    if not first:
                        pool.wait_ge(sums_done, i - GB + 1)
                    pool.wait_ge(rec_in[q], 16 * (t + 1))
                    gate(nc, g, gated, i)
                    for k in range(SUB):
                        nc.gpsimd.indirect_dma_start(
                            got[q][:, k, :], None, g.xp[:, :],
                            bass.IndirectOffsetOnAxis(rec[q][:, k, SRC_AT:SRC_AT + 1].bitcast(I32), 0)).then_inc(got_in[q], 16)
                each(pool, gather)

            @block.scalar
            def _(act):
                def weights(i, t, q, first):
                    if not (first and q < HB):
                        act.wait_ge(sums_done, i - HB + 1)
                    for k in range(SUB):
                        act.wait_ge(one_done, SUB * i + k + 1)
                        for h in range(H):
                            ins = nc.scalar.activation(hot[q % HB][:, k, h, :], one[q % HB][:, k, :], ACT.Copy,
                                                       scale=rec[q][:, k, h:h + 1])
                    ins.then_inc(hot_done, 1)
                each(act, weights)

            @block.vector
            def _(dve):
                def weigh(i, t, q, first):
                    b = dve.value_load(g.blk_i[0:1, bass.ds(i, 1)], min_val=0, max_val=NB - 1)
                    nodes = g.iota[:, bass.ds(b * P, P)]
                    dve.wait_ge(rec_in[q], 16 * (t + 1))
                    if not (first and q < HB):
                        dve.wait_ge(sums_done, i - HB + 1)
                    for k in range(SUB):
                        nc.vector.tensor_scalar(one[q % HB][:, k, :], nodes, rec[q][:, k, DST_AT:DST_AT + 1], None,
                                                ALU.is_equal).then_inc(one_done, 1)

                def add(i, q, first):
                    b = dve.value_load(g.blk_i[0:1, bass.ds(i, 1)], min_val=0, max_val=NB - 1)
                    dve.wait_ge(sums_done, i + 1)
                    if not first:
                        dve.wait_ge(added, 2 * i)
                    at = g.big[:, bass.ds(b, 1), :].rearrange("p a n -> p (a n)")
                    nc.vector.tensor_tensor(at, at, msg[q % 2][:], ALU.add).then_inc(added, 1)
                    at = g.acc_side[:, bass.ds(b, 1), :].rearrange("p a n -> p (a n)")
                    nc.vector.tensor_tensor(at, at, side[q % 2][:], ALU.add).then_inc(added, 1)

                def step(i, t, q, first):
                    weigh(i, t, q, first)
                    if not (first and q < LAG):
                        add(i - LAG, (q - LAG) % GB, first and q == LAG)
                each(dve, step)
                for q in range(GB - LAG, GB):
                    add(ITEMS - GB + q, q, False)

            @block.tensor
            def _(pe):
                def sums(i, t, q, first):
                    pe.wait_ge(hot_done, i + 1)
                    pe.wait_ge(got_in[q], 16 * SUB * (t + 1))
                    if not (first and q < 2):
                        pe.wait_ge(added, 2 * (i - 1))
                    for h in range(H):
                        for k in range(SUB):
                            nc.tensor.matmul(msg[q % 2][:, h * C:(h + 1) * C], hot[q % HB][:, k, h, :],
                                             got[q][:, k, h * C:(h + 1) * C], start=(k == 0), stop=(k == SUB - 1))
                    for k in range(SUB):
                        t_ = nc.tensor.matmul(side[q % 2][:], one[q % HB][:, k, :],
                                              rec[q][:, k, SUMMED_AT:SUMMED_AT + SUMMED // 2].bitcast(BF16),
                                              start=(k == 0), stop=(k == SUB - 1))
                    t_.then_inc(sums_done, 1)
                each(pe, sums)


RR = 6


def stage_residual(nc, g, x, bias, gate_w):
    with ExitStack() as ctx:
        sb = lambda n, s, d=F32: ctx.enter_context(nc.sbuf_tensor(n, s, d))
        ps = lambda n, s: ctx.enter_context(nc.psum_tensor(n, s, F32))
        ring = lambda n, s: [sb(f"{n}{i}", s) for i in range(RR)]
        xr, xn = ring("r_x", [P, D]), ring("r_xn", [P, D])
        xt = [sb(f"r_xt{i}", [P, D]) for i in range(2)]
        bias_b = sb("bias_b", [P, D])
        gw = sb("gate_rows", [X, D])
        gwt = sb("gate_t", [P, KT, X])
        wself, rz = sb("wself", [P, NB, H]), sb("rz", [P, NB, H])
        stats, mv, std, rstd, shift = (ring(n, [P, k]) for n, k in
                                       (("r_stats", 12), ("r_mv", 2), ("r_std", 1), ("r_rstd", 1), ("r_shift", 1)))
        eps = sb("r_eps", [P, 1])
        top, tot = sb("r_top", [P, NB]), sb("r_tot", [P, NB])
        tp = [ps(f"r_tp{i}", [P, D]) for i in range(2)]
        sp_ = [ps(f"r_sc{i}", [P, X]) for i in range(2)]
        gp = ps("gate_ps", [P, KT, X])
        (cons_in, own_dve, gp_done, gwt_done, own_added, msg_done, relu_done, x1_done, stats_done, var_done, std_done,
         rstd_done, shift_done, xn_done, tp_done, xt_done, sc_done, sc_copied, soft_in, soft_done) = new_sems(
            nc, g.ctx, "r_consts_in", "residual_dve", "gate_ps_done", "gate_t_done", "r_own_added", "r_msg_done",
            "r_relu_done", "x1_done", "r_stats_done", "r_var_done", "r_std_done", "r_rstd_done", "r_shift_done",
            "r_xn_done", "r_tp_done", "r_xt_done", "r_sc_done", "r_sc_copied", "soft_in", "soft_done")
        loaded = new_sems(nc, g.ctx, *[f"r_in{i}" for i in range(RR)])
        stored = new_sems(nc, g.ctx, *[f"r_out{i}" for i in range(RR)])

        def each(eng, *parts):
            deepest = max(lag for lag, _ in parts)

            def step(s, q, n, known):
                for lag, part in parts:
                    if not known or 0 <= s - lag < NB:
                        part(s - lag, (q - lag) % RR, n + 1 + (q - lag) // RR)
            for s in range(RR):
                step(s, s, 0, True)
            with eng.Fori(1, NB // RR) as n:
                for q in range(RR):
                    step(n * RR + q, q, n, False)
            for s in range(NB // RR * RR, NB + deepest):
                step(s, s % RR, s // RR, True)

        def x1(b):
            return g.big[:, bass.ds(b, 1), :].rearrange("p a n -> p (a n)")

        def is_first(b, k):
            return isinstance(b, int) and b < k

        def size(b):
            return LAST if isinstance(b, int) and b == NB - 1 else P

        with nc.Block() as block:
            @block.sync
            def _(sp):
                sp.dma_start(gw[:], gate_w).then_inc(cons_in, 16)
                sp.dma_start(bias_b[:], bias.unsqueeze(0).broadcast_to([P, D])).then_inc(cons_in, 16)

                def load(b, r, turns):
                    if not is_first(b, RR):
                        sp.wait_ge(stored[r], 16 * (turns - 1))
                        sp.wait_ge(tp_done, b - RR + 1)
                    k = size(b)
                    sp.dma_start(xr[r][0:k, :], x[bass.ds(b * P, k), :]).then_inc(loaded[r], 16)
                    sp.dma_start(xn[r][:], g.xp[bass.ds(b * P, P), :]).then_inc(loaded[r], 16)

                def store(b, r, turns):
                    k = size(b)
                    sp.wait_ge(xn_done, b + 1)
                    sp.dma_start(g.xn1[bass.ds(b * P, k), :], xn[r][0:k, :]).then_inc(stored[r], 16)
                each(sp, (0, load), (4, store))
                for r in range(RR):
                    sp.wait_ge(stored[r], 16 * ((NB - 1 - r) // RR + 1))

            @block.gpsimd
            def _(pool):
                def add_x(b, r, turns):
                    pool.wait_ge(relu_done, b + 1)
                    nc.gpsimd.tensor_tensor(x1(b), xn[r][:], xr[r][:], ALU.add).then_inc(x1_done, 1)
                each(pool, (0, add_x))

            @block.vector
            def _(dve):
                v = nc.vector
                own = Links(dve, own_dve)
                own.add(v.memset(eps[:], EPS))
                have = g.acc_side[:, :, FIRST_AT:FIRST_AT + 1].broadcast_to([P, NB, H])
                for t, at in ((rz, 0), (wself, SELF_AT)):
                    part = [g.acc_side[:, :, at + n * H:at + (n + 1) * H] for n in range(PARTS)]
                    own.link(v.tensor_tensor(t[:], part[2], part[1], ALU.add))
                    own.link(v.tensor_tensor(t[:], t[:], part[0], ALU.add))
                own.link(v.tensor_tensor(wself[:], wself[:], have, ALU.subtract))
                own.link(v.tensor_scalar(wself[:], wself[:], 1.0, None, ALU.add))
                own.link(v.tensor_tensor(rz[:], rz[:], wself[:], ALU.add))
                own.link(v.reciprocal(rz[:], rz[:]))
                dve.wait_ge(gp_done, 1)
                v.tensor_copy(gwt[:], gp[:]).then_inc(gwt_done, 1)
                dve.wait_ge(cons_in, 32)

                def messages(b, r, turns):
                    dve.wait_ge(loaded[r], 32 * turns)
                    acc = x1(b)
                    own_w = wself[:, bass.ds(b, 1), :].rearrange("p a n -> p (a n)")
                    inv = rz[:, bass.ds(b, 1), :].rearrange("p a n -> p (a n)")
                    for h in range(H):
                        c = slice(h * C, (h + 1) * C)
                        ins = v.scalar_tensor_tensor(out=xn[r][:, c], in0=xn[r][:, c], scalar=own_w[:, h:h + 1],
                                                     in1=acc[:, c], op0=ALU.mult, op1=ALU.add)
                    ins.then_inc(own_added, 1)
                    dve.wait_ge(own_added, b + 1)
                    for h in range(H):
                        c = slice(h * C, (h + 1) * C)
                        ins = v.scalar_tensor_tensor(out=xn[r][:, c], in0=xn[r][:, c], scalar=inv[:, h:h + 1],
                                                     in1=bias_b[:, c], op0=ALU.mult, op1=ALU.add)
                    ins.then_inc(msg_done, 1)

                def statistics(b, r, turns):
                    v.bn_stats(stats[r][:, 0:6], x1(b)[:, 0:512]).then_inc(stats_done, 1)
                    v.bn_stats(stats[r][:, 6:12], x1(b)[:, 512:1024]).then_inc(stats_done, 1)

                def whole(b, r, turns):
                    dve.wait_ge(x1_done, b + 1)

                def taken(b, r, turns):
                    dve.wait_ge(stats_done, 2 * (b + 1))

                def copy_scores(b, r, turns):
                    dve.wait_ge(sc_done, b + 1)
                    v.tensor_copy(g.prob[:, bass.ds(b, 1), :].rearrange("p a n -> p (a n)"), sp_[r % 2][:]).then_inc(sc_copied, 1)

                def variance(b, r, turns):
                    v.bn_aggr(mv[r][:], stats[r][:]).then_inc(var_done, 1)

                def scale(b, r, turns):
                    dve.wait_ge(std_done, b + 1)
                    v.reciprocal(rstd[r][:], std[r][:]).then_inc(rstd_done, 1)
                    dve.wait_ge(rstd_done, b + 1)
                    v.scalar_tensor_tensor(out=shift[r][:], in0=mv[r][:, 0:1], scalar=-1.0, in1=rstd[r][:],
                                           op0=ALU.mult, op1=ALU.mult).then_inc(shift_done, 1)

                each(dve, (0, messages), (1, whole), (5, copy_scores), (1, statistics), (1, taken), (2, scale), (1, variance))
                dve.wait_ge(sc_copied, NB)
                wide = lambda a: a[:].unsqueeze(2).broadcast_to([P, NB, X])
                own.link(v.tensor_reduce(top[:], g.prob[:], AX.X, ALU.max))
                own.link(v.tensor_tensor(g.prob[:], g.prob[:], wide(top), ALU.subtract))
                v.tensor_copy(top[:], top[:]).then_inc(soft_in, 1)
                dve.wait_ge(soft_done, 1)
                own.link(v.tensor_reduce(tot[:], g.prob[:], AX.X, ALU.add))
                own.link(v.reciprocal(tot[:], tot[:]))
                own.link(v.tensor_tensor(g.prob[:], g.prob[:], wide(tot), ALU.mult))

            @block.scalar
            def _(act):
                def relu(b, r, turns):
                    act.wait_ge(msg_done, b + 1)
                    nc.scalar.activation(xn[r][:], xn[r][:], ACT.Relu).then_inc(relu_done, 1)

                def deviation(b, r, turns):
                    act.wait_ge(var_done, b + 1)
                    nc.scalar.activation(std[r][:], mv[r][:, 1:2], ACT.Sqrt, bias=eps[:]).then_inc(std_done, 1)

                def normalise(b, r, turns):
                    act.wait_ge(shift_done, b + 1)
                    nc.scalar.activation(xn[r][:], x1(b), ACT.Identity, bias=shift[r][:], scale=rstd[r][:]).then_inc(xn_done, 1)

                def evacuate(b, r, turns):
                    act.wait_ge(tp_done, b + 1)
                    if not is_first(b, 2):
                        act.wait_ge(sc_done, b - 1)
                    nc.scalar.copy(xt[r % 2][:], tp[r % 2][:]).then_inc(xt_done, 1)
                each(act, (0, relu), (1, deviation), (2, normalise), (3, evacuate))
                act.wait_ge(soft_in, 1)
                nc.scalar.activation(g.prob[:], g.prob[:], ACT.Exp).then_inc(soft_done, 1)

            @block.tensor
            def _(pe):
                pe.wait_ge(cons_in, 32)
                for k in range(KT):
                    m = nc.tensor.transpose(gp[:, k, :], gw[:, k * P:(k + 1) * P], g.ident[0:X, 0:X])
                m.then_inc(gp_done, 1)
                pe.wait_ge(gwt_done, 1)

                def transposes(b, r, turns):
                    pe.wait_ge(xn_done, b + 1)
                    if not is_first(b, 2):
                        pe.wait_ge(xt_done, b - 1)
                    for k in range(KT):
                        m = nc.tensor.transpose(tp[r % 2][:, k * P:(k + 1) * P], xn[r][:, k * P:(k + 1) * P], g.ident[:])
                    m.then_inc(tp_done, 1)

                def scores(b, r, turns):
                    pe.wait_ge(xt_done, b + 1)
                    if not is_first(b, 2):
                        pe.wait_ge(sc_copied, b - 1)
                    for k in range(KT):
                        m = nc.tensor.matmul(sp_[r % 2][:], xt[r % 2][:, k * P:(k + 1) * P], gwt[:, k, :],
                                             start=(k == 0), stop=(k == KT - 1))
                    m.then_inc(sc_done, 1)
                each(pe, (0, transposes), (1, scores))


SHIFTS = list(range(28, -1, -4))


def stage_select(nc, g, out):
    with ExitStack() as ctx:
        sb = lambda n, s, d=F32: ctx.enter_context(nc.sbuf_tensor(n, s, d))
        ps = lambda n, s: ctx.enter_context(nc.psum_tensor(n, s, F32))
        tid, valid = sb("tid", [P, NB]), sb("valid", [P, NB])
        rep = sb("rep", [P, NB, X, REP])
        prow, over, tie, rank = (sb(n, [P, NP]) for n in ("prow", "over", "tie", "rank"))
        pi, ji, pf = sb("sel_pi", [P, 1], I32), sb("sel_ji", [P, 1], I32), sb("sel_pf", [P, 1])
        steps = sb("sel_steps", [P, len(SHIFTS)], I32)
        gi, gf, same = sb("sel_gi", [P, P], I32), sb("sel_gf", [P, P]), sb("sel_same", [P, P])
        found, trial, dig = (sb(n, [P, 1], I32) for n in ("sel_found", "sel_trial", "sel_dig"))
        cnt, enough, digf = (sb(n, [P, 1]) for n in ("sel_cnt", "sel_enough", "sel_digf"))
        slot, slot_i = sb("slot", [P, NB, X]), sb("slot_i", [P, NB, X], I32)
        lo_i, hi_i = sb("lo_i", [P, NB, X], I32), sb("hi_i", [P, NB, X], I32)
        lo, hi = sb("lo", [P, NB, X]), sb("hi", [P, NB, X])
        VALS = 2 + PARTS
        val = sb("val", [P, NB * X, VALS, ST], BF16)
        mask = over[:, 0:NB * X * ST].rearrange("p (n t) -> p n t", t=ST)
        left = over[:, NB * X * ST:NB * X * (ST + 1)].rearrange("p (b x) -> p b x", x=X)
        value16 = over[:, NB * X * (ST + 1):NB * X * (ST + 1) + NB * X // 2].bitcast(BF16).rearrange("p (b x) -> p b x", x=X)
        assert NB * X * (ST + 2) <= NP
        tok = [sb(f"tok{i}", [P, 1, ST]) for i in range(2)]
        parts = [sb(f"tok_parts{i}", [P, VALS, ST]) for i in range(2)]
        lo_hot = [t[:, 0:NP // 2].bitcast(BF16).rearrange("p (b n) -> p b n", b=NB) for t in (prow, tie)]
        tp = [ps(f"sel_tp{i}", [P, 512]) for i in range(2)]
        vp = ps("sel_votes", [P, 1])
        lp = [ps(f"sel_list{i}", [P, VALS, ST]) for i in range(2)]
        x1_out, own_dve, rep_done, tp_done, tp_copied, votes_in, votes_done, slot_done, hot_done, list_done, list_copied = new_sems(
            nc, g.ctx, "x1_out", "select_dve", "rep_done", "sel_tp_done", "sel_tp_copied", "votes_in", "votes_done", "slots_done",
            "lo_hot_done", "list_done", "list_copied")
        groups = [(n, min(4, NB - n)) for n in range(0, NB, 4)]
        with nc.Block() as block:
            @block.sync
            def _(sp):
                sp.dma_start(out[0:(NB - 1) * P, :].rearrange("(b p) d -> p b d", p=P), g.big[:, 0:NB - 1, :]).then_inc(x1_out, 16)
                sp.dma_start(out[(NB - 1) * P:N, :], g.big[0:LAST, NB - 1, :]).then_inc(x1_out, 16)
                sp.wait_ge(x1_out, 32)

            @block.vector
            def _(dve):
                v = nc.vector
                own = Links(dve, own_dve)
                own.link(v.tensor_scalar(tid[:], g.iota[:, 0:NB], float(P), g.pcol[:], ALU.mult, ALU.add))
                own.link(v.tensor_scalar(valid[:], tid[:], float(N), None, ALU.is_lt))
                wide = lambda a: a[:].unsqueeze(2).broadcast_to([P, NB, X])
                own.link(v.tensor_tensor(g.prob[:], g.prob[:], wide(valid), ALU.mult))
                own.link(v.tensor_scalar(valid[:], valid[:], -1.0, None, ALU.add))
                own.link(v.tensor_tensor(g.prob[:], g.prob[:], wide(valid), ALU.add))
                own.link(v.tensor_copy(rep[:], g.prob[:].unsqueeze(3).broadcast_to([P, NB, X, REP])))
                v.engine_nop().then_inc(rep_done, 1)
                own.link(v.tensor_copy(pi[:], g.pcol[:]))
                own.link(v.tensor_scalar(ji[:], pi[:], REP - 1, None, ALU.bitwise_and))
                for n, s in enumerate(SHIFTS):
                    if n == 0:
                        own.link(v.tensor_scalar(steps[:, 0:1], ji[:], 3, s, ALU.bitwise_and, ALU.logical_shift_left))
                    else:
                        own.link(v.tensor_scalar(steps[:, n:n + 1], ji[:], s, None, ALU.logical_shift_left))
                own.link(v.tensor_scalar(pi[:], pi[:], REP.bit_length() - 1, None, ALU.logical_shift_right))
                own.link(v.tensor_copy(pf[:], pi[:]))
                own.link(v.tensor_copy(gi[:], g.iota[:, 0:P]))
                own.link(v.tensor_scalar(gi[:], gi[:], REP.bit_length() - 1, None, ALU.logical_shift_right))
                own.link(v.tensor_copy(gf[:], gi[:]))
                own.link(v.tensor_scalar(same[:], gf[:], pf[:], None, ALU.is_equal))
                own.link(v.memset(found[:], 0))

                for n, (b, k) in enumerate(groups):
                    dve.wait_ge(tp_done, n + 1)
                    v.tensor_copy(prow[:, b * P:(b + k) * P], tp[n % 2][:, 0:k * P]).then_inc(tp_copied, 1)
                dve.wait_ge(tp_copied, len(groups))

                for n, s in enumerate(SHIFTS):
                    own.link(v.tensor_tensor(trial[:], found[:], steps[:, n:n + 1], ALU.bitwise_or))
                    own.link(v.tensor_scalar(rank[:], prow[:], trial[:].bitcast(F32), None, ALU.is_ge, ALU.add, accum_out=cnt[:]))
                    own.link(v.tensor_scalar(enough[:], cnt[:], float(TOPK), None, ALU.is_ge))
                    v.engine_nop().then_inc(votes_in, 1)
                    dve.wait_ge(votes_done, n + 1)
                    own.link(v.tensor_scalar(digf[:], vp[:], 0.25 if n == 0 else 1.0, -1.0, ALU.mult, ALU.add))
                    own.link(v.tensor_copy(dig[:], digf[:]))
                    own.link(v.tensor_scalar(dig[:], dig[:], s, None, ALU.logical_shift_left))
                    own.link(v.tensor_tensor(found[:], found[:], dig[:], ALU.bitwise_or))

                thr = found[:].bitcast(F32)
                own.link(v.tensor_scalar(over[:], prow[:], thr, None, ALU.is_gt, ALU.add, accum_out=cnt[:]))
                own.add(v.tensor_scalar(cnt[:], cnt[:], -1.0, float(TOPK), ALU.mult, ALU.add))
                own.link(v.tensor_scalar(tie[:], prow[:], thr, None, ALU.is_equal))
                own.link(v.tensor_tensor_scan(rank[:], tie[:], tie[:], 0.0, ALU.add, ALU.max))
                own.link(v.scalar_tensor_tensor(out=tie[:], in0=rank[:], scalar=cnt[:], in1=tie[:], op0=ALU.is_le, op1=ALU.mult))
                own.link(v.tensor_tensor(over[:], over[:], tie[:], ALU.add))
                own.link(v.tensor_tensor_scan(rank[:], over[:], over[:], 0.0, ALU.add, ALU.max))
                own.link(v.tensor_tensor(rank[:], rank[:], over[:], ALU.mult))
                own.link(v.tensor_scalar(rank[:], rank[:], -1.0, None, ALU.add))
                v.engine_nop().then_inc(slot_done, 1)
                for n, (b, k) in enumerate(groups):
                    n += len(groups)
                    dve.wait_ge(tp_done, n + 1)
                    view = tp[n % 2][:, 0:k * P].rearrange("p (b x r) -> p b x r", x=X, r=REP)[:, :, :, 0]
                    v.tensor_copy(slot[:, b:b + k, :], view).then_inc(tp_copied, 1)
                dve.wait_ge(tp_copied, 2 * len(groups))
                own.link(v.tensor_copy(slot_i[:], slot[:]))
                own.add(v.tensor_scalar(lo_i[:], slot_i[:], P - 1, None, ALU.bitwise_and))
                own.link(v.tensor_scalar(hi_i[:], slot_i[:], P.bit_length() - 1, None, ALU.arith_shift_right))
                own.add(v.tensor_copy(lo[:], lo_i[:]))
                own.link(v.tensor_copy(hi[:], hi_i[:]))
                flat = lambda a: a.rearrange("p b x -> p (b x)").unsqueeze(2).broadcast_to([P, NB * X, ST])
                m = mask
                own.link(v.tensor_tensor(m, flat(hi[:]), g.iota[:, 0:ST].unsqueeze(1).broadcast_to([P, NB * X, ST]), ALU.is_equal))
                own.link(v.tensor_copy(left, tid[:].unsqueeze(2).broadcast_to([P, NB, X])))
                for n in range(VALS):
                    if n == 2:
                        own.link(v.tensor_copy(left, g.prob[:]))
                    own.link(v.tensor_tensor(val[:, :, n, :], m, flat(left), ALU.mult))
                    if n not in (1, VALS - 1):
                        own.link(v.tensor_copy(value16, left))
                        own.link(v.tensor_tensor(left, left, value16, ALU.subtract))

                def hot(e, i, first):
                    if not first:
                        dve.wait_ge(list_done, e - 1)
                    v.tensor_tensor(lo_hot[i], lo[:, :, bass.ds(e, 1)].broadcast_to([P, NB, P]),
                                    g.iota[:, 0:P].unsqueeze(1).broadcast_to([P, NB, P]), ALU.is_equal).then_inc(hot_done, 1)

                def keep(e, i):
                    dve.wait_ge(list_done, e + 1)
                    v.tensor_copy(parts[i][:], lp[i][:]).then_inc(list_copied, 1)
                    dve.wait_ge(list_copied, e * 4 + 1)
                    v.tensor_tensor(tok[i][:, 0, :], parts[i][:, 4, :], parts[i][:, 3, :], ALU.add).then_inc(list_copied, 1)
                    v.tensor_tensor(g.tok_i[:, bass.ds(e, 1), :].rearrange("p a t -> p (a t)"), parts[i][:, 1, :],
                                    parts[i][:, 0, :], ALU.add).then_inc(list_copied, 1)
                    dve.wait_ge(list_copied, e * 4 + 3)
                    v.tensor_tensor(g.tok_p[:, bass.ds(e, 1), :].rearrange("p a t -> p (a t)"), tok[i][:, 0, :],
                                    parts[i][:, 2, :], ALU.add).then_inc(list_copied, 1)

                hot(0, 0, True)
                hot(1, 1, True)
                with dve.Fori(1, X // 2) as n:
                    for i in range(2):
                        keep(n * 2 - 2 + i, i)
                        hot(n * 2 + i, i, False)
                keep(X - 2, 0)
                keep(X - 1, 1)
                dve.wait_ge(list_copied, 4 * X)

            @block.tensor
            def _(pe):
                for n, (b, k) in enumerate(groups):
                    if n == 0:
                        pe.wait_ge(rep_done, 1)
                    if n >= 2:
                        pe.wait_ge(tp_copied, n - 1)
                    for j in range(k):
                        m = nc.tensor.transpose(tp[n % 2][:, j * P:(j + 1) * P],
                                                rep[:, b + j, :, :].rearrange("p x r -> p (x r)"), g.ident[:])
                    m.then_inc(tp_done, 1)
                for n in range(len(SHIFTS)):
                    pe.wait_ge(votes_in, n + 1)
                    nc.tensor.matmul(vp[:], same[:], enough[:], start=True, stop=True).then_inc(votes_done, 1)
                for n, (b, k) in enumerate(groups):
                    n += len(groups)
                    if n == len(groups):
                        pe.wait_ge(slot_done, 1)
                    pe.wait_ge(tp_copied, n - 1)
                    for j in range(k):
                        m = nc.tensor.transpose(tp[n % 2][:, j * P:(j + 1) * P], rank[:, (b + j) * P:(b + j + 1) * P], g.ident[:])
                    m.then_inc(tp_done, 1)

                def lists(e, i, first):
                    pe.wait_ge(hot_done, e + 1)
                    if not first:
                        pe.wait_ge(list_copied, 4 * (e - 1))
                    for b in range(NB):
                        m = nc.tensor.matmul(lp[i][:].rearrange("p v t -> p (v t)"), lo_hot[i][:, b, :],
                                             val[:, bass.ds(e + b * X, 1), :, :].rearrange("p a v t -> p (a v t)"),
                                             start=(b == 0), stop=(b == NB - 1))
                    m.then_inc(list_done, 1)
                lists(0, 0, True)
                lists(1, 1, True)
                with pe.Fori(1, X // 2) as n:
                    for i in range(2):
                        lists(n * 2 + i, i, False)


def stage_experts(nc, g, w1, w2, out):
    with ExitStack() as ctx:
        sb = lambda n, s, d=F32: ctx.enter_context(nc.sbuf_tensor(n, s, d))
        ps = lambda n, s: ctx.enter_context(nc.psum_tensor(n, s, F32))
        WIDE = TOPK + TOPK % 2
        HALF = (WIDE // 2 + 1) // 2 * 2
        HK, HF = KT // 2, FT // 2
        raw = [sb(f"w_raw{i}", [P, HK * FH]) for i in range(2)]
        w1h, w1l = sb("w1_high", [P, KT * FH], F32R), sb("w1_low", [P, KT * FH], F32R)
        w2h, w2l = sb("w2_high", [P, FT * D], F32R), sb("w2_low", [P, FT * D], F32R)
        xg = sb("xg", [P, ST, D])
        xh, xl = (sb(n, [P, KT, WIDE], F32R) for n in ("e_x_high", "e_x_low"))
        hs = [sb(f"e_hidden{i}", [P, HALF]) for i in range(2)]
        hh, hl = (sb(n, [P, FT, WIDE], F32R) for n in ("e_hidden_high", "e_hidden_low"))
        ob = [sb(f"e_out{i}", [P, D]) for i in range(2)]
        idx = [sb(f"e_idx{i}", [P, ST], I32) for i in range(2)]
        pr = [sb(f"e_pr{i}", [P, ST]) for i in range(2)]
        tp = [ps(f"e_tp{i}", [P, 4, P]) for i in range(2)]
        hp = [ps(f"e_hp{i}", [P, 512]) for i in range(2)]
        op = [ps(f"e_op{i}", [P, D]) for i in range(2)]
        (idx_done, tp_done, xh_done, xl_done, h_done, hs_done, hh_done, hl_done, wh_done, wl_done, o_done, o_scaled,
         gated, padded) = new_sems(
            nc, g.ctx, "e_idx_done", "e_tp_done", "e_x_high_done", "e_x_low_done", "e_h_done", "e_hidden_done",
            "e_hidden_high_done", "e_hidden_low_done", "e_w_high_done", "e_w_low_done", "e_o_done", "e_o_scaled",
            "experts_gated", "e_padded")
        raw_in = new_sems(nc, g.ctx, "w_raw_in0", "w_raw_in1")
        xg_in = new_sems(nc, g.ctx, *[f"xg_in{t}" for t in range(ST)])
        o_out = new_sems(nc, g.ctx, "o_out0", "o_out1")
        size = lambda t: P if t < ST - 1 else SLAST
        wide = lambda t: min(P, WIDE - t * P)
        halves = [(0, HALF), (HALF, WIDE)]
        UT = 2 * ST
        UH = FT * len(halves)
        uses = [(ST + 1) // 2, ST // 2]
        w1r, w2r = w1.rearrange("e d f -> (e d) f"), w2.rearrange("e f d -> (e f) d")

        def each(eng, body):
            body(0, 0, 0, True, False)
            with eng.Fori(0, X // 2 - 1) as n:
                body(n * 2 + 1, 1, n, False, False)
                body(n * 2 + 2, 0, n + 1, False, False)
            body(X - 1, 1, X // 2 - 1, False, True)

        W1_AT = {1: (0,), 3: (1,)}
        def piece_of(high, j):
            return high[:, (j % 2) * HK * FH:(j % 2 + 1) * HK * FH]

        with nc.Block() as block:
            @block.sync
            def _(sp):
                def load(e, first):
                    for j in range(4):
                        if not (first and j < 2):
                            sp.wait_ge(wl_done, 4 * e + j - 1)
                        if j < 2:
                            sp.dma_start(raw[j % 2][:].rearrange("p (k f) -> p k f", f=FH),
                                         w1r[bass.ds(e * D + j * HK * P, HK * P), :].rearrange("(k p) f -> p k f", p=P)
                                         ).then_inc(raw_in[j % 2], 16)
                        else:
                            sp.dma_start(raw[j % 2][:].rearrange("p (k d) -> p k d", d=D),
                                         w2r[bass.ds(e * FH + (j - 2) * HF * P, HF * P), :].rearrange("(k p) d -> p k d", p=P)
                                         ).then_inc(raw_in[j % 2], 16)
                load(0, True)
                with sp.Fori(1, X) as e:
                    load(e, False)

            @block.gpsimd
            def _(pool):
                nc.gpsimd.memset(g.gate[0:1, 1:2], 0.0).then_inc(gated, 1)

                def gather(e, i, turn):
                    pool.wait_ge(idx_done, 2 * e + 2)
                    if turn is not None:
                        pool.wait_ge(tp_done, UT * e)
                    gate(nc, g, gated, turn if turn is not None else 0)
                    for t in range(ST):
                        nc.gpsimd.indirect_dma_start(
                            xg[0:size(t), t, :], None, g.xn1[:, :],
                            bass.IndirectOffsetOnAxis(idx[i][0:size(t), t:t + 1], 0)).then_inc(xg_in[t], 16)

                def scatter(e, i, n, first, last):
                    base = e * (ST + 1) + 1
                    if not last:
                        gather(e + 1, 1 - i, base)
                    for t in range(ST):
                        if t == 0 and not first:
                            for j in range(2):
                                pool.wait_ge(o_out[j], 16 * uses[j] * e)
                        pool.wait_ge(o_scaled, ST * e + t + 1)
                        gate(nc, g, gated, base + t + (0 if last else 1))
                        nc.gpsimd.indirect_dma_start(
                            out[:, :], bass.IndirectOffsetOnAxis(idx[i][0:size(t), t:t + 1], 0), ob[t % 2][0:size(t), :],
                            None, bounds_check=N - 1, oob_is_err=True, compute_op=ALU.add).then_inc(o_out[t % 2], 16)
                pool.wait_ge(padded, 1)
                gather(0, 0, None)
                each(pool, scatter)
                for j in range(2):
                    pool.wait_ge(o_out[j], 16 * uses[j] * X)

            @block.vector
            def _(dve):
                v = nc.vector

                def lists(e, i, first):
                    if not first:
                        for j in range(2):
                            dve.wait_ge(o_out[j], 16 * uses[j] * (e - 1))
                    v.tensor_copy(idx[i][:], g.tok_i[:, bass.ds(e, 1), :].rearrange("p a t -> p (a t)")).then_inc(idx_done, 1)
                    v.tensor_copy(pr[i][:], g.tok_p[:, bass.ds(e, 1), :].rearrange("p a t -> p (a t)")).then_inc(idx_done, 1)

                def weights_low(e, js):
                    for j in js:
                        high, low = (w1h, w1l) if j < 2 else (w2h, w2l)
                        dve.wait_ge(wh_done, 4 * e + j + 1)
                        v.tensor_tensor(piece_of(low, j), raw[j % 2][:], piece_of(high, j).bitcast(F32), ALU.subtract).then_inc(wl_done, 1)

                def tokens_low(e, us=range(UT)):
                    for u in us:
                        t, k = u // 2, (u % 2) * 4
                        dve.wait_ge(xh_done, UT * e + u + 1)
                        c = slice(t * P, t * P + wide(t))
                        v.tensor_tensor(xl[:, k:k + 4, c], tp[u % 2][:, :, 0:wide(t)], xh[:, k:k + 4, c].bitcast(F32),
                                        ALU.subtract).then_inc(xl_done, 1)

                def hidden(e):
                    for u in range(UH):
                        f, (a, b) = u // 2, halves[u % 2]
                        dve.wait_ge(hs_done, UH * e + u + 1)
                        v.tensor_copy(hh[:, f, a:b], hs[u % 2][:, 0:b - a]).then_inc(hh_done, 1)
                        dve.wait_ge(hh_done, UH * e + u + 1)
                        v.tensor_tensor(hl[:, f, a:b], hs[u % 2][:, 0:b - a], hh[:, f, a:b].bitcast(F32), ALU.subtract).then_inc(hl_done, 1)

                def step(e, i, n, first, last):
                    weights_low(e, (2, 3))
                    if not first:
                        dve.wait_ge(o_done, ST * e)
                    hidden(e)
                    if not last:
                        lists(e + 1, 1 - i, first)
                    for t in range(ST):
                        if not last:
                            tokens_low(e + 1, (2 * t, 2 * t + 1))
                            weights_low(e + 1, W1_AT.get(t, ()))
                        dve.wait_ge(idx_done, 2 * e + 2)
                        j = t % 2
                        dve.wait_ge(o_done, ST * e + t + 1)
                        if not (first and t < 2):
                            dve.wait_ge(o_out[j], 16 * (uses[j] * e + t // 2))
                        v.tensor_scalar(ob[j][0:size(t), :], op[j][0:size(t), :], pr[i][0:size(t), t:t + 1], None,
                                        ALU.mult).then_inc(o_scaled, 1)
                v.memset(xg[:, ST - 1, :], 0.0).then_inc(padded, 1)
                lists(0, 0, True)
                weights_low(0, (0, 1))
                tokens_low(0)
                each(dve, step)

            @block.scalar
            def _(act):
                def weights_high(e, js, first):
                    for j in js:
                        act.wait_ge(raw_in[j % 2], 16 * (2 * e + j // 2 + 1))
                        if not first and j == 0:
                            act.wait_ge(h_done, UH * e)
                        if not first and j == 2:
                            act.wait_ge(o_done, ST * e)
                        nc.scalar.copy(piece_of(w1h if j < 2 else w2h, j), raw[j % 2][:]).then_inc(wh_done, 1)

                def tokens_high(e, first, us=range(UT)):
                    if not first:
                        act.wait_ge(h_done, UH * e)
                    for u in us:
                        t, k = u // 2, (u % 2) * 4
                        act.wait_ge(tp_done, UT * e + u + 1)
                        nc.scalar.copy(xh[:, k:k + 4, t * P:t * P + wide(t)], tp[u % 2][:, :, 0:wide(t)]).then_inc(xh_done, 1)

                def step(e, i, n, first, last):
                    weights_high(e, (2, 3), first)
                    for u in range(UH):
                        f, (a, b) = u // 2, halves[u % 2]
                        act.wait_ge(h_done, UH * e + u + 1)
                        if not (first and u < 2):
                            act.wait_ge(hl_done, UH * e + u - 1)
                        nc.scalar.activation(hs[u % 2][:, 0:b - a], hp[u % 2][:, 0:b - a], ACT.Gelu).then_inc(hs_done, 1)
                    for t in range(ST):
                        if not last:
                            tokens_high(e + 1, False, (2 * t, 2 * t + 1))
                            weights_high(e + 1, W1_AT.get(t, ()), False)
                weights_high(0, (0, 1), True)
                tokens_high(0, True)
                each(act, step)

            @block.tensor
            def _(pe):
                def turn(e, first, us=range(UT)):
                    for u in us:
                        t, k = u // 2, (u % 2) * 4
                        if u % 2 == 0:
                            pe.wait_ge(xg_in[t], 16 * (e + 1))
                        if not (first and u < 2):
                            pe.wait_ge(xl_done, UT * e + u - 1)
                        for j in range(4):
                            m = nc.tensor.transpose(tp[u % 2][:, j, :], xg[:, t, (k + j) * P:(k + j + 1) * P], g.ident[:])
                        m.then_inc(tp_done, 1)

                def products(dst, left, right, tiles):
                    passes = [(a, b) for a, b in ((0, 0), (0, 1), (1, 0))]
                    for n, (a, b) in enumerate(passes):
                        for k in range(tiles):
                            m = nc.tensor.matmul(dst, left(a, k), right(b, k), start=(n == 0 and k == 0),
                                                 stop=(n == len(passes) - 1 and k == tiles - 1))
                    return m

                def step(e, i, n, first, last):
                    pe.wait_ge(xl_done, UT * (e + 1))
                    pe.wait_ge(wl_done, 4 * e + 2)
                    for u in range(UH):
                        f, (a, b) = u // 2, halves[u % 2]
                        if not (first and u < 2):
                            pe.wait_ge(hs_done, UH * e + u - 1)
                        products(hp[u % 2][:, 0:b - a],
                                 lambda s, k: (w1h, w1l)[s][:, k * FH + f * P:k * FH + (f + 1) * P],
                                 lambda s, k: (xh, xl)[s][:, k, a:b], KT).then_inc(h_done, 1)
                    for t in range(ST):
                        if not last:
                            turn(e + 1, False, (2 * t, 2 * t + 1))
                        if t == 0:
                            pe.wait_ge(hl_done, UH * (e + 1))
                            pe.wait_ge(wl_done, 4 * (e + 1))
                        if not (first and t < 2):
                            pe.wait_ge(o_scaled, ST * e + max(t - 1, 0))
                        for c in range(0, D, 512):
                            m = products(op[t % 2][0:wide(t), c:c + 512],
                                         lambda s, f: (hh, hl)[s][:, f, t * P:t * P + wide(t)],
                                         lambda s, f: (w2h, w2l)[s][:, f * D + c:f * D + c + 512], FT)
                        m.then_inc(o_done, 1)
                turn(0, True)
                each(pe, step)


def build(nc, x, src, dst, W, att_src, att_dst, bias, gate_w, w1, w2, out):
    from_dram = lambda n, s, d=F32: nc.dram_tensor(n, s, d).ap()
    with ExitStack() as top:
        g = Core()
        g.ctx = []
        g.dst_s = from_dram("dst_sorted", (NC * CH, 1), I32)
        g.src_s = from_dram("src_sorted", (NC * CH, 1), I32)
        g.lines = from_dram("dst_lines", (P, EC))
        g.starts = from_dram("edge_starts", (NP + 1,))
        g.laid = from_dram("laid_scores", (NC * CH, 2 * H))
        g.low = from_dram("low_addresses", (EC, P), BF16)
        g.xp = from_dram("xp_rows", (NP, D))
        g.rec = from_dram("edge_records", (NC * CH, REC))
        g.xn1 = from_dram("xn1_rows", (N, D))
        setup(nc, top, g)
        stage_order(nc, g, src, dst)
        keep = lambda c, n, s, d=F32: c.enter_context(nc.sbuf_tensor(n, s, d))
        g.prob = keep(top, "prob", [P, NB, X])
        g.tok_i = keep(top, "tok_i", [P, X, ST], I32)
        g.tok_p = keep(top, "tok_p", [P, X, ST])
        with ExitStack() as gnn:
            g.big = keep(gnn, "big", [P, NB, D])
            g.acc_side = keep(gnn, "acc_side", [P, NB, SUMMED])
            g.blk_i = keep(gnn, "blk_i", [P, ITEMS], I32)
            g.chk_i = keep(gnn, "chk_i", [P, ITEMS], I32)
            with ExitStack() as mid:
                g.first, g.last = keep(mid, "first", [P, EC]), keep(mid, "last", [P, EC])
                g.src_i = keep(mid, "src_i", [P, EC], I32)
                g.dst_f = keep(mid, "dst_f", [P, EC + 2])
                g.start_i = keep(mid, "start_i", [P, NB], I32)
                g.atab = keep(mid, "atab", [P, NB, 2 * H])
                stage_nodes(nc, g, x, W, att_src, att_dst)
                clear_sems(nc, g.ctx)
                g.edge_s = keep(mid, "edge_s", [P, EC, H])
                g.edge_d = keep(mid, "edge_d", [P, EC, 2 * H])
                stage_scores(nc, g)
                stage_weights(nc, g)
            stage_messages(nc, g)
            stage_residual(nc, g, x, bias, gate_w)
            stage_select(nc, g, out)
        stage_experts(nc, g, w1, w2, out)


_INS = ["x", "src", "dst", "L0_gnn_W", "L0_gnn_att_src", "L0_gnn_att_dst", "L0_gnn_bias", "L0_ffn_gate_w",
        "L0_ffn_w1", "L0_ffn_w2"]


def kernel(**inputs):
    import numpy as np
    import concourse.bacc as bacc
    from concourse.bass_utils import run_bass_kernel_spmd

    nc = bacc.Bacc("TRN2", target_bir_lowering=False, num_devices=1)
    arrays, args = {}, []
    for name in _INS:
        a = np.ascontiguousarray(inputs[name])
        arrays[f"in_{name}"] = a
        args.append(nc.dram_tensor(f"in_{name}", a.shape, mybir.dt.from_np(a.dtype), kind="ExternalInput").ap())
    args.append(nc.dram_tensor("out_rows", (N, D), F32, kind="ExternalOutput").ap())
    build(nc, *args)
    r = run_bass_kernel_spmd(nc, [arrays], core_ids=[0])
    return r.results[0]["out_rows"]
```
